# Optimizing a Trainium2 kernel written in Bass

```python
import numpy as np
import jax
import jax.numpy as jnp

def _softmax(x, axis=-1):
    return jax.nn.softmax(x, axis=axis)

def _gelu(x):
    return jax.nn.gelu(x, approximate=True)

def _silu(x):
    return jax.nn.silu(x)

def _sigmoid(x):
    return jax.nn.sigmoid(x)

def _layernorm(x, axis=-1, eps=1e-05):
    m = jnp.mean(x, axis=axis, keepdims=True)
    v = jnp.var(x, axis=axis, keepdims=True)
    return (x - m) / jnp.sqrt(v + eps)

def _scatter_add(tgt, idx, src, axis=0):
    return tgt.at[idx].add(src)

def _segment_sum(src, seg, n):
    return jax.ops.segment_sum(src, seg, n)
kernel_name = 'mk_macaron_d2_jaxref_r8_d034b1'

def setup_inputs(seed: int=0):
    np.random.seed(seed)
    _w = jnp.asarray

    def _L0_attn_setup():
        import jax, jax.numpy as jnp
        import numpy as np
        B, N, C = (4, 512, 128)
        H = 16
        D = C // H
        EPS = 1e-06

        def _feature_map(x):
            return jax.nn.elu(x) + 1.0
        key = jax.random.key(seed)
        k1, k2, k3, k4 = jax.random.split(key, 4)
        x = jax.random.normal(k1, (B, N, C), dtype=jnp.float32)
        Wqkv = jax.random.normal(k2, (3 * C, C), dtype=jnp.float32) * 0.02
        Wproj = jax.random.normal(k3, (C, C), dtype=jnp.float32) * 0.02
        bproj = jax.random.normal(k4, (C,), dtype=jnp.float32) * 0.02
        return {'x': x, 'Wqkv': Wqkv, 'Wproj': Wproj, 'bproj': bproj}
    _L0_attn_in = _L0_attn_setup()

    def _L0_ffn_setup():
        import jax, jax.numpy as jnp
        import numpy as np
        B, N, D = (4, 512, 128)
        E, S, F = (16, 64, 256)
        DO = 128
        EPS = 1e-05

        def _layernorm(x, g, b):
            mu = jnp.mean(x, axis=-1, keepdims=True)
            var = jnp.mean(jnp.square(x - mu), axis=-1, keepdims=True)
            return (x - mu) * jax.lax.rsqrt(var + EPS) * g + b
        key = jax.random.key(seed)
        ks = jax.random.split(key, 8)
        d = {'x': jax.random.normal(ks[0], (B, N, D), dtype=jnp.float32), 'norm_g': jnp.ones((D,), jnp.float32), 'norm_b': jnp.zeros((D,), jnp.float32), 'slot_g': jnp.ones((D,), jnp.float32), 'slot_b': jnp.zeros((D,), jnp.float32), 'scale': jnp.ones((1,), jnp.float32), 'slot_embeds': jax.random.normal(ks[1], (E, S, D), jnp.float32) / np.sqrt(D), 'Wg': jax.random.normal(ks[2], (E, D, F), jnp.float32) * np.sqrt(2.0 / (D + F)), 'bg': jnp.zeros((E, F), jnp.float32), 'Wu': jax.random.normal(ks[3], (E, D, F), jnp.float32) * np.sqrt(2.0 / (D + F)), 'bu': jnp.zeros((E, F), jnp.float32), 'Wd': jax.random.normal(ks[4], (E, F, DO), jnp.float32) * np.sqrt(2.0 / (F + DO)), 'bd': jnp.zeros((E, DO), jnp.float32)}
        return d
    _L0_ffn_in = _L0_ffn_setup()

    def _L1_attn_setup():
        import jax, jax.numpy as jnp
        import numpy as np
        import math
        EPS = 1e-06

        def favorplus_features(x, proj):
            xw = jnp.einsum('bhtd,hmd->bhtm', x, proj)
            xw = xw - jnp.max(xw, axis=-1, keepdims=True)
            x_norm_sq = jnp.sum(x * x, axis=-1, keepdims=True)
            return jnp.exp(xw) * jnp.exp(-0.5 * x_norm_sq) + EPS
        key = jax.random.key(seed)
        ks = jax.random.split(key, 6)
        B, T, d = (2, 512, 128)
        h, m = (16, 32)
        dk = d // h
        s = 1.0 / math.sqrt(d)
        return {'x': jax.random.normal(ks[0], (B, T, d), dtype=jnp.float32), 'Wq': jax.random.normal(ks[1], (d, d), dtype=jnp.float32) * s, 'Wk': jax.random.normal(ks[2], (d, d), dtype=jnp.float32) * s, 'Wv': jax.random.normal(ks[3], (d, d), dtype=jnp.float32) * s, 'Wo': jax.random.normal(ks[4], (d, d), dtype=jnp.float32) * s, 'bo': jnp.zeros((d,), dtype=jnp.float32), 'proj': jax.random.normal(ks[5], (h, m, dk), dtype=jnp.float32)}
    _L1_attn_in = _L1_attn_setup()

    def _L1_ffn_setup():
        import jax, jax.numpy as jnp
        import numpy as np
        D_IN, D_HID = (128, 512)

        def _ternary(key, shape):
            return jax.random.randint(key, shape, -1, 2).astype(jnp.float32)

        def _tlin(x, w, s):
            return jnp.einsum('bsi,oi->bso', x, w) * s
        key = jax.random.key(seed)
        ks = jax.random.split(key, 12)
        inv = lambda fan: 1.0 / np.sqrt(fan).astype(np.float32)
        return {'x': jax.random.normal(ks[0], (4, 256, D_IN), dtype=jnp.float32), 'w1_w': _ternary(ks[1], (D_HID, D_IN)), 'w1_s': jax.random.uniform(ks[2], (D_HID,), dtype=jnp.float32) * inv(D_IN), 'w2_w': _ternary(ks[3], (D_HID, D_IN)), 'w2_s': jax.random.uniform(ks[4], (D_HID,), dtype=jnp.float32) * inv(D_IN), 'h1_w': _ternary(ks[5], (D_HID, D_HID)), 'h1_s': jax.random.uniform(ks[6], (D_HID,), dtype=jnp.float32) * inv(D_HID), 'h2_w': _ternary(ks[7], (D_HID, D_HID)), 'h2_s': jax.random.uniform(ks[8], (D_HID,), dtype=jnp.float32) * inv(D_HID), 'w3_w': _ternary(ks[9], (D_IN, D_HID)), 'w3_s': jax.random.uniform(ks[10], (D_IN,), dtype=jnp.float32) * inv(D_HID)}
    _L1_ffn_in = _L1_ffn_setup()
    _d = {'L0_attn_x': _L0_attn_in['x'], 'L0_attn_Wqkv': _L0_attn_in['Wqkv'], 'L0_attn_Wproj': _L0_attn_in['Wproj'], 'L0_attn_bproj': _L0_attn_in['bproj'], 'L0_ffn_norm_g': _L0_ffn_in['norm_g'], 'L0_ffn_norm_b': _L0_ffn_in['norm_b'], 'L0_ffn_slot_g': _L0_ffn_in['slot_g'], 'L0_ffn_slot_b': _L0_ffn_in['slot_b'], 'L0_ffn_scale': _L0_ffn_in['scale'], 'L0_ffn_slot_embeds': _L0_ffn_in['slot_embeds'], 'L0_ffn_Wg': _L0_ffn_in['Wg'], 'L0_ffn_bg': _L0_ffn_in['bg'], 'L0_ffn_Wu': _L0_ffn_in['Wu'], 'L0_ffn_bu': _L0_ffn_in['bu'], 'L0_ffn_Wd': _L0_ffn_in['Wd'], 'L0_ffn_bd': _L0_ffn_in['bd'], 'L1_attn_Wq': _L1_attn_in['Wq'], 'L1_attn_Wk': _L1_attn_in['Wk'], 'L1_attn_Wv': _L1_attn_in['Wv'], 'L1_attn_Wo': _L1_attn_in['Wo'], 'L1_attn_bo': _L1_attn_in['bo'], 'L1_attn_proj': _L1_attn_in['proj'], 'L1_ffn_w1_w': _L1_ffn_in['w1_w'], 'L1_ffn_w1_s': _L1_ffn_in['w1_s'], 'L1_ffn_w2_w': _L1_ffn_in['w2_w'], 'L1_ffn_w2_s': _L1_ffn_in['w2_s'], 'L1_ffn_h1_w': _L1_ffn_in['h1_w'], 'L1_ffn_h1_s': _L1_ffn_in['h1_s'], 'L1_ffn_h2_w': _L1_ffn_in['h2_w'], 'L1_ffn_h2_s': _L1_ffn_in['h2_s'], 'L1_ffn_w3_w': _L1_ffn_in['w3_w'], 'L1_ffn_w3_s': _L1_ffn_in['w3_s']}
    _x0 = _d['L0_attn_x']
    _d['L0_attn_x'] = jax.random.normal(jax.random.fold_in(jax.random.key(seed), 1), (8, 256, 128), dtype=_x0.dtype)
    del _x0
    return _d

def reference(L0_attn_x, L0_attn_Wqkv, L0_attn_Wproj, L0_attn_bproj, L0_ffn_norm_g, L0_ffn_norm_b, L0_ffn_slot_g, L0_ffn_slot_b, L0_ffn_scale, L0_ffn_slot_embeds, L0_ffn_Wg, L0_ffn_bg, L0_ffn_Wu, L0_ffn_bu, L0_ffn_Wd, L0_ffn_bd, L1_attn_Wq, L1_attn_Wk, L1_attn_Wv, L1_attn_Wo, L1_attn_bo, L1_attn_proj, L1_ffn_w1_w, L1_ffn_w1_s, L1_ffn_w2_w, L1_ffn_w2_s, L1_ffn_h1_w, L1_ffn_h1_s, L1_ffn_h2_w, L1_ffn_h2_s, L1_ffn_w3_w, L1_ffn_w3_s):

    def _L0_attn_ref(x, Wqkv, Wproj, bproj):
        import jax, jax.numpy as jnp
        import numpy as np
        B, N, C = (4, 512, 128)
        H = 16
        D = C // H
        EPS = 1e-06

        def _feature_map(x):
            return jax.nn.elu(x) + 1.0
        b, n, c = x.shape
        qkv = jnp.einsum('bnc,fc->bnf', x, Wqkv).reshape(b, n, 3, H, D)
        qkv = jnp.transpose(qkv, (2, 0, 3, 1, 4))
        q, k, v = (qkv[0], qkv[1], qkv[2])
        q = _feature_map(q)
        k = _feature_map(k)
        kv = jnp.einsum('bhnd,bhne->bhde', k, v)
        k_sum = k.sum(axis=2)
        z = 1.0 / (jnp.einsum('bhnd,bhd->bhn', q, k_sum)[..., None] + EPS)
        out = jnp.einsum('bhnd,bhde->bhne', q, kv) * z
        out = jnp.transpose(out, (0, 2, 1, 3)).reshape(b, n, c)
        out = jnp.einsum('bnc,oc->bno', out, Wproj) + bproj
        return out

    def _L0_ffn_ref(x, norm_g, norm_b, slot_g, slot_b, scale, slot_embeds, Wg, bg, Wu, bu, Wd, bd):
        import jax, jax.numpy as jnp
        import numpy as np
        B, N, D = (4, 512, 128)
        E, S, F = (16, 64, 256)
        DO = 128
        EPS = 1e-05

        def _layernorm(x, g, b):
            mu = jnp.mean(x, axis=-1, keepdims=True)
            var = jnp.mean(jnp.square(x - mu), axis=-1, keepdims=True)
            return (x - mu) * jax.lax.rsqrt(var + EPS) * g + b
        x = _layernorm(x, norm_g, norm_b)
        se = _layernorm(slot_embeds, slot_g, slot_b) * scale
        logits = jnp.einsum('bnd,esd->bnes', x, se)
        dispatch = jax.nn.softmax(logits, axis=1)
        combine = jax.nn.softmax(logits.reshape(x.shape[0], x.shape[1], -1), axis=-1)
        slots = jnp.einsum('bnd,bnes->besd', x, dispatch)
        gate = jax.nn.gelu(jnp.einsum('besd,edf->besf', slots, Wg) + bg[None, :, None, :], approximate=False)
        up = jnp.einsum('besd,edf->besf', slots, Wu) + bu[None, :, None, :]
        eout = jnp.einsum('besf,efo->beso', gate * up, Wd) + bd[None, :, None, :]
        eout = eout.reshape(eout.shape[0], -1, eout.shape[-1])
        return jnp.einsum('bns,bso->bno', combine, eout)

    def _L1_attn_ref(x, Wq, Wk, Wv, Wo, bo, proj):
        import jax, jax.numpy as jnp
        import numpy as np
        import math
        EPS = 1e-06

        def favorplus_features(x, proj):
            xw = jnp.einsum('bhtd,hmd->bhtm', x, proj)
            xw = xw - jnp.max(xw, axis=-1, keepdims=True)
            x_norm_sq = jnp.sum(x * x, axis=-1, keepdims=True)
            return jnp.exp(xw) * jnp.exp(-0.5 * x_norm_sq) + EPS
        B, T, d = x.shape
        h, m, dk = proj.shape

        def heads(W):
            y = jnp.einsum('btd,ed->bte', x, W)
            return y.reshape(B, T, h, dk).transpose(0, 2, 1, 3)
        Q = heads(Wq) / math.sqrt(dk)
        K = heads(Wk) / math.sqrt(dk)
        V = heads(Wv)
        inv_sqrt_m = 1.0 / math.sqrt(m)
        phiQ = favorplus_features(Q, proj) * inv_sqrt_m
        phiK = favorplus_features(K, proj) * inv_sqrt_m
        KV = jnp.einsum('bhtm,bhtd->bhmd', phiK, V)
        Ksum = jnp.sum(phiK, axis=2)
        num = jnp.einsum('bhtm,bhmd->bhtd', phiQ, KV)
        den = jnp.einsum('bhtm,bhm->bht', phiQ, Ksum)[..., None] + EPS
        out_heads = num / den
        merged = out_heads.transpose(0, 2, 1, 3).reshape(B, T, d)
        return jnp.einsum('btd,ed->bte', merged, Wo) + bo

    def _L1_ffn_ref(x, w1_w, w1_s, w2_w, w2_s, h1_w, h1_s, h2_w, h2_s, w3_w, w3_s):
        import jax, jax.numpy as jnp
        import numpy as np
        D_IN, D_HID = (128, 512)

        def _ternary(key, shape):
            return jax.random.randint(key, shape, -1, 2).astype(jnp.float32)

        def _tlin(x, w, s):
            return jnp.einsum('bsi,oi->bso', x, w) * s
        h = jax.nn.silu(_tlin(x, w1_w, w1_s)) * _tlin(x, w2_w, w2_s)
        h = jax.nn.gelu(_tlin(h, h1_w, h1_s), approximate=False)
        h = jax.nn.gelu(_tlin(h, h2_w, h2_s), approximate=False)
        return _tlin(h, w3_w, w3_s)
    x = L0_attn_x
    x = x + 0.5 * _L0_ffn_ref(_layernorm(x, axis=-1), L0_ffn_norm_g, L0_ffn_norm_b, L0_ffn_slot_g, L0_ffn_slot_b, L0_ffn_scale, L0_ffn_slot_embeds, L0_ffn_Wg, L0_ffn_bg, L0_ffn_Wu, L0_ffn_bu, L0_ffn_Wd, L0_ffn_bd)
    x = x + _L0_attn_ref(_layernorm(x, axis=-1), L0_attn_Wqkv, L0_attn_Wproj, L0_attn_bproj)
    x = x + 0.5 * _L0_ffn_ref(_layernorm(x, axis=-1), L0_ffn_norm_g, L0_ffn_norm_b, L0_ffn_slot_g, L0_ffn_slot_b, L0_ffn_scale, L0_ffn_slot_embeds, L0_ffn_Wg, L0_ffn_bg, L0_ffn_Wu, L0_ffn_bu, L0_ffn_Wd, L0_ffn_bd)
    x = x + 0.5 * _L1_ffn_ref(_layernorm(x, axis=-1), L1_ffn_w1_w, L1_ffn_w1_s, L1_ffn_w2_w, L1_ffn_w2_s, L1_ffn_h1_w, L1_ffn_h1_s, L1_ffn_h2_w, L1_ffn_h2_s, L1_ffn_w3_w, L1_ffn_w3_s)
    x = x + _L1_attn_ref(_layernorm(x, axis=-1), L1_attn_Wq, L1_attn_Wk, L1_attn_Wv, L1_attn_Wo, L1_attn_bo, L1_attn_proj)
    x = x + 0.5 * _L1_ffn_ref(_layernorm(x, axis=-1), L1_ffn_w1_w, L1_ffn_w1_s, L1_ffn_w2_w, L1_ffn_w2_s, L1_ffn_h1_w, L1_ffn_h1_s, L1_ffn_h2_w, L1_ffn_h2_s, L1_ffn_w3_w, L1_ffn_w3_s)
    return x

_drawn_inputs = setup_inputs


def setup_inputs(seed=0):
    import zlib

    import numpy as np

    out = dict(_drawn_inputs(seed))
    spreads = {'L0_ffn_norm_g': (1.0, 0.2),
     'L0_ffn_norm_b': (0.0, 0.1),
     'L0_ffn_slot_g': (1.0, 0.2),
     'L0_ffn_slot_b': (0.0, 0.1),
     'L0_ffn_bg': (0.0, 0.1),
     'L0_ffn_bu': (0.0, 0.1),
     'L0_ffn_bd': (0.0, 0.1),
     'L1_attn_bo': (0.0, 0.1)}
    factors = {}
    for name, (base, spread) in spreads.items():
        noise = np.random.default_rng([zlib.crc32(name.encode()), seed]).standard_normal(out[name].shape)
        drawn = base * np.exp(spread * noise) if base else spread * noise
        out[name] = jnp.asarray(drawn.astype(out[name].dtype))
    for name, factor in factors.items():
        out[name] = (out[name] * factor).astype(out[name].dtype)
    return out
```

```python
from contextlib import ExitStack

import concourse.bass as bass
import concourse.mybir as mybir
import numpy as np

ALU = mybir.AluOpType
ACT = mybir.ActivationFunctionType
F32 = mybir.dt.float32
F32R = mybir.dt.float32r
AX_X = mybir.AxisListType.X

P = 128
BATCHES, SEQ, D = 8, 256, 128
TILES = BATCHES * SEQ // P
PER = SEQ // P
EXPERTS, SLOTS, FE = 16, 64, 256
NSLOT = EXPERTS * SLOTS
ST = NSLOT // P
OW = D + 2
HEADS, HD = 16, 8
FEAT = 32
HF = HEADS * FEAT
FG = HF // P
VA = P // FEAT * HD + P // FEAT
HID = 512
HK = HID // P
CHUNK = 512
CHUNKS = BATCHES * SEQ // CHUNK
LN_EPS = 1e-5
ATT_EPS = 1e-6
QK_SCALE = HD ** -0.5


LN_STEPS = {"m": 11, "a": 4}
MOE_TOTALS = dict(
    pool=BATCHES * LN_STEPS["m"], turned=BATCHES, kept=BATCHES, zthi=BATCHES, ztlo=BATCHES, rows=BATCHES * PER,
    copied=BATCHES * PER, maxn=BATCHES * PER, columns=BATCHES * 4, maxs=BATCHES * 4,
    zs=BATCHES * 4, lnz=BATCHES, shift=BATCHES * 3, spread=BATCHES, sub=BATCHES * PER,
    disp=BATCHES * PER, shifted=BATCHES * 4, comb=BATCHES * 4, slots=BATCHES, slots_a=BATCHES, slots_b=BATCHES,
    wgu0=EXPERTS // 2 * 16, wgu1=EXPERTS // 2 * 16, wd0=EXPERTS // 2 * 16, wd1=EXPERTS // 2 * 16, gate=EXPERTS * 2, up=EXPERTS * 2, gelu=EXPERTS * 2, h=EXPERTS * 2,
    down=EXPERTS, eo=EXPERTS * 2, sums=ST, staged_a=BATCHES, staged_b=BATCHES, combined=BATCHES * PER,
    steps=BATCHES * 4, mom=BATCHES * 4)
FFN_TOTALS = dict(
    pool=BATCHES * LN_STEPS["a"], turned=BATCHES, zt=BATCHES, p1=CHUNKS * HK, p2=CHUNKS * HK, silu=CHUNKS * HK,
    ha=CHUNKS * HK, pb=CHUNKS * HK, hb=CHUNKS * HK, pc=CHUNKS * HK, hc=CHUNKS * HK, p3=CHUNKS, yt=CHUNKS, yp=CHUNKS,
    added=CHUNKS, mom=BATCHES * 4)
TOTALS = {"m0": MOE_TOTALS, "m1": MOE_TOTALS, "f0": FFN_TOTALS, "f1": FFN_TOTALS}


def as32(ap):
    return ap.bitcast(F32)


def build(nc, ins, out, stages=("m0", "la", "m1", "f0", "fa", "f1")):
    before = dict(zip(stages, ("init",) + tuple(stages[:-1])))
    with ExitStack() as ctx:
        def sb(name, shape, dtype=F32, scope=ctx):
            return scope.enter_context(nc.sbuf_tensor(name, shape, dtype))

        sems = {}

        def sem(name):
            stage, _, what = name.partition("_")
            if stage in TOTALS and what != "x":
                name = f"{stage[0]}_{what}"
            if name not in sems:
                sems[name] = ctx.enter_context(nc.semaphore(name))
            return sems[name]

        def earlier(name):
            stage, _, what = name.partition("_")
            second = stage in ("m1", "f1") and stage[0] + "0" in stages and what != "x"
            return TOTALS[stage][what] if second else 0

        def plain(eng, value):
            if isinstance(value, int):
                return value
            count = eng.to_reg(value)
            eng.wait_ge(sem("pool_const" if eng is nc.gpsimd else "dve_const"), 1)
            return count

        def reached(name, value, eng=None):
            value = value + earlier(name)
            return sem(name), value if eng is None else plain(eng, value)

        def due(value):
            return not isinstance(value, int) or value > 0

        class Steps:
            def __init__(self, name, base=0):
                self.sem, self.n = sem(name), base + earlier(name)

            def step(self):
                self.n = self.n + 1
                return 1

        x = sb("x", [P, TILES, D])
        moments = sb("moments", [P, TILES, 2])
        ident = sb("ident", [P, P])
        ident_r = sb("ident_r", [P, P], F32R)
        half_power = sb("half_power", [P, 16])
        eps2 = sb("eps2", [P, PER])
        two = sb("two", [P, 2 * BATCHES])
        fresh = sb("fresh", [P, PER, 2])
        bn6 = sb("bn6", [P, 4, 6])
        rstd = sb("rstd", [P, 2, 8])
        z_in = sb("z_in", [P, 2, PER, D])
        bproj_bc = sb("bproj_bc", [P, D])
        bo_bc = sb("bo_bc", [P, D])
        headmask = sb("headmask", [P, D])
        featmask = sb("featmask", [P, VA])
        wqkv = sb("wqkv", [P, 3 * D])
        wproj = sb("wproj", [P, D])
        fw = sb("fw", [P, 4, D])
        proj_bd = sb("proj_bd", [P, HF])
        ffn_s = sb("ffn_s", [P, 4, HK])
        w3_s = sb("w3_s", [P, 2])

        moe = ExitStack()
        se_hi = sb("se_hi", [P, 2, NSLOT], F32R, moe)
        se_lo = sb("se_lo", [P, 2, NSLOT], F32R, moe)
        zt_hi = sb("zt_hi", [P, 2, SEQ], F32R, moe)
        zt_lo = sb("zt_lo", [P, 2, SEQ], F32R, moe)
        junk = sb("junk", [P, 4, SEQ], F32, moe)
        moe2 = ExitStack()
        expert_io = sb("expert_io", [P, ST + 1, BATCHES * OW], F32, moe2)
        bd_bc = sb("bd_bc", [P, EXPERTS, D], F32, moe2)
        wx = sb("wx", [P, 2, 3 * FE], F32, moe2)
        bgu = sb("bgu", [P, 2, EXPERTS, 2], F32, moe2)
        logits = sb("logits", [P, 2, PER, NSLOT], F32, moe2)
        negmax_n = sb("negmax_n", [P, 2, PER], F32R, moe2)
        negmax_s = sb("negmax_s", [P, 2, ST], F32, moe2)
        zsum_s = sb("zsum_s", [P, 2, ST], F32, moe2)
        lnz_s = sb("lnz_s", [P, 2, ST], F32, moe2)
        shift_s = sb("shift_s", [P, 2, ST], F32, moe2)
        shift_hi = sb("shift_hi", [P, 2, ST], F32R, moe2)
        shift_lo = sb("shift_lo", [P, 2, ST], F32R, moe2)
        z_slots = sb("z_slots", [P, 2, PER, D], F32, moe2)
        gate = sb("gate", [P, 2, CHUNK], F32, moe2)
        hmid = sb("hmid", [P, 2, 2, CHUNK], F32, moe2)
        affine = sb("affine", [P, 2, D], F32, moe2)
        cols = sb("cols", [P, 6], F32, moe2)
        zcol = sb("zcol", [P, 2, PER], F32, moe2)
        se_stat = sb("se_stat", [P, ST, 8], F32, moe2)
        se_r = sb("se_r", [P, 2, ST], F32, moe2)
        moe3 = ExitStack()
        comb = sb("comb", [P, BATCHES, ST, SEQ], F32, moe3)
        moe3.close()
        la = ExitStack()
        la_zt = sb("la_zt", [P, 2, SEQ], F32, la)
        la_min = sb("la_min", [P, 2, 2 * SEQ], F32, la)
        la_qk = sb("la_qk", [P, 2, 2 * SEQ], F32, la)
        la_v = sb("la_v", [P, 2, PER, D + 1], F32, la)
        la_kv = sb("la_kv", [P, 2, 2, D], F32, la)
        la_o = sb("la_o", [P, 2, 2, SEQ], F32, la)
        la.close()
        moe2.close()
        moe.close()

        l1 = ExitStack()
        ffw = sb("ffw", [P, 2 * HID + 2 * HK * HID + HK * D], F32, l1)
        w1, w2 = ffw[:, 0:HID], ffw[:, HID:2 * HID]
        h1 = ffw[:, 2 * HID:(2 + HK) * HID].rearrange("p (k o) -> p k o", k=HK)
        h2 = ffw[:, (2 + HK) * HID:(2 + 2 * HK) * HID].rearrange("p (k o) -> p k o", k=HK)
        w3 = ffw[:, (2 + 2 * HK) * HID:].rearrange("p (k o) -> p k o", k=HK)
        pad = sb("pad", [P, 4 * NSLOT + 8 * SEQ - ffw.shape[1]], F32, l1)
        ffn = ExitStack()
        zt_all = sb("zt_all", [P, BATCHES, SEQ], F32, ffn)
        act_a = sb("act_a", [P, HK, CHUNKS * CHUNK], F32, ffn)
        act_b = sb("act_b", [P, HK, CHUNKS * CHUNK], F32, ffn)
        silu_out = sb("silu_out", [P, 2, CHUNK], F32, ffn)
        y_t = sb("y_t", [P, 2, CHUNK], F32, ffn)
        ffn.close()
        fa = ExitStack()
        fa_zt = sb("fa_zt", [P, 2, SEQ], F32, fa)
        fa_qkt = sb("fa_qkt", [P, 2, 2, SEQ], F32, fa)
        fa_sq = sb("fa_sq", [P, 2, 2 * SEQ], F32, fa)
        fa_c = sb("fa_c", [P, 2, 3, 4 * HEADS], F32, fa)
        fa_phi = sb("fa_phi", [P, 2, 4, HF], F32, fa)
        fa_phit = sb("fa_phit", [P, 2, PER, FG, P], F32, fa)
        fa_vaug = sb("fa_vaug", [P, 2, PER, FG, VA], F32, fa)
        fa_kv = sb("fa_kv", [P, 2, FG, VA], F32, fa)
        fa_den = sb("fa_den", [P, 2, PER * HEADS], F32, fa)
        fa_o = sb("fa_o", [P, 2, PER, D], F32, fa)
        fa_ot = sb("fa_ot", [P, 2, SEQ], F32, fa)
        fa_y = sb("fa_y", [P, 2, PER, D], F32, fa)
        fa.close()
        l1.close()

        ps = ctx.enter_context(nc.psum_tensor("ps", [P, 8, 512], F32))
        block = ctx.enter_context(nc.Block())

        def batch(b):
            return bass.ds(b * PER, PER) if not isinstance(b, int) else slice(b * PER, b * PER + PER)

        def looped(eng, step, first, last):
            pairs = (last - first) // 2
            with eng.Fori(0, pairs) as it:
                step(it * 2 + first, it + (first // 2), 1)
                step(it * 2 + (first + 1), it + (first + 1) // 2, 0)

        def all_batches(eng, step):
            step(0, 0, 0)
            looped(eng, step, 1, BATCHES - 1)
            step(BATCHES - 1, (BATCHES - 1) // 2, 1)

        def store_slots(copy, j, p, k):
            for h in range(2):
                col = (h ^ p) * 512 + h * SLOTS
                dst = expert_io[:, 1 + 4 * k:5 + 4 * k, :]
                dst = dst[:, :, j * P + col:j * P + col + SLOTS] if isinstance(j, int) else dst[:, :, bass.ds(j * P + col, SLOTS)]
                last = copy(dst, ps[:, 6 + k, :].rearrange("p (t h s) -> p t h s", t=4, h=2)[:, :, h, :])
            return last


        @block.sync
        def _(sp):
            sp.dma_start(ident[:], ins["ident"]).then_inc(sem("ld_const"), 16)
            for h in range(2):
                sp.dma_start(x[:, h * 8:h * 8 + 8, :],
                             ins["x"].rearrange("(t p) d -> p t d", p=P)[:, h * 8:h * 8 + 8, :]).then_inc(sem(f"ld_x{h}"), 16)
            sp.dma_start(logits[:, 1, 0, :].rearrange("p (t d) -> p t d", t=ST),
                         ins["slot_embeds"].rearrange("(t p) d -> p t d", p=P)).then_inc(sem("ld_se"), 16)
            sp.dma_start(cols[:, 0:3], ins["cols"]).then_inc(sem("ld_se"), 16)
            sp.dma_start(affine[:], ins["affine"].partition_broadcast(P)).then_inc(sem("ld_affine"), 16)
            sp.dma_start(bgu[:].rearrange("p a b c -> p (a b c)"), ins["bgu"]).then_inc(sem("ld_w"), 16)
            sp.dma_start(bd_bc[:], ins["bd"].partition_broadcast(P)).then_inc(sem("ld_w"), 16)
            for dst, name in ((wqkv, "wqkv"), (wproj, "wproj"), (headmask, "headmask"), (featmask, "featmask"),
                              (proj_bd, "proj_bd"), (w3_s[:, 0:1], "w3_s")):
                sp.dma_start(dst[:] if dst is not w3_s else dst, ins[name]).then_inc(sem("ld_w"), 16)
            sp.dma_start(bproj_bc[:], ins["bproj"].partition_broadcast(P)).then_inc(sem("ld_w"), 16)
            sp.dma_start(bo_bc[:], ins["bo"].partition_broadcast(P)).then_inc(sem("ld_w"), 16)
            sp.dma_start(fw[:].rearrange("p a d -> p (a d)"), ins["fw"]).then_inc(sem("ld_w"), 16)
            sp.dma_start(ffn_s[:].rearrange("p a k -> p (a k)"), ins["ffn_s"]).then_inc(sem("ld_w"), 16)

            for st in stages:
                if st[0] == "m":
                    for p in range(2):
                        if st == "m1":
                            sp.wait_ge(*reached("m0_down", EXPERTS))
                        sp.dma_start(wx[:, p, 0:2 * FE], ins["wx"][p, :, 0:2 * FE]).then_inc(sem(f"{st}_wgu{p}"), 16)
                        sp.dma_start(wx[:, p, 2 * FE:], ins["wx"][p, :, 2 * FE:]).then_inc(sem(f"{st}_wd{p}"), 16)
                    with sp.Fori(0, EXPERTS // 2 - 1) as t:
                        for p in range(2):
                            sp.wait_ge(*reached(f"{st}_up", t * 4 + (2 * p + 2)))
                            sp.dma_start(wx[:, p, 0:2 * FE], ins["wx"][t * 2 + (p + 2), :, 0:2 * FE]).then_inc(sem(f"{st}_wgu{p}"), 16)
                            sp.wait_ge(*reached(f"{st}_down", t * 2 + (p + 1)))
                            sp.dma_start(wx[:, p, 2 * FE:], ins["wx"][t * 2 + (p + 2), :, 2 * FE:]).then_inc(sem(f"{st}_wd{p}"), 16)
                if st == "f0":
                    if "m1" in stages:
                        sp.wait_ge(*reached("m1_slots", BATCHES))
                    sp.dma_start(ffw[:], ins["ffw"]).then_inc(sem("ld_ffw"), 16)
            last = stages[-1]
            view = out.rearrange("(t p) d -> p t d", p=P)
            for c in range(CHUNKS):
                sp.wait_ge(sem(f"{last}_x"), 2 * c + 2)
                sp.dma_start(view[:, 4 * c:4 * c + 4, :], x[:, 4 * c:4 * c + 4, :]).then_inc(sem("stored"), 16)
            sp.wait_ge(sem("stored"), 16 * CHUNKS)

        @block.gpsimd
        def _(pool):
            pool.memset(half_power[:], -0.5).then_inc(sem("pool_const"), 1)
            pool.memset(eps2[:], LN_EPS).then_inc(sem("pool_const"), 1)
            pool.wait_ge(sem("pool_const"), 2)

            def slot_norm():
                pool.wait_ge(sem("se_moments"), ST)
                go = Steps("se_pool")
                pool.tensor_scalar(se_r[:, 0, :], se_stat[:, :, 7], LN_EPS, None, ALU.add).then_inc(go.sem, go.step())
                pool.wait_ge(go.sem, plain(pool, go.n))
                pool.tensor_tensor(se_r[:, 1, :], se_r[:, 0, :], half_power[:, 0:ST], ALU.pow).then_inc(go.sem, go.step())
                pool.wait_ge(go.sem, plain(pool, go.n))
                for t in range(ST):
                    row = logits[:, 1, 0, t * D:t * D + D]
                    pool.tensor_scalar(row, row, se_stat[:, t, 6:7], se_r[:, 1, t:t + 1],
                                       ALU.subtract, ALU.mult).then_inc(sem("se_norm"), 1)

            def norm(st, b, p):
                moe_ln = st[0] == "m"
                key = "m" if moe_ln else "a"
                pool.wait_ge(*reached(f"{before[st]}_x", b + 1, pool))
                go = Steps(f"{st}_pool", b * LN_STEPS[key])
                var = moments[:, batch(b), 1]
                r = rstd[:, p, :]
                pool.tensor_tensor(r[:, 0:2], var, eps2[:], ALU.add).then_inc(go.sem, go.step())
                pool.wait_ge(go.sem, plain(pool, go.n))
                pool.tensor_tensor(r[:, 2:4], r[:, 0:2], half_power[:, 0:2], ALU.pow).then_inc(go.sem, go.step())
                pool.wait_ge(go.sem, plain(pool, go.n))
                scale = r[:, 2:4]
                if moe_ln:
                    pool.tensor_tensor(r[:, 4:6], scale, scale, ALU.mult).then_inc(go.sem, go.step())
                    pool.wait_ge(go.sem, plain(pool, go.n))
                    pool.tensor_tensor(r[:, 0:2], r[:, 4:6], var, ALU.mult).then_inc(go.sem, go.step())
                    pool.wait_ge(go.sem, plain(pool, go.n))
                    pool.tensor_scalar(r[:, 4:6], r[:, 0:2], LN_EPS, None, ALU.add).then_inc(go.sem, go.step())
                    pool.wait_ge(go.sem, plain(pool, go.n))
                    pool.tensor_tensor(r[:, 0:2], r[:, 4:6], half_power[:, 0:2], ALU.pow).then_inc(go.sem, go.step())
                    pool.wait_ge(go.sem, plain(pool, go.n))
                    pool.tensor_tensor(r[:, 6:8], r[:, 0:2], scale, ALU.mult).then_inc(go.sem, go.step())
                    pool.wait_ge(go.sem, plain(pool, go.n))
                    scale = r[:, 6:8]
                if due(b - 1):
                    pool.wait_ge(*reached(f"{st}_turned", b - 1, pool))
                if isinstance(b, int) and b == 0 and before[st] != "init":
                    pool.wait_ge(*reached(f"{before[st]}_turned", BATCHES, pool))
                pool.tensor_tensor(z_in[:, p], x[:, batch(b), :],
                                          moments[:, batch(b), 0:1].broadcast_to([P, PER, D]), ALU.subtract).then_inc(go.sem, go.step())
                pool.wait_ge(go.sem, plain(pool, go.n))
                pool.tensor_tensor(z_in[:, p], z_in[:, p], scale.unsqueeze(2).broadcast_to([P, PER, D]), ALU.mult).then_inc(go.sem, go.step())
                if moe_ln:
                    pool.wait_ge(go.sem, plain(pool, go.n))
                    pool.tensor_tensor(z_in[:, p], z_in[:, p],
                                              affine[:, 0:1, :].broadcast_to([P, PER, D]), ALU.mult).then_inc(go.sem, go.step())
                    pool.wait_ge(go.sem, plain(pool, go.n))
                    pool.tensor_tensor(z_in[:, p], z_in[:, p],
                                              affine[:, 1:2, :].broadcast_to([P, PER, D]), ALU.add).then_inc(go.sem, go.step())

            def moe_pool(st):
                def keep(b, p):
                    if due(b - 1):
                        pool.wait_ge(*reached(f"{st}_slots", b - 1, pool))
                    pool.wait_ge(*reached(f"{st}_pool", b * LN_STEPS["m"] + LN_STEPS["m"], pool))
                    pool.tensor_copy(z_slots[:, p], z_in[:, p]).then_inc(sem(f"{st}_kept"), 1)

                def slot_shifts(b, p):
                    if due(b - 1):
                        pool.wait_ge(*reached(f"{st}_spread", b - 1, pool))
                    pool.wait_ge(*reached(f"{st}_lnz", b + 1, pool))
                    go = Steps(f"{st}_shift", b * 3)
                    pool.tensor_tensor(shift_s[:, p], negmax_s[:, p, :], lnz_s[:, p, :], ALU.subtract).then_inc(go.sem, go.step())
                    pool.wait_ge(go.sem, plain(pool, go.n))
                    pool.tensor_copy(shift_hi[:, p], shift_s[:, p]).then_inc(go.sem, go.step())
                    pool.wait_ge(go.sem, plain(pool, go.n))
                    pool.tensor_tensor(shift_lo[:, p], shift_s[:, p], as32(shift_hi[:, p]), ALU.subtract).then_inc(go.sem, go.step())

                norm(st, 0, 0)
                keep(0, 0)
                norm(st, 1, 1)
                keep(1, 1)
                slot_shifts(0, 0)

                def step(b, j, p, ahead=True):
                    if ahead:
                        norm(st, b + 2, p)
                    if ahead or isinstance(b, int) and b < BATCHES - 1:
                        slot_shifts(b + 1, 1 - p)
                    if ahead:
                        keep(b + 2, p)

                step(0, 0, 0)
                looped(pool, step, 1, BATCHES - 3)
                step(BATCHES - 3, 2, 1)
                step(BATCHES - 2, 3, 0, False)

            for st in stages:
                if st == "m0":
                    slot_norm()
                if st[0] == "m":
                    pool.wait_ge(sem("ld_affine"), 16)
                    moe_pool(st)
                else:
                    all_batches(pool, lambda b, j, p: norm(st, b, p))

        @block.tensor
        def _(pe):
            def turn(dst, src):
                return pe.transpose(dst, src, ident[:])

            def three(dst, a_hi, a_lo, b_hi, b_lo, start, stop):
                pe.matmul(dst, a_hi, b_lo, start=start, stop=False, skip_group_check=True)
                pe.matmul(dst, a_lo, b_hi, start=False, stop=False, skip_group_check=True)
                return pe.matmul(dst, a_hi, b_hi, start=False, stop=stop, skip_group_check=True)

            def turn_batch(st, b, p, bank):
                k = LN_STEPS["m" if st[0] == "m" else "a"]
                pe.wait_ge(*reached(f"{st}_pool", b * k + k))
                for i in range(PER):
                    mm = turn(ps[:, bank, i * P:i * P + P], z_in[:, p, i, :])
                mm.then_inc(sem(f"{st}_turned"), 1)

            def moe_tensor(st):
                ROW0, ROW1 = 4, 6

                def tokens(b, p):
                    if due((b - 1) * 2):
                        pe.wait_ge(*reached(f"{st}_sub", (b - 1) * 2))
                    turn_batch(st, b, p, ROW0)

                def rows(b, p):
                    pe.wait_ge(*reached(f"{st}_zthi", b + 1))
                    pe.wait_ge(*reached(f"{st}_ztlo", b + 1))
                    for i in range(PER):
                        if i == 1:
                            if due(b - 1):
                                pe.wait_ge(*reached(f"{st}_slots_a", b - 1))
                            if due(b - 1):
                                pe.wait_ge(*reached(f"{st}_slots_b", b - 1))
                        for h in range(2):
                            cut = slice(h * 512, h * 512 + 512)
                            mm = three(ps[:, (ROW0, ROW1)[i] + h, :], zt_hi[:, p, i * P:i * P + P], zt_lo[:, p, i * P:i * P + P],
                                       se_hi[:, p, cut], se_lo[:, p, cut], True, True)
                        mm.then_inc(sem(f"{st}_rows"), 1)

                def columns(b, p, ks):
                    for k in ks:
                        if due((b - 1) * 4 + (k + 1)):
                            pe.wait_ge(*reached(f"{st}_comb", (b - 1) * 4 + (k + 1)))
                        for h in range(2):
                            t = 2 * k + h
                            cut = slice(t * P, t * P + P)
                            mm = three(ps[:, k, h * SEQ:h * SEQ + SEQ], se_hi[:, p, cut], se_lo[:, p, cut],
                                       zt_hi[:, p, :], zt_lo[:, p, :], h == 0, False)
                        mm.then_inc(sem(f"{st}_columns"), 1)

                def spread(b, p):
                    pe.wait_ge(*reached(f"{st}_shift", b * 3 + 3))
                    for t in range(ST):
                        dst = ps[:, ROW0 + t // 4, t % 4 * P:t % 4 * P + P]
                        pe.matmul(dst, shift_lo[:, p, t:t + 1].broadcast_to([P, P]), ident_r[:], start=True, stop=False)
                        mm = pe.matmul(dst, shift_hi[:, p, t:t + 1].broadcast_to([P, P]), ident_r[:], start=False, stop=True)
                    mm.then_inc(sem(f"{st}_spread"), 1)

                def shift(b, p):
                    pe.wait_ge(*reached(f"{st}_maxn", b * 2 + 2))
                    for k in range(4):
                        pe.wait_ge(*reached(f"{st}_zs", b * 4 + (k + 1)))
                        for i in range(PER):
                            mm = pe.matmul(ps[:, k, :].rearrange("p (h i n) -> p i h n", h=2, i=PER)[:, i],
                                           negmax_n[:, p, i:i + 1].broadcast_to([P, P]),
                                           ident_r[:].unsqueeze(1).broadcast_to([P, 2, P]),
                                           start=False, stop=i == PER - 1, skip_group_check=True)
                        mm.then_inc(sem(f"{st}_shifted"), 1)

                def slots(b, p):
                    pe.wait_ge(*reached(f"{st}_disp", b * 2 + 2))
                    pe.wait_ge(*reached(f"{st}_kept", b + 1))
                    for h in range(2):
                        for i in range(PER):
                            mm = pe.matmul(ps[:, ROW1 + h, :], z_slots[:, p, i, :], logits[:, p, i, h * 512:h * 512 + 512],
                                           start=i == 0, stop=i == PER - 1)
                    mm.then_inc(sem(f"{st}_slots"), 1)

                tokens(0, 0)
                rows(0, 0)
                columns(0, 0, range(4))
                pe.wait_ge(*reached(f"{st}_copied", 1))
                shift(0, 0)
                tokens(1, 1)

                def step(b, j, p, ahead=True, last=False):
                    if not last:
                        rows(b + 1, 1 - p)
                        columns(b + 1, 1 - p, (0, 1))
                        pe.wait_ge(*reached(f"{st}_copied", b * 2 + 3))
                    spread(b, p)
                    if not last:
                        columns(b + 1, 1 - p, (2, 3))
                        pe.wait_ge(*reached(f"{st}_copied", b * 2 + 4))
                    slots(b, p)
                    if ahead:
                        tokens(b + 2, p)
                    if not last:
                        shift(b + 1, 1 - p)

                step(0, 0, 0)
                looped(pe, step, 1, BATCHES - 3)
                step(BATCHES - 3, 2, 1)
                step(BATCHES - 2, 3, 0, False)
                step(BATCHES - 1, 3, 1, False, True)

                def up(e, t, p):
                    pe.wait_ge(*reached(f"{st}_wgu{p}", (t + 1) * 16))
                    for f in range(2):
                        for which in range(2):
                            if due((e - 1) * 2 + (f + 1)):
                                pe.wait_ge(*reached(f"{st}_gelu" if which == 0 else f"{st}_h", (e - 1) * 2 + (f + 1)))
                            w0 = which * FE + f * P
                            mm = pe.matmul(ps[:, 2 * which + f, :], wx[:, p, w0:w0 + P],
                                           expert_io[:, t + 1, p * 512:p * 512 + 512] if isinstance(t, int) else
                                           expert_io[:, bass.ds(t + 1, 1), p * 512:p * 512 + 512].rearrange("p a n -> p (a n)"),
                                           start=True, stop=True)
                            mm.then_inc(sem(f"{st}_gate" if which == 0 else f"{st}_up"), 1)

                def down(e, t, p):
                    pe.wait_ge(*reached(f"{st}_wd{p}", (t + 1) * 16))
                    pe.wait_ge(*reached(f"{st}_h", e * 2 + 2))
                    if due((e - 1) * 2):
                        pe.wait_ge(*reached(f"{st}_eo", (e - 1) * 2))
                    for jj in range(BATCHES // 2):
                        for f in range(2):
                            mm = pe.matmul(ps[:, 4 + p, jj * P:jj * P + P], hmid[:, p, f, jj * P:jj * P + P],
                                           wx[:, p, 2 * FE + f * D:2 * FE + f * D + D], start=f == 0, stop=f == 1)
                    mm.then_inc(sem(f"{st}_down"), 1)

                pe.wait_ge(*reached(f"{st}_comb", BATCHES * 4))
                pe.wait_ge(*reached(f"{st}_slots_a", BATCHES))
                pe.wait_ge(*reached(f"{st}_slots_b", BATCHES))
                def pair(t):
                    up(t * 2 + 1, t, 1)
                    down(t * 2, t, 0)
                    up(t * 2 + 2, t + 1, 0)
                    down(t * 2 + 1, t, 1)

                up(0, 0, 0)
                pair(0)
                with pe.Fori(1, ST - 1) as t:
                    pair(t)
                up(EXPERTS - 1, ST - 1, 1)
                down(EXPERTS - 2, ST - 1, 0)
                down(EXPERTS - 1, ST - 1, 1)

                def combine(b, j, p):
                    pe.wait_ge(*reached(f"{st}_staged_a", b + 1))
                    pe.wait_ge(*reached(f"{st}_staged_b", b + 1))
                    if due(b - 1):
                        pe.wait_ge(*reached(f"{st}_x", b - 1))
                    for i in range(PER):
                        for t in range(ST):
                            w = logits[:, p].rearrange("p i (t n) -> p (i t) n", t=ST // PER)
                            mm = pe.matmul(ps[:, 2 * p + i, 0:OW - 1], w[:, t, i * P:i * P + P],
                                           expert_io[:, t, b * OW:b * OW + OW - 1] if isinstance(b, int) else
                                           expert_io[:, t, bass.ds(b * OW, OW - 1)],
                                           start=t == 0, stop=t == ST - 1)
                        mm.then_inc(sem(f"{st}_combined"), 1)

                pe.wait_ge(*reached(f"{st}_eo", EXPERTS * 2))
                pe.wait_ge(*reached(f"{st}_sums", ST))
                pe.wait_ge(*reached(f"{st}_gelu", EXPERTS * 2))
                all_batches(pe, combine)

            def linear_attention_tensor(st):
                def first(b, p):
                    B = 4 * p
                    if due(b - 1):
                        pe.wait_ge(*reached(f"{st}_x", b - 1))
                    turn_batch(st, b, p, B + 2)
                    pe.wait_ge(*reached(f"{st}_zt", b + 1))
                    pe.matmul(ps[:, B, 0:SEQ], wqkv[:, 0:D], la_zt[:, p, :], start=True, stop=True)
                    for i in range(PER):
                        mm = pe.matmul(ps[:, B, SEQ + i * P:SEQ + i * P + P], la_zt[:, p, i * P:i * P + P], wqkv[:, D:2 * D],
                                       start=True, stop=True)
                    mm.then_inc(sem(f"{st}_qkp"), 1)
                    for i in range(PER):
                        mm = pe.matmul(ps[:, B + 1, i * P:i * P + P], la_zt[:, p, i * P:i * P + P], wqkv[:, 2 * D:3 * D],
                                       start=True, stop=True)
                    mm.then_inc(sem(f"{st}_vp"), 1)

                def second(b, p):
                    B = 4 * p
                    pe.wait_ge(*reached(f"{st}_v", b + 1))
                    pe.wait_ge(*reached(f"{st}_qk", b + 1))
                    for i in range(PER):
                        mm = pe.matmul(ps[:, B + 1, SEQ:SEQ + D + 1], la_qk[:, p, SEQ + i * P:SEQ + i * P + P],
                                       la_v[:, p, i, :], start=i == 0, stop=i == PER - 1)
                    mm.then_inc(sem(f"{st}_kvp"), 1)
                    pe.wait_ge(*reached(f"{st}_kv", b * 2 + 2))
                    for k in range(2):
                        mm = pe.matmul(ps[:, B + 3, k * SEQ:k * SEQ + SEQ], la_kv[:, p, k, :], la_qk[:, p, 0:SEQ],
                                       start=True, stop=True)
                    mm.then_inc(sem(f"{st}_op"), 1)
                    pe.wait_ge(*reached(f"{st}_steps", b * 5 + 3))
                    for i in range(PER):
                        mm = pe.matmul(ps[:, B + 2, SEQ + i * P:SEQ + i * P + P], la_o[:, p, 0, i * P:i * P + P], wproj[:],
                                       start=True, stop=True)
                    mm.then_inc(sem(f"{st}_yp"), 1)

                def step(b, j, p):
                    if not (isinstance(b, int) and b == BATCHES - 1):
                        first(b + 1, 1 - p)
                    second(b, p)

                first(0, 0)
                all_batches(pe, step)

            def ffn_tensor(st):
                def tokens(b, p):
                    if due(b - 1):
                        pe.wait_ge(*reached(f"{st}_zt", b - 1))
                    turn_batch(st, b, p, 4 + p)

                def chunk_of(t, c, k=None):
                    cut = slice(c * CHUNK, c * CHUNK + CHUNK) if isinstance(c, int) else bass.ds(c * CHUNK, CHUNK)
                    return t[:, cut] if k is None else t[:, k, cut]

                def gated(c):
                    pe.wait_ge(*reached(f"{st}_zt", c * 2 + 2))
                    flat = zt_all[:].rearrange("p b n -> p (b n)")
                    for o in range(HK):
                        r = o % 2
                        if due(c * 4 + (o - 1)):
                            pe.wait_ge(*reached(f"{st}_silu", c * 4 + (o - 1)))
                        pe.matmul(ps[:, 2 * r, :], w1[:, o * P:o * P + P], chunk_of(flat, c), start=True, stop=True)\
                            .then_inc(sem(f"{st}_p1"), 1)
                        if due(c * 4 + (o - 1)):
                            pe.wait_ge(*reached(f"{st}_ha", c * 4 + (o - 1)))
                        pe.matmul(ps[:, 2 * r + 1, :], w2[:, o * P:o * P + P], chunk_of(flat, c), start=True, stop=True)\
                            .then_inc(sem(f"{st}_p2"), 1)

                def hidden(c, q, w, src, done, made):
                    for o in range(HK):
                        if due(c * 4 + (o + 1 - 8)):
                            pe.wait_ge(*reached(f"{st}_{done}", c * 4 + (o + 1 - 8)))
                        for k in range(HK):
                            mm = pe.matmul(ps[:, 4 * q + o, :], w[:, k, o * P:o * P + P], chunk_of(src, c, k),
                                           start=k == 0, stop=k == HK - 1)
                        mm.then_inc(sem(f"{st}_{made}"), 1)

                def last_product(c, q):
                    if due(c - 1):
                        pe.wait_ge(*reached(f"{st}_yt", c - 1))
                    for k in range(HK):
                        mm = pe.matmul(ps[:, q, :], w3[:, k, :], chunk_of(act_a, c, k), start=k == 0, stop=k == HK - 1)
                    mm.then_inc(sem(f"{st}_p3"), 1)

                def turn_back(c, q):
                    pe.wait_ge(*reached(f"{st}_yt", c + 1))
                    if due((c - 1) * 2):
                        pe.wait_ge(*reached(f"{st}_x", (c - 1) * 2))
                    for i in range(CHUNK // P):
                        mm = turn(ps[:, 2 + q, i * P:i * P + P], y_t[:, q, i * P:i * P + P])
                    mm.then_inc(sem(f"{st}_yp"), 1)

                pe.wait_ge(sem("ld_ffw"), 16)
                tokens(0, 0)
                tokens(1, 1)
                tokens(2, 0)
                tokens(3, 1)
                gated(0)
                with pe.Fori(1, CHUNKS - 1) as c:
                    tokens(c * 2 + 2, 0)
                    tokens(c * 2 + 3, 1)
                    gated(c)
                gated(CHUNKS - 1)
                pe.wait_ge(*reached(f"{st}_zt", BATCHES))
                pe.wait_ge(*reached(f"{st}_ha", CHUNKS * HK))
                hidden(0, 0, h1, act_a, "hb", "pb")
                hidden(1, 1, h1, act_a, "hb", "pb")
                with pe.Fori(1, CHUNKS // 2) as c:
                    hidden(c * 2, 0, h1, act_a, "hb", "pb")
                    hidden(c * 2 + 1, 1, h1, act_a, "hb", "pb")
                pe.wait_ge(*reached(f"{st}_hb", CHUNKS * HK))
                hidden(0, 0, h2, act_b, "hc", "pc")
                hidden(1, 1, h2, act_b, "hc", "pc")
                with pe.Fori(1, CHUNKS // 2) as c:
                    hidden(c * 2, 0, h2, act_b, "hc", "pc")
                    hidden(c * 2 + 1, 1, h2, act_b, "hc", "pc")
                pe.wait_ge(*reached(f"{st}_hc", CHUNKS * HK))
                last_product(0, 0)
                for c in range(CHUNKS):
                    if c < CHUNKS - 1:
                        last_product(c + 1, (c + 1) % 2)
                    turn_back(c, c % 2)

            def favor_tensor(st):
                def first(b, p):
                    if due((b - 1) * 2):
                        pe.wait_ge(*reached(f"{st}_phit", (b - 1) * 2))
                    turn_batch(st, b, p, 0)
                    pe.wait_ge(*reached(f"{st}_zt", b + 1))
                    for k in range(2):
                        mm = pe.matmul(ps[:, 1, k * SEQ:k * SEQ + SEQ], fw[:, k, :], fa_zt[:, p, :], start=True, stop=True)
                    mm.then_inc(sem(f"{st}_qktp"), 1)
                    for k in range(2):
                        for i in range(PER):
                            mm = pe.matmul(ps[:, 2, k * SEQ + i * P:k * SEQ + i * P + P], fa_zt[:, p, i * P:i * P + P], fw[:, k, :],
                                           start=True, stop=True)
                    mm.then_inc(sem(f"{st}_qkp"), 1)
                    for i in range(PER):
                        mm = pe.matmul(ps[:, 3, i * P:i * P + P], fa_zt[:, p, i * P:i * P + P], fw[:, 2, :], start=True, stop=True)
                    mm.then_inc(sem(f"{st}_vp"), 1)
                    pe.wait_ge(*reached(f"{st}_qkt", b + 1))
                    for k in range(2):
                        for i in range(PER):
                            if due((b - 1) * 4 + (2 * k + i + 1)):
                                pe.wait_ge(*reached(f"{st}_sub", (b - 1) * 4 + (2 * k + i + 1)))
                            pe.matmul(ps[:, 4 + 2 * k + i, :], fa_qkt[:, p, k, i * P:i * P + P], proj_bd[:], start=True, stop=True)\
                                .then_inc(sem(f"{st}_xw"), 1)

                def second(b, p):
                    pe.wait_ge(*reached(f"{st}_phi", b + 1))
                    pe.wait_ge(*reached(f"{st}_v", b + 1))
                    for g in range(FG):
                        for i in range(PER):
                            mm = pe.matmul(ps[:, 3, SEQ + g * VA:SEQ + g * VA + VA], fa_phi[:, p, 2 + i, g * P:g * P + P],
                                           fa_vaug[:, p, i, g, :], start=i == 0, stop=i == PER - 1)
                    mm.then_inc(sem(f"{st}_kvp"), 1)
                    for i in range(PER):
                        for g in range(FG):
                            mm = turn(ps[:, i, g * P:g * P + P], fa_phi[:, p, i, g * P:g * P + P])
                        mm.then_inc(sem(f"{st}_phitp"), 1)
                    pe.wait_ge(*reached(f"{st}_phit", b * 2 + 2))
                    pe.wait_ge(*reached(f"{st}_kv", b + 1))
                    for i in range(PER):
                        for g in range(FG):
                            mm = pe.matmul(ps[:, 2, i * SEQ + g * VA:i * SEQ + g * VA + VA], fa_phit[:, p, i, g, :], fa_kv[:, p, g, :],
                                           start=True, stop=True)
                    mm.then_inc(sem(f"{st}_np"), 1)
                    pe.wait_ge(*reached(f"{st}_o", b + 1))
                    for i in range(PER):
                        mm = turn(ps[:, 0, i * P:i * P + P], fa_o[:, p, i, :])
                    mm.then_inc(sem(f"{st}_otp"), 1)
                    pe.wait_ge(*reached(f"{st}_ot", b + 1))
                    for i in range(PER):
                        mm = pe.matmul(ps[:, 1, i * P:i * P + P], fa_ot[:, p, i * P:i * P + P], fw[:, 3, :], start=True, stop=True)
                    mm.then_inc(sem(f"{st}_yp"), 1)

                def step(b, j, p):
                    second(b, p)
                    if not (isinstance(b, int) and b == BATCHES - 1):
                        pe.wait_ge(*reached(f"{st}_x", b + 1))
                        first(b + 1, 1 - p)

                first(0, 0)
                all_batches(pe, step)

            pe.wait_ge(sem("ld_const"), 16)
            if "m0" in stages:
                for t in range(ST):
                    pe.wait_ge(sem("se_norm"), t + 1)
                    turn(ps[:, t // 4, t % 4 * P:t % 4 * P + P], logits[:, 1, 0, t * D:t * D + D]).then_inc(sem("se_turned"), 1)
                pe.wait_ge(sem("se_ready"), 7)
                pe.wait_ge(sem("dve_const"), 1)
            for st in stages:
                if before[st] != "init":
                    pe.wait_ge(sem(f"{before[st]}_x"), BATCHES)
                if st == "la" or before[st] == "init":
                    pe.wait_ge(sem("ld_w"), 16 * 12)
                {"m": moe_tensor, "l": linear_attention_tensor, "f": ffn_tensor}[st[0]](st) if st != "fa" else favor_tensor(st)

        @block.scalar
        def _(act):
            def moe_scalar(st):
                def tokens(b, p):
                    act.wait_ge(*reached(f"{st}_turned", b + 1))
                    act.copy(zt_hi[:, p, :], ps[:, 4, 0:SEQ]).then_inc(sem(f"{st}_zthi"), 1)

                def copies(b, p):
                    if due(b - 1):
                        act.wait_ge(*reached(f"{st}_slots", b - 1))
                    for i in range(PER):
                        act.wait_ge(*reached(f"{st}_rows", b * 2 + (i + 1)))
                        act.copy(logits[:, p, i, :], ps[:, 4 + 2 * i:6 + 2 * i, :].rearrange("p h n -> p (h n)"))\
                            .then_inc(sem(f"{st}_copied"), 1)

                def sums(b, p, ks):
                    for k in ks:
                        act.wait_ge(*reached(f"{st}_maxs", b * 4 + (k + 1)))
                        if due(b * 4 + (k - 1)):
                            act.wait_ge(*reached(f"{st}_zs", b * 4 + (k - 1)))
                        for h in range(2):
                            t = 2 * k + h
                            last = act.activation(junk[:, 2 * (k % 2) + h, :], ps[:, k, h * SEQ:h * SEQ + SEQ], ACT.Exp,
                                                  bias=negmax_s[:, p, t:t + 1], accum_out=zsum_s[:, p, t:t + 1])
                        last.then_inc(sem(f"{st}_zs"), 1)

                def logs(b, p):
                    act.wait_ge(*reached(f"{st}_zs", b * 4 + 4))
                    act.activation(lnz_s[:, p, :], zsum_s[:, p, :], ACT.Ln).then_inc(sem(f"{st}_lnz"), 1)

                def dispatch(b, p):
                    for i in range(PER):
                        act.wait_ge(*reached(f"{st}_sub", b * 2 + (i + 1)))
                        act.activation(logits[:, p, i, :], logits[:, p, i, :], ACT.Exp).then_inc(sem(f"{st}_disp"), 1)

                def weights(b, p):
                    for k in range(4):
                        act.wait_ge(*reached(f"{st}_shifted", b * 4 + (k + 1)))
                        dst = comb[:, b, 2 * k:2 * k + 2, :] if isinstance(b, int) else comb[:, bass.ds(b, 1), 2 * k:2 * k + 2, :].rearrange("p a t n -> p (a t) n")
                        act.activation(dst, ps[:, k, :].rearrange("p (t n) -> p t n", t=2), ACT.Exp).then_inc(sem(f"{st}_comb"), 1)

                def slots_out(b, j, p):
                    act.wait_ge(*reached(f"{st}_slots", b + 1))
                    store_slots(act.copy, j, p, 0).then_inc(sem(f"{st}_slots_a"), 1)

                act.preload_act_table_set("natural_log_exp_and_others")
                tokens(0, 0)
                copies(0, 0)
                sums(0, 0, range(4))
                logs(0, 0)
                weights(0, 0)
                tokens(1, 1)

                def step(b, j, p, ahead=True, last=False):
                    if not last:
                        copies(b + 1, 1 - p)
                        sums(b + 1, 1 - p, (0, 1))
                    dispatch(b, p)
                    if not last:
                        sums(b + 1, 1 - p, (2, 3))
                        logs(b + 1, 1 - p)
                    slots_out(b, j, p)
                    if ahead:
                        tokens(b + 2, p)
                    if not last:
                        weights(b + 1, 1 - p)

                step(0, 0, 0)
                looped(act, step, 1, BATCHES - 3)
                step(BATCHES - 3, 2, 1)
                step(BATCHES - 2, 3, 0, False)
                step(BATCHES - 1, 3, 1, False, True)

                def gelus(e, p):
                    for f in range(2):
                        act.wait_ge(*reached(f"{st}_gate", e * 2 + (f + 1)))
                        if due((e - 1) * 2 + (f + 1)):
                            act.wait_ge(*reached(f"{st}_h", (e - 1) * 2 + (f + 1)))
                        bias = bgu[:, 0, e, f:f + 1] if isinstance(e, int) else bgu[:, 0, bass.ds(e, 1), f]
                        act.activation(gate[:, f, :], ps[:, f, :], ACT.Gelu, bias=bias).then_inc(sem(f"{st}_gelu"), 1)

                gelus(0, 0)
                with act.Fori(0, ST - 1) as t:
                    gelus(t * 2 + 1, 1)
                    gelus(t * 2 + 2, 0)
                gelus(EXPERTS - 1, 1)

                def stage(b, j, p):
                    if due((b - 1) * 2):
                        act.wait_ge(*reached(f"{st}_combined", (b - 1) * 2))
                    src = comb[:, b, 0:ST // 2, :] if isinstance(b, int) else comb[:, bass.ds(b, 1), 0:ST // 2, :].rearrange("p a t n -> p (a t) n")
                    act.copy(logits[:, p, 0, :].rearrange("p (t n) -> p t n", t=ST // 2), src).then_inc(sem(f"{st}_staged_a"), 1)

                all_batches(act, stage)

            def linear_attention_scalar(st):
                def first(b, p):
                    B = 4 * p
                    act.wait_ge(*reached(f"{st}_turned", b + 1))
                    act.copy(la_zt[:, p, :], ps[:, B + 2, 0:SEQ]).then_inc(sem(f"{st}_zt"), 1)
                    act.wait_ge(*reached(f"{st}_vp", b + 1))
                    act.copy(la_v[:, p, :, 0:D], ps[:, B + 1, 0:SEQ].rearrange("p (i d) -> p i d", i=PER)).then_inc(sem(f"{st}_v"), 1)
                    act.wait_ge(*reached(f"{st}_min", b + 1))
                    act.activation(la_min[:, p, :], la_min[:, p, :], ACT.Exp).then_inc(sem(f"{st}_exp"), 1)
                act.wait_ge(*reached(f"{st}_vones", 1))
                all_batches(act, lambda b, j, p: first(b, p))

            def ffn_scalar(st):
                def chunk_of(t, c, o):
                    return t[:, o, c * CHUNK:c * CHUNK + CHUNK] if isinstance(c, int) else t[:, o, bass.ds(c * CHUNK, CHUNK)]

                def tokens(b, p):
                    act.wait_ge(*reached(f"{st}_turned", b + 1))
                    dst = zt_all[:, b, :] if isinstance(b, int) else zt_all[:, bass.ds(b, 1), :].rearrange("p a n -> p (a n)")
                    act.copy(dst, ps[:, 4 + p, 0:SEQ]).then_inc(sem(f"{st}_zt"), 1)

                def silus(c):
                    for o in range(HK):
                        r = o % 2
                        act.wait_ge(*reached(f"{st}_p1", c * 4 + (o + 1)))
                        if due(c * 4 + (o - 1)):
                            act.wait_ge(*reached(f"{st}_ha", c * 4 + (o - 1)))
                        act.activation(silu_out[:, r, :], ps[:, 2 * r, :], ACT.Silu, scale=ffn_s[:, 0, o:o + 1])\
                            .then_inc(sem(f"{st}_silu"), 1)

                def gelus(c, q, dst, which, made, done):
                    for o in range(HK):
                        act.wait_ge(*reached(f"{st}_{made}", c * 4 + (o + 1)))
                        act.activation(chunk_of(dst, c, o), ps[:, 4 * q + o, :], ACT.Gelu, scale=ffn_s[:, which, o:o + 1])\
                            .then_inc(sem(f"{st}_{done}"), 1)

                for b in range(4):
                    tokens(b, b % 2)
                silus(0)
                with act.Fori(1, CHUNKS - 1) as c:
                    tokens(c * 2 + 2, 0)
                    tokens(c * 2 + 3, 1)
                    silus(c)
                silus(CHUNKS - 1)
                for dst, which, made, done in ((act_b, 2, "pb", "hb"), (act_a, 3, "pc", "hc")):
                    with act.Fori(0, CHUNKS // 2) as c:
                        gelus(c * 2, 0, dst, which, made, done)
                        gelus(c * 2 + 1, 1, dst, which, made, done)
                for c in range(CHUNKS):
                    act.wait_ge(*reached(f"{st}_p3", c + 1))
                    if due(c - 1):
                        act.wait_ge(*reached(f"{st}_yp", c - 1))
                    act.mul(y_t[:, c % 2, :], ps[:, c % 2, :], w3_s[:, 1:2]).then_inc(sem(f"{st}_yt"), 1)

            def favor_scalar(st):
                def first(b, p):
                    act.wait_ge(*reached(f"{st}_turned", b + 1))
                    act.copy(fa_zt[:, p, :], ps[:, 0, 0:SEQ]).then_inc(sem(f"{st}_zt"), 1)
                    act.wait_ge(*reached(f"{st}_qktp", b + 1))
                    act.mul(fa_qkt[:, p].rearrange("p k n -> p (k n)"), ps[:, 1, :], QK_SCALE).then_inc(sem(f"{st}_qkt"), 1)
                    act.wait_ge(*reached(f"{st}_qkp", b + 1))
                    act.activation(fa_sq[:, p, :], ps[:, 2, :], ACT.Square, scale=QK_SCALE * 0.5 ** 0.5).then_inc(sem(f"{st}_sq"), 1)
                    act.wait_ge(*reached(f"{st}_vp", b + 1))
                    act.copy(fa_vaug[:, p, :, :, 0:VA - 4], ps[:, 3, 0:SEQ].rearrange("p (i g d) -> p i g d", i=PER, g=FG))\
                        .then_inc(sem(f"{st}_v"), 1)
                    act.wait_ge(*reached(f"{st}_sub", b * 4 + 4))
                    act.activation(fa_phi[:, p].rearrange("p a f -> p (a f)"), fa_phi[:, p].rearrange("p a f -> p (a f)"), ACT.Exp)\
                        .then_inc(sem(f"{st}_exp"), 1)

                def second(b, p):
                    for i in range(PER):
                        act.wait_ge(*reached(f"{st}_phitp", b * 2 + (i + 1)))
                        act.copy(fa_phit[:, p, i].rearrange("p g n -> p (g n)"), ps[:, i, :]).then_inc(sem(f"{st}_phit"), 1)
                    act.wait_ge(*reached(f"{st}_otp", b + 1))
                    act.copy(fa_ot[:, p, :], ps[:, 0, 0:SEQ]).then_inc(sem(f"{st}_ot"), 1)

                def step(b, j, p):
                    second(b, p)
                    if not (isinstance(b, int) and b == BATCHES - 1):
                        first(b + 1, 1 - p)
                act.wait_ge(*reached(f"{st}_vones", 1))
                first(0, 0)
                all_batches(act, step)

            for st in stages:
                if before[st] != "init":
                    act.wait_ge(sem(f"{before[st]}_x"), BATCHES)
                if before[st] == "init":
                    act.wait_ge(sem("ld_w"), 16 * 12)
                {"m": moe_scalar, "l": linear_attention_scalar, "f": ffn_scalar}[st[0]](st) if st != "fa" else favor_scalar(st)

        @block.vector
        def _(dve):
            def after(st, b):
                go = Steps(f"{st}_mom", b * 4)
                if due(b):
                    dve.wait_ge(*reached(f"{st}_x", b, dve))
                for i in range(PER):
                    src = x[:, b * PER + i, :] if isinstance(b, int) else x[:, bass.ds(b * PER + i, 1), :].rearrange("p a d -> p (a d)")
                    dve.bn_stats(bn6[:, i, :], src).then_inc(go.sem, go.step())
                dve.wait_ge(go.sem, plain(dve, go.n))
                for i in range(PER):
                    dve.bn_aggr(fresh[:, i, :], bn6[:, i, :]).then_inc(go.sem, go.step())
                dve.wait_ge(go.sem, plain(dve, go.n))
                dve.tensor_copy(moments[:, batch(b), :], fresh[:]).then_inc(sem(f"{st}_x"), 1)

            def moe_vector(st):
                def tokens(b, p):
                    dve.wait_ge(*reached(f"{st}_zthi", b + 1))
                    dve.tensor_tensor(zt_lo[:, p, :], ps[:, 4, 0:SEQ], as32(zt_hi[:, p, :]), ALU.subtract)\
                        .then_inc(sem(f"{st}_ztlo"), 1)

                def max_n(b, p):
                    if due((b - 1) * 4):
                        dve.wait_ge(*reached(f"{st}_shifted", (b - 1) * 4))
                    for i in range(PER):
                        dve.wait_ge(*reached(f"{st}_copied", b * 2 + (i + 1)))
                        dve.tensor_reduce(negmax_n[:, p, i:i + 1], logits[:, p, i, :], AX_X, ALU.max, negate=True)\
                            .then_inc(sem(f"{st}_maxn"), 1)

                def max_s(b, p, ks):
                    for k in ks:
                        dve.wait_ge(*reached(f"{st}_columns", b * 4 + (k + 1)))
                        dve.tensor_reduce(negmax_s[:, p, 2 * k:2 * k + 2], ps[:, k, :].rearrange("p (t n) -> p t n", t=2),
                                          AX_X, ALU.max, negate=True).then_inc(sem(f"{st}_maxs"), 1)

                def subtract(b, p):
                    dve.wait_ge(*reached(f"{st}_spread", b + 1))
                    for i in range(PER):
                        dve.tensor_tensor(logits[:, p, i, :], logits[:, p, i, :],
                                          ps[:, 4:6, :].rearrange("p h n -> p (h n)"), ALU.add).then_inc(sem(f"{st}_sub"), 1)

                def slots_out(b, j, p):
                    dve.wait_ge(*reached(f"{st}_slots", b + 1))
                    store_slots(dve.tensor_copy, j, p, 1).then_inc(sem(f"{st}_slots_b"), 1)

                tokens(0, 0)
                max_n(0, 0)
                max_s(0, 0, range(4))
                tokens(1, 1)

                def step(b, j, p, ahead=True, last=False):
                    if not last:
                        max_s(b + 1, 1 - p, (0, 1))
                    subtract(b, p)
                    if not last:
                        max_s(b + 1, 1 - p, (2, 3))
                        max_n(b + 1, 1 - p)
                    slots_out(b, j, p)
                    if ahead:
                        tokens(b + 2, p)

                step(0, 0, 0)
                looped(dve, step, 1, BATCHES - 3)
                step(BATCHES - 3, 2, 1)
                step(BATCHES - 2, 3, 0, False)
                step(BATCHES - 1, 3, 1, False, True)

                def mix(e, p):
                    for f in range(2):
                        dve.wait_ge(*reached(f"{st}_gelu", e * 2 + (f + 1)))
                        dve.wait_ge(*reached(f"{st}_up", e * 2 + (f + 1)))
                        if due(e - 1):
                            dve.wait_ge(*reached(f"{st}_down", e - 1))
                        bias = bgu[:, 1, e, f:f + 1] if isinstance(e, int) else bgu[:, 1, bass.ds(e, 1), f]
                        dve.scalar_tensor_tensor(hmid[:, p, f, :], ps[:, 2 + f, :], bias, gate[:, f, :], ALU.add, ALU.mult)\
                            .then_inc(sem(f"{st}_h"), 1)

                def outputs(e, t, p):
                    dve.wait_ge(*reached(f"{st}_down", e + 1))
                    for half in range(2):
                        rows = slice(half * 64, half * 64 + 64)
                        block_t = expert_io[rows, t, :] if isinstance(t, int) else expert_io[rows, bass.ds(t, 1), :].rearrange("p a n -> p (a n)")
                        dst = block_t.rearrange("p (j q o) -> p q j o", q=2, o=OW)[:, half ^ p, :, 0:D]
                        bias = bd_bc[rows, e:e + 1, :] if isinstance(e, int) else bd_bc[rows, bass.ds(e, 1), :]
                        dve.tensor_tensor(dst, ps[rows, 4 + p, :].rearrange("p (j o) -> p j o", o=D),
                                          bias.broadcast_to([64, BATCHES // 2, D]), ALU.add).then_inc(sem(f"{st}_eo"), 1)

                dve.wait_ge(sem("dve_two"), 1)

                def sum_columns(t):
                    block_t = expert_io[:, t, :] if isinstance(t, int) else expert_io[:, bass.ds(t, 1), :].rearrange("p a n -> p (a n)")
                    dve.tensor_copy(block_t.rearrange("p (b o) -> p b o", o=OW)[:, :, D:OW], two[:].rearrange("p (b o) -> p b o", o=2)).then_inc(sem(f"{st}_sums"), 1)

                mix(0, 0)
                with dve.Fori(0, ST - 1) as t:
                    mix(t * 2 + 1, 1)
                    outputs(t * 2, t, 0)
                    mix(t * 2 + 2, 0)
                    outputs(t * 2 + 1, t, 1)
                    sum_columns(t)
                mix(EXPERTS - 1, 1)
                outputs(EXPERTS - 2, ST - 1, 0)
                outputs(EXPERTS - 1, ST - 1, 1)
                sum_columns(ST - 1)

                def stage(b, j, p):
                    if due((b - 1) * 2):
                        dve.wait_ge(*reached(f"{st}_combined", (b - 1) * 2))
                    src = comb[:, b, ST // 2:ST, :] if isinstance(b, int) else comb[:, bass.ds(b, 1), ST // 2:ST, :].rearrange("p a t n -> p (a t) n")
                    dve.tensor_copy(logits[:, p, 1, :].rearrange("p (t n) -> p t n", t=ST // 2), src).then_inc(sem(f"{st}_staged_b"), 1)

                def residual(b, j, p):
                    go = Steps(f"{st}_steps", b * 4)
                    for i in range(PER):
                        dve.wait_ge(*reached(f"{st}_combined", b * 2 + (i + 1)))
                        dve.reciprocal(zcol[:, p, i:i + 1], ps[:, 2 * p + i, D:D + 1]).then_inc(go.sem, go.step())
                    dve.wait_ge(go.sem, go.n)
                    for i in range(PER):
                        tile = b * PER + i
                        xt = x[:, tile, :] if isinstance(b, int) else x[:, bass.ds(tile, 1), :].rearrange("p a d -> p (a d)")
                        dve.scalar_tensor_tensor(xt, ps[:, 2 * p + i, 0:D], zcol[:, p, i:i + 1], xt, ALU.mult, ALU.add).then_inc(go.sem, go.step())
                    dve.wait_ge(go.sem, plain(dve, go.n))
                    after(st, b)

                stage(0, 0, 0)
                def finish(b, j, p):
                    if not (isinstance(b, int) and b == BATCHES - 1):
                        stage(b + 1, None, 1 - p)
                    residual(b, j, p)
                all_batches(dve, finish)

            def linear_attention_vector(st):
                def first(b, p):
                    B = 4 * p
                    dve.wait_ge(*reached(f"{st}_qkp", b + 1))
                    dve.tensor_scalar(la_min[:, p, :], ps[:, B, :], 0.0, None, ALU.min).then_inc(sem(f"{st}_min"), 1)
                    dve.wait_ge(*reached(f"{st}_exp", b + 1))
                    dve.scalar_tensor_tensor(la_qk[:, p, :], ps[:, B, :], 0.0, la_min[:, p, :], ALU.max, ALU.add)\
                        .then_inc(sem(f"{st}_qk"), 1)

                def second(b, p):
                    B = 4 * p
                    dve.wait_ge(*reached(f"{st}_kvp", b + 1))
                    dve.tensor_tensor(la_kv[:, p, 0, :], ps[:, B + 1, SEQ:SEQ + D], headmask[:], ALU.mult).then_inc(sem(f"{st}_kv"), 1)
                    dve.tensor_scalar(la_kv[:, p, 1, :], headmask[:], ps[:, B + 1, SEQ + D:SEQ + D + 1], None, ALU.mult)\
                        .then_inc(sem(f"{st}_kv"), 1)
                    go = Steps(f"{st}_steps", b * 5)
                    den = la_o[:, p, 1, :]
                    dve.wait_ge(*reached(f"{st}_op", b + 1))
                    dve.tensor_scalar(den, ps[:, B + 3, SEQ:2 * SEQ], ATT_EPS, None, ALU.add).then_inc(go.sem, go.step())
                    dve.wait_ge(go.sem, go.n)
                    dve.reciprocal(den, den).then_inc(go.sem, go.step())
                    dve.wait_ge(go.sem, go.n)
                    dve.tensor_tensor(la_o[:, p, 0, :], ps[:, B + 3, 0:SEQ], den, ALU.mult).then_inc(go.sem, go.step())
                    dve.wait_ge(*reached(f"{st}_yp", b + 1))
                    tmp = la_min[:, p, 0:SEQ].rearrange("p (i d) -> p i d", i=PER)
                    dve.tensor_tensor(tmp, ps[:, B + 2, SEQ:2 * SEQ].rearrange("p (i d) -> p i d", i=PER),
                                             bproj_bc[:].unsqueeze(1).broadcast_to([P, PER, D]), ALU.add).then_inc(go.sem, go.step())
                    dve.wait_ge(go.sem, go.n)
                    xb = x[:, batch(b), :]
                    dve.tensor_tensor(xb, xb, tmp, ALU.add).then_inc(go.sem, go.step())
                    dve.wait_ge(go.sem, plain(dve, go.n))
                    after(st, b)

                def step(b, j, p):
                    if not (isinstance(b, int) and b == BATCHES - 1):
                        first(b + 1, 1 - p)
                    second(b, p)

                dve.memset(la_v[:, :, :, D:D + 1], 1.0).then_inc(sem(f"{st}_vones"), 1)
                first(0, 0)
                all_batches(dve, step)

            def ffn_vector(st):
                def gated(c):
                    for o in range(HK):
                        r = o % 2
                        dve.wait_ge(*reached(f"{st}_p2", c * 4 + (o + 1)))
                        dve.wait_ge(*reached(f"{st}_silu", c * 4 + (o + 1)))
                        dst = act_a[:, o, c * CHUNK:c * CHUNK + CHUNK] if isinstance(c, int) else act_a[:, o, bass.ds(c * CHUNK, CHUNK)]
                        dve.scalar_tensor_tensor(dst, ps[:, 2 * r + 1, :], ffn_s[:, 1, o:o + 1], silu_out[:, r, :], ALU.mult, ALU.mult)\
                            .then_inc(sem(f"{st}_ha"), 1)

                with dve.Fori(0, CHUNKS) as c:
                    gated(c)
                for c in range(CHUNKS):
                    dve.wait_ge(*reached(f"{st}_yp", c + 1))
                    xc = x[:, 4 * c:4 * c + 4, :]
                    dve.tensor_tensor(xc, xc, ps[:, 2 + c % 2, :].rearrange("p (t d) -> p t d", d=D), ALU.add)\
                        .then_inc(sem(f"{st}_added"), 1)
                    dve.wait_ge(*reached(f"{st}_added", c + 1))
                    for b in (2 * c, 2 * c + 1):
                        after(st, b)

            def favor_vector(st):
                def first(b, p):
                    cc = fa_c[:, p]
                    go = Steps(f"{st}_steps", b * 11)
                    for a in range(4):
                        dve.wait_ge(*reached(f"{st}_xw", b * 4 + (a + 1)))
                        dve.tensor_reduce(cc[:, 1, a * HEADS:a * HEADS + HEADS], ps[:, 4 + a, :].rearrange("p (h m) -> p h m", m=FEAT),
                                                 AX_X, ALU.max).then_inc(go.sem, go.step())
                    dve.wait_ge(*reached(f"{st}_sq", b + 1))
                    dve.tensor_reduce(cc[:, 0, :], fa_sq[:, p, :].rearrange("p (h d) -> p h d", d=HD), AX_X, ALU.add).then_inc(go.sem, go.step())
                    dve.wait_ge(go.sem, go.n)
                    dve.tensor_tensor(cc[:, 2, :], cc[:, 0, :], cc[:, 1, :], ALU.add).then_inc(go.sem, go.step())
                    dve.wait_ge(go.sem, go.n)
                    for a in range(4):
                        dve.tensor_tensor(fa_phi[:, p, a, :].rearrange("p (h m) -> p h m", m=FEAT),
                                          ps[:, 4 + a, :].rearrange("p (h m) -> p h m", m=FEAT),
                                          cc[:, 2, a * HEADS:a * HEADS + HEADS].unsqueeze(2).broadcast_to([P, HEADS, FEAT]),
                                          ALU.subtract).then_inc(sem(f"{st}_sub"), 1)
                    dve.wait_ge(*reached(f"{st}_exp", b + 1))
                    phi = fa_phi[:, p].rearrange("p a f -> p (a f)")
                    dve.tensor_scalar(phi, phi, ATT_EPS, None, ALU.add).then_inc(sem(f"{st}_phi"), 1)
                    return go

                def second(b, p):
                    go = Steps(f"{st}_steps", b * 11 + 6)
                    dve.wait_ge(*reached(f"{st}_kvp", b + 1))
                    dve.tensor_tensor(fa_kv[:, p], ps[:, 3, SEQ:SEQ + FG * VA].rearrange("p (g v) -> p g v", g=FG),
                                      featmask[:].unsqueeze(1).broadcast_to([P, FG, VA]), ALU.mult).then_inc(sem(f"{st}_kv"), 1)
                    dve.wait_ge(*reached(f"{st}_np", b + 1))
                    num = ps[:, 2, :].rearrange("p (i r) -> p i r", i=PER)[:, :, 0:FG * VA].rearrange("p i (g v) -> p i g v", g=FG)
                    den = fa_den[:, p, :].rearrange("p (i g h) -> p i g h", i=PER, g=FG)
                    dve.tensor_scalar(den, num[:, :, :, VA - 4:VA], ATT_EPS * FEAT, None, ALU.add).then_inc(go.sem, go.step())
                    dve.wait_ge(go.sem, go.n)
                    dve.reciprocal(fa_den[:, p, :], fa_den[:, p, :]).then_inc(go.sem, go.step())
                    dve.wait_ge(go.sem, go.n)
                    for i in range(PER):
                        last = dve.tensor_tensor(fa_o[:, p, i, :].rearrange("p (g h d) -> p g h d", g=FG, h=4),
                                                 num[:, i, :, 0:VA - 4].rearrange("p g (h d) -> p g h d", h=4),
                                                 den[:, i].unsqueeze(3).broadcast_to([P, FG, 4, HD]), ALU.mult)
                        if i == 0:
                            last.then_inc(go.sem, go.step())
                    last.then_inc(sem(f"{st}_o"), 1)
                    dve.wait_ge(*reached(f"{st}_yp", b + 1))
                    dve.tensor_tensor(fa_y[:, p], ps[:, 1, 0:SEQ].rearrange("p (i d) -> p i d", i=PER),
                                             bo_bc[:].unsqueeze(1).broadcast_to([P, PER, D]), ALU.add).then_inc(go.sem, go.step())
                    dve.wait_ge(go.sem, go.n)
                    xb = x[:, batch(b), :]
                    dve.tensor_tensor(xb, xb, fa_y[:, p], ALU.add).then_inc(go.sem, go.step())
                    dve.wait_ge(go.sem, plain(dve, go.n))
                    after(st, b)

                def step(b, j, p):
                    second(b, p)
                    if not (isinstance(b, int) and b == BATCHES - 1):
                        first(b + 1, 1 - p)

                dve.memset(fa_vaug[:, :, :, :, VA - 4:VA], 1.0).then_inc(sem(f"{st}_vones"), 1)
                first(0, 0)
                all_batches(dve, step)

            dve.memset(two[:], 2.0).then_inc(sem("dve_two"), 1)
            dve.wait_ge(sem("ld_const"), 16)
            dve.tensor_copy(ident_r[:], ident[:]).then_inc(sem("dve_const"), 1)
            dve.wait_ge(sem("dve_const"), 1)
            for b in range(BATCHES):
                if b % 4 == 0:
                    dve.wait_ge(sem(f"ld_x{b // 4}"), 16)
                after("init", b)
            if "m0" in stages:
                dve.wait_ge(sem("ld_se"), 32)
                go = Steps("se_steps")
                for k in range(2):
                    dve.tensor_tensor(cols[:, 3 + k:4 + k], cols[:, k:k + 1], cols[:, 2:3], ALU.mult).then_inc(go.sem, go.step())
                for t in range(ST):
                    dve.bn_stats(se_stat[:, t, 0:6], logits[:, 1, 0, t * D:t * D + D]).then_inc(go.sem, go.step())
                dve.wait_ge(go.sem, go.n)
                for t in range(ST):
                    dve.bn_aggr(se_stat[:, t, 6:8], se_stat[:, t, 0:6]).then_inc(sem("se_moments"), 1)
                flat = logits[:, 0, 0, :]
                for k in range(2):
                    dve.wait_ge(sem("se_turned"), 4 * k + 4)
                    dve.tensor_scalar(flat[:, k * 512:k * 512 + 512], ps[:, k, :], cols[:, 3:4], cols[:, 4:5], ALU.mult, ALU.add).then_inc(go.sem, go.step())
                dve.wait_ge(go.sem, go.n)
                pairs = flat.rearrange("p (t h s) -> p t h s", t=ST, h=2)
                go2 = Steps("se_ready")
                dve.tensor_copy(se_hi[:, 0, :], flat).then_inc(go2.sem, go2.step())
                swapped = [t[:, 1, :].rearrange("p (t h s) -> p t h s", t=ST, h=2) for t in (se_hi, se_lo)]
                for h in range(2):
                    dve.tensor_copy(swapped[0][:, :, 1 - h, :], pairs[:, :, h, :]).then_inc(go2.sem, go2.step())
                dve.wait_ge(go2.sem, go2.n)
                dve.tensor_tensor(se_lo[:, 0, :], flat, as32(se_hi[:, 0, :]), ALU.subtract).then_inc(go2.sem, go2.step())
                for h in range(2):
                    dve.tensor_tensor(swapped[1][:, :, 1 - h, :], pairs[:, :, h, :],
                                              as32(swapped[0][:, :, 1 - h, :]), ALU.subtract).then_inc(go2.sem, go2.step())
                dve.memset(junk[:, 0, 0:1], 0.0).then_inc(sem("se_ready"), 1)
                go2.n += 1
                dve.wait_ge(go2.sem, go2.n)
            for st in stages:
                if before[st] != "init":
                    dve.wait_ge(sem(f"{before[st]}_x"), BATCHES)
                if before[st] == "init":
                    dve.wait_ge(sem("ld_w"), 16 * 12)
                if st == "f0":
                    dve.tensor_scalar(w3_s[:, 1:2], w3_s[:, 0:1], 0.5, None, ALU.mult).then_inc(sem("w3_half"), 1)
                {"m": moe_vector, "l": linear_attention_vector, "f": ffn_vector}[st[0]](st) if st != "fa" else favor_vector(st)


def arrange(a):
    f = np.float32
    t = lambda m: np.ascontiguousarray(np.transpose(m))
    rows = lambda m, k: np.ascontiguousarray(m.reshape(k, P, -1).transpose(1, 0, 2).reshape(P, -1))
    got = {
        "x": np.ascontiguousarray(a["L0_attn_x"].reshape(BATCHES * SEQ, D)),
        "ident": np.eye(P, dtype=f),
        "slot_embeds": np.ascontiguousarray(a["L0_ffn_slot_embeds"].reshape(NSLOT, D)),
        "cols": np.ascontiguousarray(np.stack([a["L0_ffn_slot_g"], a["L0_ffn_slot_b"], np.broadcast_to(a["L0_ffn_scale"], (D,))], 1)),
        "affine": np.stack([a["L0_ffn_norm_g"], a["L0_ffn_norm_b"]]),
        "bgu": np.ascontiguousarray(np.stack([a["L0_ffn_bg"], a["L0_ffn_bu"]]).reshape(2, EXPERTS, 2, P).transpose(3, 0, 1, 2).reshape(P, -1)),
        "bd": np.ascontiguousarray(a["L0_ffn_bd"]),
        "wqkv": t(a["L0_attn_Wqkv"]),
        "wproj": t(a["L0_attn_Wproj"]),
        "headmask": np.kron(np.eye(HEADS, dtype=f), np.ones((HD, HD), f)),
        "bproj": np.ascontiguousarray(a["L0_attn_bproj"]),
        "bo": np.ascontiguousarray(a["L1_attn_bo"]),
        "fw": np.concatenate([t(a[f"L1_attn_W{k}"]) for k in "qkvo"], 1),
        "ffn_s": np.concatenate([a[f"L1_ffn_{k}_s"].reshape(HK, P).T for k in ("w1", "w2", "h1", "h2")], 1),
        "w3_s": np.ascontiguousarray(a["L1_ffn_w3_s"].reshape(D, 1)),
        "wx": np.concatenate([a["L0_ffn_Wg"], a["L0_ffn_Wu"],
                              a["L0_ffn_Wd"].reshape(EXPERTS, 2, P, D).transpose(0, 2, 1, 3).reshape(EXPERTS, P, 2 * D)], 2),
        "ffw": np.concatenate([t(a["L1_ffn_w1_w"]), t(a["L1_ffn_w2_w"]), rows(t(a["L1_ffn_h1_w"]), HK),
                               rows(t(a["L1_ffn_h2_w"]), HK), rows(t(a["L1_ffn_w3_w"]), HK)], 1),
    }
    bd = np.zeros((HEADS, HD, HEADS, FEAT), f)
    for h in range(HEADS):
        bd[h, :, h, :] = a["L1_attn_proj"][h].T
    got["proj_bd"] = bd.reshape(P, HF)
    mask = np.zeros((P, VA), f)
    for h in range(4):
        mask[h * FEAT:h * FEAT + FEAT, h * HD:h * HD + HD] = 1.0
        mask[h * FEAT:h * FEAT + FEAT, 4 * HD + h] = 1.0
    got["featmask"] = mask
    return {k: np.ascontiguousarray(v) for k, v in got.items()}


def kernel(**inputs):
    import concourse.bacc as bacc
    from concourse.bass_utils import run_bass_kernel_spmd

    nc = bacc.Bacc("TRN2", target_bir_lowering=False, num_devices=1)
    arrays = {f"in_{k}": v for k, v in arrange({k: np.asarray(v) for k, v in inputs.items()}).items()}
    ins = {k[3:]: nc.dram_tensor(k, v.shape, F32, kind="ExternalInput").ap() for k, v in arrays.items()}
    out = nc.dram_tensor("out_0", (BATCHES * SEQ, D), F32, kind="ExternalOutput").ap()
    build(nc, ins, out)
    r = run_bass_kernel_spmd(nc, [arrays], core_ids=[0])
    return r.results[0]["out_0"].reshape(BATCHES, SEQ, D)
```

```python
from contextlib import ExitStack

import concourse.bass as bass
import concourse.mybir as mybir
import numpy as np

ALU = mybir.AluOpType
ACT = mybir.ActivationFunctionType
F32 = mybir.dt.float32
F32R = mybir.dt.float32r
AX_X = mybir.AxisListType.X

P = 128
BATCHES, SEQ, D = 8, 256, 128
TILES = BATCHES * SEQ // P
PER = SEQ // P
EXPERTS, SLOTS, FE = 16, 64, 256
NSLOT = EXPERTS * SLOTS
ST = NSLOT // P
OW = D + 2
HEADS, HD = 16, 8
FEAT = 32
HF = HEADS * FEAT
FG = HF // P
VA = P // FEAT * HD + P // FEAT
NORMS = SEQ + FG * VA
HID = 512
HK = HID // P
CHUNK = 512
CHUNKS = BATCHES * SEQ // CHUNK
LN_EPS = 1e-5
ATT_EPS = 1e-6
QK_SCALE = HD ** -0.5


LN_STEPS = {"m": 11, "a": 4}
MOE_TOTALS = dict(
    pool=BATCHES * LN_STEPS["m"], turned=BATCHES, kept=BATCHES, zthi=BATCHES, ztlo=BATCHES, rows=BATCHES * PER,
    copied=BATCHES * PER, maxn=BATCHES * PER, columns=BATCHES * 4, maxs=BATCHES * 4,
    zs=BATCHES * 4, lnz=BATCHES, shift=BATCHES * 3, spread=BATCHES, sub=BATCHES * PER,
    disp=BATCHES * PER, shifted=BATCHES * 4, comb=BATCHES * 4, slots=BATCHES, slots_a=BATCHES, slots_b=BATCHES,
    wgu0=EXPERTS // 2 * 16, wgu1=EXPERTS // 2 * 16, wd0=EXPERTS // 2 * 16, wd1=EXPERTS // 2 * 16, gate=EXPERTS * 2, up=EXPERTS * 2, gelu=EXPERTS * 2, h=EXPERTS * 2,
    down=EXPERTS, eo=EXPERTS * 2, sums=ST, staged_a=BATCHES, staged_b=BATCHES, combined=BATCHES * PER,
    steps=BATCHES * 4, mom=BATCHES * 4)
FFN_TOTALS = dict(
    pool=BATCHES * LN_STEPS["a"], turned=BATCHES, zthi=CHUNKS, ztlo=CHUNKS, p1=CHUNKS * HK, p2=CHUNKS * HK,
    silu=CHUNKS * HK, mixed=CHUNKS * HK, mixhi=CHUNKS * HK, prod=2 * CHUNKS * HK, gelu=2 * CHUNKS * HK,
    gelhi=2 * CHUNKS * HK, lo=3 * CHUNKS * HK, p3=CHUNKS, yt=CHUNKS, yp=CHUNKS, added=CHUNKS, mom=BATCHES * 4)
TOTALS = {"m0": MOE_TOTALS, "m1": MOE_TOTALS, "f0": FFN_TOTALS, "f1": FFN_TOTALS}


def as32(ap):
    return ap.bitcast(F32)


def build(nc, ins, out, stages=("m0", "la", "m1", "f0", "fa", "f1")):
    ffns = [st for st in stages if st in ("f0", "f1")]
    before = dict(zip(stages, ("init",) + tuple(stages[:-1])))
    with ExitStack() as ctx:
        def sb(name, shape, dtype=F32, scope=ctx):
            return scope.enter_context(nc.sbuf_tensor(name, shape, dtype))

        sems = {}

        def sem(name):
            stage, _, what = name.partition("_")
            if stage in TOTALS and what != "x":
                name = f"{stage[0]}_{what}"
            if name not in sems:
                sems[name] = ctx.enter_context(nc.semaphore(name))
            return sems[name]

        def earlier(name):
            stage, _, what = name.partition("_")
            second = stage in ("m1", "f1") and stage[0] + "0" in stages and what != "x"
            return TOTALS[stage][what] if second else 0

        def plain(eng, value):
            if isinstance(value, int):
                return value
            count = eng.to_reg(value)
            eng.wait_ge(sem("pool_const" if eng is nc.gpsimd else "dve_const"), 1)
            return count

        def reached(name, value, eng=None):
            value = value + earlier(name)
            return sem(name), value if eng is None else plain(eng, value)

        def due(value):
            return not isinstance(value, int) or value > 0

        class Steps:
            def __init__(self, name, base=0):
                self.sem, self.n = sem(name), base + earlier(name)

            def step(self):
                self.n = self.n + 1
                return 1

        x = sb("x", [P, TILES, D])
        moments = sb("moments", [P, TILES, 2])
        ident = sb("ident", [P, P])
        ident_r = sb("ident_r", [P, P], F32R)
        half_power = sb("half_power", [P, 16])
        eps2 = sb("eps2", [P, PER])
        two = sb("two", [P, 2 * BATCHES])
        fresh = sb("fresh", [P, PER, 2])
        bn6 = sb("bn6", [P, 4, 6])
        rstd = sb("rstd", [P, 2, 8])
        z_in = sb("z_in", [P, 2, PER, D])
        bproj_bc = sb("bproj_bc", [P, D])
        bo_bc = sb("bo_bc", [P, D])
        headmask = sb("headmask", [P, D])
        featmask = sb("featmask", [P, VA])
        wqkv = sb("wqkv", [P, 3 * D])
        wproj = sb("wproj", [P, D])
        fw = sb("fw", [P, 4, D])
        proj_bd = sb("proj_bd", [P, HF])
        ffn_s = sb("ffn_s", [P, 4, HK])
        w3_s = sb("w3_s", [P, 2])

        moe = ExitStack()
        se_hi = sb("se_hi", [P, 2, NSLOT], F32R, moe)
        se_lo = sb("se_lo", [P, 2, NSLOT], F32R, moe)
        zt_hi = sb("zt_hi", [P, 2, SEQ], F32R, moe)
        zt_lo = sb("zt_lo", [P, 2, SEQ], F32R, moe)
        junk = sb("junk", [P, 4, SEQ], F32, moe)
        moe2 = ExitStack()
        expert_io = sb("expert_io", [P, ST + 1, BATCHES * OW], F32, moe2)
        bd_bc = sb("bd_bc", [P, EXPERTS, D], F32, moe2)
        wx = sb("wx", [P, 2, 3 * FE], F32, moe2)
        bgu = sb("bgu", [P, 2, EXPERTS, 2], F32, moe2)
        logits = sb("logits", [P, 2, PER, NSLOT], F32, moe2)
        negmax_n = sb("negmax_n", [P, 2, PER], F32R, moe2)
        negmax_s = sb("negmax_s", [P, 2, ST], F32, moe2)
        zsum_s = sb("zsum_s", [P, 2, ST], F32, moe2)
        lnz_s = sb("lnz_s", [P, 2, ST], F32, moe2)
        shift_s = sb("shift_s", [P, 2, ST], F32, moe2)
        shift_hi = sb("shift_hi", [P, 2, ST], F32R, moe2)
        shift_lo = sb("shift_lo", [P, 2, ST], F32R, moe2)
        z_slots = sb("z_slots", [P, 2, PER, D], F32, moe2)
        gate = sb("gate", [P, 2, CHUNK], F32, moe2)
        hmid = sb("hmid", [P, 2, 2, CHUNK], F32, moe2)
        affine = sb("affine", [P, 2, D], F32, moe2)
        cols = sb("cols", [P, 6], F32, moe2)
        zcol = sb("zcol", [P, 2, PER], F32, moe2)
        se_stat = sb("se_stat", [P, ST, 8], F32, moe2)
        se_r = sb("se_r", [P, 2, ST], F32, moe2)
        moe3 = ExitStack()
        comb = sb("comb", [P, BATCHES, ST, SEQ], F32, moe3)
        moe3.close()
        la = ExitStack()
        la_zt = sb("la_zt", [P, 2, SEQ], F32, la)
        la_min = sb("la_min", [P, 2, 2 * SEQ], F32, la)
        la_qk = sb("la_qk", [P, 2, 2 * SEQ], F32, la)
        la_v = sb("la_v", [P, 2, PER, D + 1], F32, la)
        la_kv = sb("la_kv", [P, 2, 2, D], F32, la)
        la_o = sb("la_o", [P, 2, 2, SEQ], F32, la)
        la.close()
        moe2.close()
        moe.close()

        l1 = ExitStack()
        ffw = sb("ffw", [P, 2 * HID + 2 * HK * HID + HK * D], F32, l1)
        pad = sb("pad", [P, 4 * NSLOT + 8 * SEQ - ffw.shape[1]], F32, l1)
        ffw_hi = sb("ffw_hi", ffw.shape, F32R, l1)
        ffw_lo = sb("ffw_lo", ffw.shape, F32R, l1)
        W12 = 2 * HID
        H1 = W12 + HK * HID
        H2 = H1 + HK * HID
        ffn = ExitStack()
        fz_hi = sb("fz_hi", [P, 2, CHUNK], F32R, ffn)
        fz_lo = sb("fz_lo", [P, 2, CHUNK], F32R, ffn)
        even_hi = sb("even_hi", [P, 2, HK, CHUNK], F32R, ffn)
        even_lo = sb("even_lo", [P, 2, HK, CHUNK], F32R, ffn)
        odd_hi = sb("odd_hi", [P, 2, HK, CHUNK], F32R, ffn)
        odd_lo = sb("odd_lo", [P, 2, HK, CHUNK], F32R, ffn)
        whole = sb("whole", [P, HK, CHUNK], F32, ffn)
        silu_out = sb("silu_out", [P, 2, CHUNK], F32, ffn)
        y_t = sb("y_t", [P, 2, CHUNK], F32, ffn)
        ffn.close()
        fa = ExitStack()
        fa_zt = sb("fa_zt", [P, 2, SEQ], F32, fa)
        fa_qkt = sb("fa_qkt", [P, 2, 2, SEQ], F32, fa)
        fa_sq = sb("fa_sq", [P, 2, 2 * SEQ], F32, fa)
        fa_c = sb("fa_c", [P, 2, 2, 4 * HEADS], F32, fa)
        fa_phi = sb("fa_phi", [P, 2, 4, HF], F32, fa)
        fa_phit = sb("fa_phit", [P, 2, PER, FG, P], F32, fa)
        fa_vaug = sb("fa_vaug", [P, 2, PER, FG, VA], F32, fa)
        fa_kv = sb("fa_kv", [P, 2, FG, VA], F32, fa)
        fa_den = sb("fa_den", [P, 2, PER * HEADS], F32, fa)
        fa_o = sb("fa_o", [P, 2, PER, D], F32, fa)
        fa_ot = sb("fa_ot", [P, 2, SEQ], F32, fa)
        fa_y = sb("fa_y", [P, 2, PER, D], F32, fa)
        fa.close()
        l1.close()

        ps = ctx.enter_context(nc.psum_tensor("ps", [P, 8, 512], F32))
        block = ctx.enter_context(nc.Block())

        def batch(b):
            return bass.ds(b * PER, PER) if not isinstance(b, int) else slice(b * PER, b * PER + PER)

        def looped(eng, step, first, last):
            pairs = (last - first) // 2
            with eng.Fori(0, pairs) as it:
                step(it * 2 + first, it + (first // 2), 1)
                step(it * 2 + (first + 1), it + (first + 1) // 2, 0)

        def all_batches(eng, step):
            step(0, 0, 0)
            looped(eng, step, 1, BATCHES - 1)
            step(BATCHES - 1, (BATCHES - 1) // 2, 1)

        def store_slots(copy, j, p, k):
            for h in range(2):
                col = (h ^ p) * 512 + h * SLOTS
                dst = expert_io[:, 1 + 4 * k:5 + 4 * k, :]
                dst = dst[:, :, j * P + col:j * P + col + SLOTS] if isinstance(j, int) else dst[:, :, bass.ds(j * P + col, SLOTS)]
                last = copy(dst, ps[:, 6 + k, :].rearrange("p (t h s) -> p t h s", t=4, h=2)[:, :, h, :])
            return last


        @block.sync
        def _(sp):
            sp.dma_start(ident[:], ins["ident"]).then_inc(sem("ld_const"), 16)
            for h in range(2):
                sp.dma_start(x[:, h * 8:h * 8 + 8, :],
                             ins["x"].rearrange("(t p) d -> p t d", p=P)[:, h * 8:h * 8 + 8, :]).then_inc(sem(f"ld_x{h}"), 16)
            sp.dma_start(logits[:, 1, 0, :].rearrange("p (t d) -> p t d", t=ST),
                         ins["slot_embeds"].rearrange("(t p) d -> p t d", p=P)).then_inc(sem("ld_se"), 16)
            sp.dma_start(cols[:, 0:3], ins["cols"]).then_inc(sem("ld_se"), 16)
            sp.dma_start(affine[:], ins["affine"].partition_broadcast(P)).then_inc(sem("ld_affine"), 16)
            sp.dma_start(bgu[:].rearrange("p a b c -> p (a b c)"), ins["bgu"]).then_inc(sem("ld_w"), 16)
            sp.dma_start(bd_bc[:], ins["bd"].partition_broadcast(P)).then_inc(sem("ld_w"), 16)
            for dst, name in ((wqkv, "wqkv"), (wproj, "wproj"), (headmask, "headmask"), (featmask, "featmask"),
                              (proj_bd, "proj_bd"), (w3_s[:, 0:1], "w3_s")):
                sp.dma_start(dst[:] if dst is not w3_s else dst, ins[name]).then_inc(sem("ld_w"), 16)
            sp.dma_start(bproj_bc[:], ins["bproj"].partition_broadcast(P)).then_inc(sem("ld_w"), 16)
            sp.dma_start(bo_bc[:], ins["bo"].partition_broadcast(P)).then_inc(sem("ld_w"), 16)
            sp.dma_start(fw[:].rearrange("p a d -> p (a d)"), ins["fw"]).then_inc(sem("ld_w"), 16)
            sp.dma_start(ffn_s[:].rearrange("p a k -> p (a k)"), ins["ffn_s"]).then_inc(sem("ld_w"), 16)

            for st in stages:
                if st[0] == "m":
                    for p in range(2):
                        if st == "m1":
                            sp.wait_ge(*reached("m0_down", EXPERTS))
                        sp.dma_start(wx[:, p, 0:2 * FE], ins["wx"][p, :, 0:2 * FE]).then_inc(sem(f"{st}_wgu{p}"), 16)
                        sp.dma_start(wx[:, p, 2 * FE:], ins["wx"][p, :, 2 * FE:]).then_inc(sem(f"{st}_wd{p}"), 16)
                    with sp.Fori(0, EXPERTS // 2 - 1) as t:
                        for p in range(2):
                            sp.wait_ge(*reached(f"{st}_up", t * 4 + (2 * p + 2)))
                            sp.dma_start(wx[:, p, 0:2 * FE], ins["wx"][t * 2 + (p + 2), :, 0:2 * FE]).then_inc(sem(f"{st}_wgu{p}"), 16)
                            sp.wait_ge(*reached(f"{st}_down", t * 2 + (p + 1)))
                            sp.dma_start(wx[:, p, 2 * FE:], ins["wx"][t * 2 + (p + 2), :, 2 * FE:]).then_inc(sem(f"{st}_wd{p}"), 16)
                if st == "f0":
                    if "m1" in stages:
                        sp.wait_ge(*reached("m1_slots", BATCHES))
                    sp.dma_start(ffw[:], ins["ffw"]).then_inc(sem("ld_ffw"), 16)
            last = stages[-1]
            view = out.rearrange("(t p) d -> p t d", p=P)
            for c in range(CHUNKS):
                sp.wait_ge(sem(f"{last}_x"), 2 * c + 2)
                sp.dma_start(view[:, 4 * c:4 * c + 4, :], x[:, 4 * c:4 * c + 4, :]).then_inc(sem("stored"), 16)
            sp.wait_ge(sem("stored"), 16 * CHUNKS)

        @block.gpsimd
        def _(pool):
            pool.memset(half_power[:], -0.5).then_inc(sem("pool_const"), 1)
            pool.memset(eps2[:], LN_EPS).then_inc(sem("pool_const"), 1)
            pool.wait_ge(sem("pool_const"), 2)

            def slot_norm():
                pool.wait_ge(sem("se_moments"), ST)
                go = Steps("se_pool")
                pool.tensor_scalar(se_r[:, 0, :], se_stat[:, :, 7], LN_EPS, None, ALU.add).then_inc(go.sem, go.step())
                pool.wait_ge(go.sem, plain(pool, go.n))
                pool.tensor_tensor(se_r[:, 1, :], se_r[:, 0, :], half_power[:, 0:ST], ALU.pow).then_inc(go.sem, go.step())
                pool.wait_ge(go.sem, plain(pool, go.n))
                for t in range(ST):
                    row = logits[:, 1, 0, t * D:t * D + D]
                    pool.tensor_scalar(row, row, se_stat[:, t, 6:7], se_r[:, 1, t:t + 1],
                                       ALU.subtract, ALU.mult).then_inc(sem("se_norm"), 1)

            def norm(st, b, p):
                moe_ln = st[0] == "m"
                key = "m" if moe_ln else "a"
                pool.wait_ge(*reached(f"{before[st]}_x", b + 1, pool))
                go = Steps(f"{st}_pool", b * LN_STEPS[key])
                var = moments[:, batch(b), 1]
                r = rstd[:, p, :]
                pool.tensor_tensor(r[:, 0:2], var, eps2[:], ALU.add).then_inc(go.sem, go.step())
                pool.wait_ge(go.sem, plain(pool, go.n))
                pool.tensor_tensor(r[:, 2:4], r[:, 0:2], half_power[:, 0:2], ALU.pow).then_inc(go.sem, go.step())
                pool.wait_ge(go.sem, plain(pool, go.n))
                scale = r[:, 2:4]
                if moe_ln:
                    pool.tensor_tensor(r[:, 4:6], scale, scale, ALU.mult).then_inc(go.sem, go.step())
                    pool.wait_ge(go.sem, plain(pool, go.n))
                    pool.tensor_tensor(r[:, 0:2], r[:, 4:6], var, ALU.mult).then_inc(go.sem, go.step())
                    pool.wait_ge(go.sem, plain(pool, go.n))
                    pool.tensor_scalar(r[:, 4:6], r[:, 0:2], LN_EPS, None, ALU.add).then_inc(go.sem, go.step())
                    pool.wait_ge(go.sem, plain(pool, go.n))
                    pool.tensor_tensor(r[:, 0:2], r[:, 4:6], half_power[:, 0:2], ALU.pow).then_inc(go.sem, go.step())
                    pool.wait_ge(go.sem, plain(pool, go.n))
                    pool.tensor_tensor(r[:, 6:8], r[:, 0:2], scale, ALU.mult).then_inc(go.sem, go.step())
                    pool.wait_ge(go.sem, plain(pool, go.n))
                    scale = r[:, 6:8]
                if due(b - 1):
                    pool.wait_ge(*reached(f"{st}_turned", b - 1, pool))
                if isinstance(b, int) and b == 0 and before[st] != "init":
                    pool.wait_ge(*reached(f"{before[st]}_turned", BATCHES, pool))
                pool.tensor_tensor(z_in[:, p], x[:, batch(b), :],
                                          moments[:, batch(b), 0:1].broadcast_to([P, PER, D]), ALU.subtract).then_inc(go.sem, go.step())
                pool.wait_ge(go.sem, plain(pool, go.n))
                pool.tensor_tensor(z_in[:, p], z_in[:, p], scale.unsqueeze(2).broadcast_to([P, PER, D]), ALU.mult).then_inc(go.sem, go.step())
                if moe_ln:
                    pool.wait_ge(go.sem, plain(pool, go.n))
                    pool.tensor_tensor(z_in[:, p], z_in[:, p],
                                              affine[:, 0:1, :].broadcast_to([P, PER, D]), ALU.mult).then_inc(go.sem, go.step())
                    pool.wait_ge(go.sem, plain(pool, go.n))
                    pool.tensor_tensor(z_in[:, p], z_in[:, p],
                                              affine[:, 1:2, :].broadcast_to([P, PER, D]), ALU.add).then_inc(go.sem, go.step())

            def moe_pool(st):
                def keep(b, p):
                    if due(b - 1):
                        pool.wait_ge(*reached(f"{st}_slots", b - 1, pool))
                    pool.wait_ge(*reached(f"{st}_pool", b * LN_STEPS["m"] + LN_STEPS["m"], pool))
                    pool.tensor_copy(z_slots[:, p], z_in[:, p]).then_inc(sem(f"{st}_kept"), 1)

                def slot_shifts(b, p):
                    if due(b - 1):
                        pool.wait_ge(*reached(f"{st}_spread", b - 1, pool))
                    pool.wait_ge(*reached(f"{st}_lnz", b + 1, pool))
                    go = Steps(f"{st}_shift", b * 3)
                    pool.tensor_tensor(shift_s[:, p], negmax_s[:, p, :], lnz_s[:, p, :], ALU.subtract).then_inc(go.sem, go.step())
                    pool.wait_ge(go.sem, plain(pool, go.n))
                    pool.tensor_copy(shift_hi[:, p], shift_s[:, p]).then_inc(go.sem, go.step())
                    pool.wait_ge(go.sem, plain(pool, go.n))
                    pool.tensor_tensor(shift_lo[:, p], shift_s[:, p], as32(shift_hi[:, p]), ALU.subtract).then_inc(go.sem, go.step())

                norm(st, 0, 0)
                keep(0, 0)
                norm(st, 1, 1)
                keep(1, 1)
                slot_shifts(0, 0)

                def step(b, j, p, ahead=True):
                    if ahead:
                        norm(st, b + 2, p)
                    if ahead or isinstance(b, int) and b < BATCHES - 1:
                        slot_shifts(b + 1, 1 - p)
                    if ahead:
                        keep(b + 2, p)

                step(0, 0, 0)
                looped(pool, step, 1, BATCHES - 3)
                step(BATCHES - 3, 2, 1)
                step(BATCHES - 2, 3, 0, False)

            for st in stages:
                if st == "m0":
                    slot_norm()
                if st[0] == "m":
                    pool.wait_ge(sem("ld_affine"), 16)
                    moe_pool(st)
                elif st in ("f0", "f1"):
                    for b in range(BATCHES):
                        if b == 4 and st == ffns[0]:
                            if before[st] != "init":
                                pool.wait_ge(sem(f"{before[st]}_x"), BATCHES)
                            pool.wait_ge(sem("ld_ffw"), 16)
                            for n, part in enumerate((slice(H1, H2), slice(H2, ffw.shape[1]))):
                                pool.tensor_scalar(ffw_hi[:, part], ffw[:, part], 1.0, None, ALU.mult).then_inc(sem("deep_w"), 1)
                                pool.wait_ge(sem("deep_w"), 2 * n + 1)
                                pool.tensor_tensor(ffw_lo[:, part], ffw[:, part], as32(ffw_hi[:, part]), ALU.subtract).then_inc(sem("deep_w"), 1)
                        norm(st, b, b % 2)
                else:
                    all_batches(pool, lambda b, j, p: norm(st, b, p))

        @block.tensor
        def _(pe):
            def turn(dst, src):
                return pe.transpose(dst, src, ident[:])

            def three(dst, a_hi, a_lo, b_hi, b_lo, start, stop):
                pe.matmul(dst, a_hi, b_lo, start=start, stop=False, skip_group_check=True)
                pe.matmul(dst, a_lo, b_hi, start=False, stop=False, skip_group_check=True)
                return pe.matmul(dst, a_hi, b_hi, start=False, stop=stop, skip_group_check=True)

            def turn_batch(st, b, p, bank, at=0):
                k = LN_STEPS["m" if st[0] == "m" else "a"]
                pe.wait_ge(*reached(f"{st}_pool", b * k + k))
                for i in range(PER):
                    mm = turn(ps[:, bank, at + i * P:at + i * P + P], z_in[:, p, i, :])
                mm.then_inc(sem(f"{st}_turned"), 1)

            def moe_tensor(st):
                ROW0, ROW1 = 4, 6

                def tokens(b, p):
                    if due((b - 1) * 2):
                        pe.wait_ge(*reached(f"{st}_sub", (b - 1) * 2))
                    turn_batch(st, b, p, ROW0)

                def rows(b, p):
                    pe.wait_ge(*reached(f"{st}_zthi", b + 1))
                    pe.wait_ge(*reached(f"{st}_ztlo", b + 1))
                    for i in range(PER):
                        if i == 1:
                            if due(b - 1):
                                pe.wait_ge(*reached(f"{st}_slots_a", b - 1))
                            if due(b - 1):
                                pe.wait_ge(*reached(f"{st}_slots_b", b - 1))
                        for h in range(2):
                            cut = slice(h * 512, h * 512 + 512)
                            mm = three(ps[:, (ROW0, ROW1)[i] + h, :], zt_hi[:, p, i * P:i * P + P], zt_lo[:, p, i * P:i * P + P],
                                       se_hi[:, p, cut], se_lo[:, p, cut], True, True)
                        mm.then_inc(sem(f"{st}_rows"), 1)

                def columns(b, p, ks):
                    for k in ks:
                        if due((b - 1) * 4 + (k + 1)):
                            pe.wait_ge(*reached(f"{st}_comb", (b - 1) * 4 + (k + 1)))
                        for h in range(2):
                            t = 2 * k + h
                            cut = slice(t * P, t * P + P)
                            mm = three(ps[:, k, h * SEQ:h * SEQ + SEQ], se_hi[:, p, cut], se_lo[:, p, cut],
                                       zt_hi[:, p, :], zt_lo[:, p, :], h == 0, False)
                        mm.then_inc(sem(f"{st}_columns"), 1)

                def spread(b, p):
                    pe.wait_ge(*reached(f"{st}_shift", b * 3 + 3))
                    for t in range(ST):
                        dst = ps[:, ROW0 + t // 4, t % 4 * P:t % 4 * P + P]
                        pe.matmul(dst, shift_lo[:, p, t:t + 1].broadcast_to([P, P]), ident_r[:], start=True, stop=False)
                        mm = pe.matmul(dst, shift_hi[:, p, t:t + 1].broadcast_to([P, P]), ident_r[:], start=False, stop=True)
                    mm.then_inc(sem(f"{st}_spread"), 1)

                def shift(b, p):
                    pe.wait_ge(*reached(f"{st}_maxn", b * 2 + 2))
                    for k in range(4):
                        pe.wait_ge(*reached(f"{st}_zs", b * 4 + (k + 1)))
                        for i in range(PER):
                            mm = pe.matmul(ps[:, k, :].rearrange("p (h i n) -> p i h n", h=2, i=PER)[:, i],
                                           negmax_n[:, p, i:i + 1].broadcast_to([P, P]),
                                           ident_r[:].unsqueeze(1).broadcast_to([P, 2, P]),
                                           start=False, stop=i == PER - 1, skip_group_check=True)
                        mm.then_inc(sem(f"{st}_shifted"), 1)

                def slots(b, p):
                    pe.wait_ge(*reached(f"{st}_disp", b * 2 + 2))
                    pe.wait_ge(*reached(f"{st}_kept", b + 1))
                    for h in range(2):
                        for i in range(PER):
                            mm = pe.matmul(ps[:, ROW1 + h, :], z_slots[:, p, i, :], logits[:, p, i, h * 512:h * 512 + 512],
                                           start=i == 0, stop=i == PER - 1)
                    mm.then_inc(sem(f"{st}_slots"), 1)

                tokens(0, 0)
                rows(0, 0)
                columns(0, 0, range(4))
                pe.wait_ge(*reached(f"{st}_copied", 1))
                shift(0, 0)
                tokens(1, 1)

                def step(b, j, p, ahead=True, last=False):
                    if not last:
                        rows(b + 1, 1 - p)
                        columns(b + 1, 1 - p, (0, 1))
                        pe.wait_ge(*reached(f"{st}_copied", b * 2 + 3))
                    spread(b, p)
                    if not last:
                        columns(b + 1, 1 - p, (2, 3))
                        pe.wait_ge(*reached(f"{st}_copied", b * 2 + 4))
                    slots(b, p)
                    if ahead:
                        tokens(b + 2, p)
                    if not last:
                        shift(b + 1, 1 - p)

                step(0, 0, 0)
                looped(pe, step, 1, BATCHES - 3)
                step(BATCHES - 3, 2, 1)
                step(BATCHES - 2, 3, 0, False)
                step(BATCHES - 1, 3, 1, False, True)

                def up(e, t, p):
                    pe.wait_ge(*reached(f"{st}_wgu{p}", (t + 1) * 16))
                    for f in range(2):
                        for which in range(2):
                            if due((e - 1) * 2 + (f + 1)):
                                pe.wait_ge(*reached(f"{st}_gelu" if which == 0 else f"{st}_h", (e - 1) * 2 + (f + 1)))
                            w0 = which * FE + f * P
                            mm = pe.matmul(ps[:, 2 * which + f, :], wx[:, p, w0:w0 + P],
                                           expert_io[:, t + 1, p * 512:p * 512 + 512] if isinstance(t, int) else
                                           expert_io[:, bass.ds(t + 1, 1), p * 512:p * 512 + 512].rearrange("p a n -> p (a n)"),
                                           start=True, stop=True)
                            mm.then_inc(sem(f"{st}_gate" if which == 0 else f"{st}_up"), 1)

                def down(e, t, p):
                    pe.wait_ge(*reached(f"{st}_wd{p}", (t + 1) * 16))
                    pe.wait_ge(*reached(f"{st}_h", e * 2 + 2))
                    if due((e - 1) * 2):
                        pe.wait_ge(*reached(f"{st}_eo", (e - 1) * 2))
                    for jj in range(BATCHES // 2):
                        for f in range(2):
                            mm = pe.matmul(ps[:, 4 + p, jj * P:jj * P + P], hmid[:, p, f, jj * P:jj * P + P],
                                           wx[:, p, 2 * FE + f * D:2 * FE + f * D + D], start=f == 0, stop=f == 1)
                    mm.then_inc(sem(f"{st}_down"), 1)

                pe.wait_ge(*reached(f"{st}_comb", BATCHES * 4))
                pe.wait_ge(*reached(f"{st}_slots_a", BATCHES))
                pe.wait_ge(*reached(f"{st}_slots_b", BATCHES))
                def pair(t):
                    up(t * 2 + 1, t, 1)
                    down(t * 2, t, 0)
                    up(t * 2 + 2, t + 1, 0)
                    down(t * 2 + 1, t, 1)

                up(0, 0, 0)
                pair(0)
                with pe.Fori(1, ST - 1) as t:
                    pair(t)
                up(EXPERTS - 1, ST - 1, 1)
                down(EXPERTS - 2, ST - 1, 0)
                down(EXPERTS - 1, ST - 1, 1)

                def combine(b, j, p):
                    pe.wait_ge(*reached(f"{st}_staged_a", b + 1))
                    pe.wait_ge(*reached(f"{st}_staged_b", b + 1))
                    if due(b - 1):
                        pe.wait_ge(*reached(f"{st}_x", b - 1))
                    for i in range(PER):
                        for t in range(ST):
                            w = logits[:, p].rearrange("p i (t n) -> p (i t) n", t=ST // PER)
                            mm = pe.matmul(ps[:, 2 * p + i, 0:OW - 1], w[:, t, i * P:i * P + P],
                                           expert_io[:, t, b * OW:b * OW + OW - 1] if isinstance(b, int) else
                                           expert_io[:, t, bass.ds(b * OW, OW - 1)],
                                           start=t == 0, stop=t == ST - 1)
                        mm.then_inc(sem(f"{st}_combined"), 1)

                pe.wait_ge(*reached(f"{st}_eo", EXPERTS * 2))
                pe.wait_ge(*reached(f"{st}_sums", ST))
                pe.wait_ge(*reached(f"{st}_gelu", EXPERTS * 2))
                all_batches(pe, combine)

            def linear_attention_tensor(st):
                def tokens(b, p):
                    turn_batch(st, b, p, 4 * p + 2)

                def first(b, p):
                    B = 4 * p
                    pe.wait_ge(*reached(f"{st}_zt", b + 1))
                    if due(b - 1):
                        pe.wait_ge(*reached(f"{st}_qk", b - 1))
                    pe.matmul(ps[:, B, 0:SEQ], wqkv[:, 0:D], la_zt[:, p, :], start=True, stop=True)
                    for i in range(PER):
                        mm = pe.matmul(ps[:, B, SEQ + i * P:SEQ + i * P + P], la_zt[:, p, i * P:i * P + P], wqkv[:, D:2 * D],
                                       start=True, stop=True)
                    mm.then_inc(sem(f"{st}_qkp"), 1)
                    if due(b - 1):
                        pe.wait_ge(*reached(f"{st}_kv", b * 2 - 2))
                    for i in range(PER):
                        mm = pe.matmul(ps[:, B + 1, i * P:i * P + P], la_zt[:, p, i * P:i * P + P], wqkv[:, 2 * D:3 * D],
                                       start=True, stop=True)
                    mm.then_inc(sem(f"{st}_vp"), 1)

                def sums(b, p):
                    B = 4 * p
                    pe.wait_ge(*reached(f"{st}_v", b + 1))
                    pe.wait_ge(*reached(f"{st}_qk", b + 1))
                    for i in range(PER):
                        mm = pe.matmul(ps[:, B + 1, SEQ:SEQ + D + 1], la_qk[:, p, SEQ + i * P:SEQ + i * P + P],
                                       la_v[:, p, i, :], start=i == 0, stop=i == PER - 1)
                    mm.then_inc(sem(f"{st}_kvp"), 1)

                def outputs(b, p):
                    pe.wait_ge(*reached(f"{st}_kv", b * 2 + 2))
                    if due(b * 3 - 3):
                        pe.wait_ge(*reached(f"{st}_steps", b * 3 - 3))
                    for k in range(2):
                        mm = pe.matmul(ps[:, 4 * p + 3, k * SEQ:k * SEQ + SEQ], la_kv[:, p, k, :], la_qk[:, p, 0:SEQ],
                                       start=True, stop=True)
                    mm.then_inc(sem(f"{st}_op"), 1)

                def project(b, p):
                    pe.wait_ge(*reached(f"{st}_steps", b * 3 + 3))
                    for i in range(PER):
                        mm = pe.matmul(ps[:, 4 * p + 2, SEQ + i * P:SEQ + i * P + P], la_o[:, p, 0, i * P:i * P + P], wproj[:],
                                       start=True, stop=True)
                    mm.then_inc(sem(f"{st}_yp"), 1)

                def step(b, j, p):
                    more = not (isinstance(b, int) and b == BATCHES - 1)
                    if more:
                        tokens(b + 1, 1 - p)
                    sums(b, p)
                    if more:
                        first(b + 1, 1 - p)
                    if due(b):
                        project(b - 1, 1 - p)
                    outputs(b, p)

                tokens(0, 0)
                first(0, 0)
                all_batches(pe, step)
                project(BATCHES - 1, 1)

            def ffn_tensor(st):
                def tokens(c, q):
                    if due(c - 1):
                        pe.wait_ge(*reached(f"{st}_gelu", c // 2 * 4 * HK - HK))
                    turn_batch(st, 2 * c, 0, 6 + q)
                    turn_batch(st, 2 * c + 1, 1, 6 + q, SEQ)

                def gated(c, q, os):
                    pe.wait_ge(*reached(f"{st}_ztlo", c + 1))
                    if c < 2:
                        pe.wait_ge(sem("first_w_lo"), 1)
                    for o in os:
                        r = o % 2
                        for which in range(2):
                            n = c * HK + o
                            if q == 0 and o < 2 and c > 0:
                                pe.wait_ge(*reached(f"{st}_gelu", c * 2 * HK))
                            elif n >= 2:
                                pe.wait_ge(*reached(f"{st}_silu" if which == 0 else f"{st}_mixed", n - 1))
                            w = slice(which * HID + o * P, which * HID + o * P + P)
                            three(ps[:, 2 * r + which, :], ffw_hi[:, w], ffw_lo[:, w], fz_hi[:, q, :], fz_lo[:, q, :], True, True)\
                                .then_inc(sem(f"{st}_p1" if which == 0 else f"{st}_p2"), 1)

                def deep(dst, w0, width, o, hi, lo):
                    for k in range(HK):
                        w = slice(w0 + k * width + o * P, w0 + k * width + o * P + P)
                        mm = three(dst, ffw_hi[:, w], ffw_lo[:, w], hi[:, k, :], lo[:, k, :], k == 0, k == HK - 1)
                    return mm

                def hidden(j, layer, q):
                    pe.wait_ge(*reached(f"{st}_lo", ((j * 3 + layer - 1) * 2 + q) * HK + HK))
                    hi, lo = ((even_hi, even_lo), (odd_hi, odd_lo))[layer - 1]
                    for o in range(HK):
                        if layer == 1 and q == 0 and j > 0:
                            pe.wait_ge(*reached(f"{st}_yt", 2 * j))
                            pe.wait_ge(*reached(f"{st}_added", 2 * j))
                        elif layer == 1 and q == 0:
                            pe.wait_ge(*reached(f"{st}_ztlo", 2))
                        elif layer == 1:
                            pe.wait_ge(*reached(f"{st}_mixed", (j * 2 + 2) * HK))
                        else:
                            pe.wait_ge(*reached(f"{st}_gelu", (j * 4 + q) * HK + o + 1))
                        deep(ps[:, (4, 0)[q] + o, :], (W12, H1)[layer - 1], HID, o, hi[:, q], lo[:, q]).then_inc(sem(f"{st}_prod"), 1)

                def last_product(c, q):
                    pe.wait_ge(*reached(f"{st}_lo", ((c // 2 * 3 + 2) * 2 + q) * HK + HK))
                    deep(ps[:, 4 + q, :], H2, D, 0, even_hi[:, q], even_lo[:, q]).then_inc(sem(f"{st}_p3"), 1)

                def turn_back(c, q):
                    pe.wait_ge(*reached(f"{st}_yt", c + 1))
                    if c < CHUNKS - 2:
                        pe.wait_ge(*reached(f"{st}_ztlo", c + 3))
                    for i in range(CHUNK // P):
                        mm = turn(ps[:, 6 + q, i * P:i * P + P], y_t[:, q, i * P:i * P + P])
                    mm.then_inc(sem(f"{st}_yp"), 1)

                for j in range(CHUNKS // 2 + 1):
                    c = 2 * j
                    if c < CHUNKS:
                        tokens(c, 0)
                    if j > 0:
                        last_product(c - 2, 0)
                        last_product(c - 1, 1)
                    if c < CHUNKS:
                        gated(c, 0, (0, 1))
                        tokens(c + 1, 1)
                        gated(c, 0, (2, 3))
                    if j > 0:
                        turn_back(c - 2, 0)
                        turn_back(c - 1, 1)
                    if c < CHUNKS:
                        gated(c + 1, 1, range(HK))
                        if j == 0 and st == ffns[0]:
                            pe.wait_ge(sem("first_w_lo"), 2)
                        hidden(j, 1, 0)
                        hidden(j, 1, 1)
                        if j == 0 and st == ffns[0]:
                            pe.wait_ge(sem("deep_w"), 4)
                        hidden(j, 2, 0)
                        hidden(j, 2, 1)

            def favor_tensor(st):
                def first(b, p):
                    if due(b - 1):
                        pe.wait_ge(*reached(f"{st}_ot", b - 1))
                    turn_batch(st, b, p, 0)
                    pe.wait_ge(*reached(f"{st}_zt", b + 1))
                    if due(b - 1):
                        pe.wait_ge(*reached(f"{st}_yout", b - 1))
                    for k in range(2):
                        mm = pe.matmul(ps[:, 1, k * SEQ:k * SEQ + SEQ], fw[:, k, :], fa_zt[:, p, :], start=True, stop=True)
                    mm.then_inc(sem(f"{st}_qktp"), 1)
                    if due(b - 1):
                        pe.wait_ge(*reached(f"{st}_kv", b - 1))
                    if due(b * 5):
                        pe.wait_ge(*reached(f"{st}_maxs", b * 5))
                    for i in range(PER):
                        mm = pe.matmul(ps[:, 3, i * P:i * P + P], fa_zt[:, p, i * P:i * P + P], fw[:, 2, :], start=True, stop=True)
                    mm.then_inc(sem(f"{st}_vp"), 1)
                    pe.wait_ge(*reached(f"{st}_qkt", b + 1))
                    for n, a in enumerate((2, 3, 0, 1)):
                        if due((b - 1) * 4 + n + 1):
                            pe.wait_ge(*reached(f"{st}_sub", (b - 1) * 4 + (n + 1)))
                        pe.matmul(ps[:, 4 + a, :], fa_qkt[:, p, a // 2, a % 2 * P:a % 2 * P + P], proj_bd[:], start=True, stop=True)\
                            .then_inc(sem(f"{st}_xw"), 1)
                    pe.wait_ge(*reached(f"{st}_sq", b + 1))
                    pe.wait_ge(*reached(f"{st}_v", b + 1))
                    for a in range(4):
                        mm = pe.matmul(ps[:, 3, NORMS + a * HEADS:NORMS + a * HEADS + HEADS], fa_sq[:, p, a * P:a * P + P],
                                       headmask[:].rearrange("p (h d) -> p h d", d=HD)[:, :, 0], start=True, stop=True)
                    mm.then_inc(sem(f"{st}_norms"), 1)

                def second(b, p):
                    pe.wait_ge(*reached(f"{st}_phi", b * 2 + 1))
                    for g in range(FG):
                        for i in range(PER):
                            mm = pe.matmul(ps[:, 3, SEQ + g * VA:SEQ + g * VA + VA], fa_phi[:, p, 2 + i, g * P:g * P + P],
                                           fa_vaug[:, p, i, g, :], start=i == 0, stop=i == PER - 1)
                    mm.then_inc(sem(f"{st}_kvp"), 1)
                    pe.wait_ge(*reached(f"{st}_phi", b * 2 + 2))
                    for i in range(PER):
                        for g in range(FG):
                            mm = turn(ps[:, i, g * P:g * P + P], fa_phi[:, p, i, g * P:g * P + P])
                        mm.then_inc(sem(f"{st}_phitp"), 1)
                    pe.wait_ge(*reached(f"{st}_kv", b + 1))
                    for i in range(PER):
                        pe.wait_ge(*reached(f"{st}_phit", b * 2 + (i + 1)))
                        for g in range(FG):
                            mm = pe.matmul(ps[:, 2, i * SEQ + g * VA:i * SEQ + g * VA + VA], fa_phit[:, p, i, g, :], fa_kv[:, p, g, :],
                                           start=True, stop=True)
                    mm.then_inc(sem(f"{st}_np"), 1)
                    pe.wait_ge(*reached(f"{st}_o", b + 1))
                    for i in range(PER):
                        mm = turn(ps[:, 0, i * P:i * P + P], fa_o[:, p, i, :])
                    mm.then_inc(sem(f"{st}_otp"), 1)
                    pe.wait_ge(*reached(f"{st}_ot", b + 1))
                    for i in range(PER):
                        mm = pe.matmul(ps[:, 1, i * P:i * P + P], fa_ot[:, p, i * P:i * P + P], fw[:, 3, :], start=True, stop=True)
                    mm.then_inc(sem(f"{st}_yp"), 1)

                def step(b, j, p):
                    if not (isinstance(b, int) and b == BATCHES - 1):
                        first(b + 1, 1 - p)
                    second(b, p)

                first(0, 0)
                all_batches(pe, step)

            pe.wait_ge(sem("ld_const"), 16)
            if "m0" in stages:
                for t in range(ST):
                    pe.wait_ge(sem("se_norm"), t + 1)
                    turn(ps[:, t // 4, t % 4 * P:t % 4 * P + P], logits[:, 1, 0, t * D:t * D + D]).then_inc(sem("se_turned"), 1)
                pe.wait_ge(sem("se_ready"), 7)
                pe.wait_ge(sem("dve_const"), 1)
            for st in stages:
                if before[st] != "init":
                    pe.wait_ge(sem(f"{before[st]}_x"), BATCHES)
                if st == "la" or before[st] == "init":
                    pe.wait_ge(sem("ld_w"), 16 * 12)
                {"m": moe_tensor, "l": linear_attention_tensor, "f": ffn_tensor}[st[0]](st) if st != "fa" else favor_tensor(st)

        @block.scalar
        def _(act):
            def moe_scalar(st):
                def tokens(b, p):
                    act.wait_ge(*reached(f"{st}_turned", b + 1))
                    act.copy(zt_hi[:, p, :], ps[:, 4, 0:SEQ]).then_inc(sem(f"{st}_zthi"), 1)

                def copies(b, p):
                    if due(b - 1):
                        act.wait_ge(*reached(f"{st}_slots", b - 1))
                    for i in range(PER):
                        act.wait_ge(*reached(f"{st}_rows", b * 2 + (i + 1)))
                        act.copy(logits[:, p, i, :], ps[:, 4 + 2 * i:6 + 2 * i, :].rearrange("p h n -> p (h n)"))\
                            .then_inc(sem(f"{st}_copied"), 1)

                def sums(b, p, ks):
                    for k in ks:
                        act.wait_ge(*reached(f"{st}_maxs", b * 4 + (k + 1)))
                        if due(b * 4 + (k - 1)):
                            act.wait_ge(*reached(f"{st}_zs", b * 4 + (k - 1)))
                        for h in range(2):
                            t = 2 * k + h
                            last = act.activation(junk[:, 2 * (k % 2) + h, :], ps[:, k, h * SEQ:h * SEQ + SEQ], ACT.Exp,
                                                  bias=negmax_s[:, p, t:t + 1], accum_out=zsum_s[:, p, t:t + 1])
                        last.then_inc(sem(f"{st}_zs"), 1)

                def logs(b, p):
                    act.wait_ge(*reached(f"{st}_zs", b * 4 + 4))
                    act.activation(lnz_s[:, p, :], zsum_s[:, p, :], ACT.Ln).then_inc(sem(f"{st}_lnz"), 1)

                def dispatch(b, p):
                    for i in range(PER):
                        act.wait_ge(*reached(f"{st}_sub", b * 2 + (i + 1)))
                        act.activation(logits[:, p, i, :], logits[:, p, i, :], ACT.Exp).then_inc(sem(f"{st}_disp"), 1)

                def weights(b, p):
                    for k in range(4):
                        act.wait_ge(*reached(f"{st}_shifted", b * 4 + (k + 1)))
                        dst = comb[:, b, 2 * k:2 * k + 2, :] if isinstance(b, int) else comb[:, bass.ds(b, 1), 2 * k:2 * k + 2, :].rearrange("p a t n -> p (a t) n")
                        act.activation(dst, ps[:, k, :].rearrange("p (t n) -> p t n", t=2), ACT.Exp).then_inc(sem(f"{st}_comb"), 1)

                def slots_out(b, j, p):
                    act.wait_ge(*reached(f"{st}_slots", b + 1))
                    store_slots(act.copy, j, p, 0).then_inc(sem(f"{st}_slots_a"), 1)

                act.preload_act_table_set("natural_log_exp_and_others")
                tokens(0, 0)
                copies(0, 0)
                sums(0, 0, range(4))
                logs(0, 0)
                weights(0, 0)
                tokens(1, 1)

                def step(b, j, p, ahead=True, last=False):
                    if not last:
                        copies(b + 1, 1 - p)
                        sums(b + 1, 1 - p, (0, 1))
                    dispatch(b, p)
                    if not last:
                        sums(b + 1, 1 - p, (2, 3))
                        logs(b + 1, 1 - p)
                    slots_out(b, j, p)
                    if ahead:
                        tokens(b + 2, p)
                    if not last:
                        weights(b + 1, 1 - p)

                step(0, 0, 0)
                looped(act, step, 1, BATCHES - 3)
                step(BATCHES - 3, 2, 1)
                step(BATCHES - 2, 3, 0, False)
                step(BATCHES - 1, 3, 1, False, True)

                def gelus(e, p):
                    for f in range(2):
                        act.wait_ge(*reached(f"{st}_gate", e * 2 + (f + 1)))
                        if due((e - 1) * 2 + (f + 1)):
                            act.wait_ge(*reached(f"{st}_h", (e - 1) * 2 + (f + 1)))
                        bias = bgu[:, 0, e, f:f + 1] if isinstance(e, int) else bgu[:, 0, bass.ds(e, 1), f]
                        act.activation(gate[:, f, :], ps[:, f, :], ACT.Gelu, bias=bias).then_inc(sem(f"{st}_gelu"), 1)

                gelus(0, 0)
                with act.Fori(0, ST - 1) as t:
                    gelus(t * 2 + 1, 1)
                    gelus(t * 2 + 2, 0)
                gelus(EXPERTS - 1, 1)

                def stage(b, j, p):
                    if due((b - 1) * 2):
                        act.wait_ge(*reached(f"{st}_combined", (b - 1) * 2))
                    src = comb[:, b, 0:ST // 2, :] if isinstance(b, int) else comb[:, bass.ds(b, 1), 0:ST // 2, :].rearrange("p a t n -> p (a t) n")
                    act.copy(logits[:, p, 0, :].rearrange("p (t n) -> p t n", t=ST // 2), src).then_inc(sem(f"{st}_staged_a"), 1)

                all_batches(act, stage)

            def linear_attention_scalar(st):
                def first(b, p):
                    B = 4 * p
                    act.wait_ge(*reached(f"{st}_turned", b + 1))
                    act.copy(la_zt[:, p, :], ps[:, B + 2, 0:SEQ]).then_inc(sem(f"{st}_zt"), 1)
                    act.wait_ge(*reached(f"{st}_vp", b + 1))
                    act.copy(la_v[:, p, :, 0:D], ps[:, B + 1, 0:SEQ].rearrange("p (i d) -> p i d", i=PER)).then_inc(sem(f"{st}_v"), 1)
                    act.wait_ge(*reached(f"{st}_min", b + 1))
                    act.activation(la_min[:, p, :], la_min[:, p, :], ACT.Exp).then_inc(sem(f"{st}_exp"), 1)
                act.wait_ge(*reached(f"{st}_vones", 1))
                all_batches(act, lambda b, j, p: first(b, p))

            def ffn_scalar(st):
                def tokens(c, q):
                    act.wait_ge(*reached(f"{st}_turned", 2 * c + 2))
                    act.copy(fz_hi[:, q, :], ps[:, 6 + q, :]).then_inc(sem(f"{st}_zthi"), 1)

                def silus(c, q, os):
                    for o in os:
                        n = c * HK + o
                        act.wait_ge(*reached(f"{st}_p1", n + 1))
                        if n >= 2:
                            act.wait_ge(*reached(f"{st}_mixed", n - 1))
                        act.activation(silu_out[:, o % 2, :], ps[:, 2 * (o % 2), :], ACT.Silu, scale=ffn_s[:, 0, o:o + 1])\
                            .then_inc(sem(f"{st}_silu"), 1)
                        if n % (2 * HK) >= 1:
                            high(n - 1)
                def high(n):
                    c, o = n // HK, n % HK
                    act.wait_ge(*reached(f"{st}_mixed", n + 1))
                    act.copy(even_hi[:, c % 2, o, :], whole[:, o, :]).then_inc(sem(f"{st}_mixhi"), 1)

                def gelus(j, layer, q):
                    for o in range(HK):
                        n = (j * 4 + (layer - 1) * 2 + q) * HK + o
                        act.wait_ge(*reached(f"{st}_prod", n + 1))
                        act.wait_ge(*reached(f"{st}_lo", ((j * 3 + layer) * 2 + q - 1) * HK + o + 1))
                        act.activation(whole[:, o, :], ps[:, (4, 0)[q] + o, :], ACT.Gelu, scale=ffn_s[:, 1 + layer, o:o + 1])\
                            .then_inc(sem(f"{st}_gelu"), 1)

                def scaled(c, q):
                    act.wait_ge(*reached(f"{st}_p3", c + 1))
                    if c >= 2:
                        act.wait_ge(*reached(f"{st}_yp", c - 1))
                    act.mul(y_t[:, q, :], ps[:, 4 + q, :], w3_s[:, 1:2]).then_inc(sem(f"{st}_yt"), 1)

                if st == ffns[0]:
                    act.wait_ge(sem("ld_ffw"), 16)
                    for part in (slice(0, W12), slice(W12, H1)):
                        act.copy(ffw_hi[:, part], ffw[:, part]).then_inc(sem("first_w_hi"), 1)
                for j in range(CHUNKS // 2 + 1):
                    c = 2 * j
                    if c < CHUNKS:
                        tokens(c, 0)
                    if j > 0:
                        scaled(c - 2, 0)
                        scaled(c - 1, 1)
                    if c < CHUNKS:
                        silus(c, 0, (0, 1))
                        tokens(c + 1, 1)
                        silus(c, 0, (2, 3))
                        silus(c + 1, 1, range(HK))
                        high((c + 2) * HK - 1)
                        for layer in (1, 2):
                            gelus(j, layer, 0)
                            gelus(j, layer, 1)

            def favor_scalar(st):
                def first(b, p):
                    act.wait_ge(*reached(f"{st}_turned", b + 1))
                    act.copy(fa_zt[:, p, :], ps[:, 0, 0:SEQ]).then_inc(sem(f"{st}_zt"), 1)
                    act.wait_ge(*reached(f"{st}_qktp", b + 1))
                    act.mul(fa_qkt[:, p].rearrange("p k n -> p (k n)"), ps[:, 1, :], QK_SCALE).then_inc(sem(f"{st}_qkt"), 1)
                    act.activation(fa_sq[:, p, :], ps[:, 1, :], ACT.Square, scale=QK_SCALE * 0.5 ** 0.5).then_inc(sem(f"{st}_sq"), 1)
                    act.wait_ge(*reached(f"{st}_vp", b + 1))
                    act.copy(fa_vaug[:, p, :, :, 0:VA - 4], ps[:, 3, 0:SEQ].rearrange("p (i g d) -> p i g d", i=PER, g=FG))\
                        .then_inc(sem(f"{st}_v"), 1)

                def exponentials(b, p, n):
                    act.wait_ge(*reached(f"{st}_sub", b * 4 + (2 * n + 2)))
                    phi = fa_phi[:, p, 2 - 2 * n:4 - 2 * n].rearrange("p a f -> p (a f)")
                    act.activation(phi, phi, ACT.Exp).then_inc(sem(f"{st}_exp"), 1)

                def turned(b, p):
                    for i in range(PER):
                        act.wait_ge(*reached(f"{st}_phitp", b * 2 + (i + 1)))
                        act.copy(fa_phit[:, p, i].rearrange("p g n -> p (g n)"), ps[:, i, :]).then_inc(sem(f"{st}_phit"), 1)

                def outputs(b, p):
                    act.wait_ge(*reached(f"{st}_otp", b + 1))
                    act.copy(fa_ot[:, p, :], ps[:, 0, 0:SEQ]).then_inc(sem(f"{st}_ot"), 1)

                def step(b, j, p):
                    more = not (isinstance(b, int) and b == BATCHES - 1)
                    if more:
                        first(b + 1, 1 - p)
                    turned(b, p)
                    if more:
                        exponentials(b + 1, 1 - p, 0)
                    outputs(b, p)
                    if more:
                        exponentials(b + 1, 1 - p, 1)

                act.wait_ge(*reached(f"{st}_vones", 1))
                first(0, 0)
                exponentials(0, 0, 0)
                exponentials(0, 0, 1)
                all_batches(act, step)

            for st in stages:
                if before[st] != "init":
                    act.wait_ge(sem(f"{before[st]}_x"), BATCHES)
                if before[st] == "init":
                    act.wait_ge(sem("ld_w"), 16 * 12)
                {"m": moe_scalar, "l": linear_attention_scalar, "f": ffn_scalar}[st[0]](st) if st != "fa" else favor_scalar(st)

        @block.vector
        def _(dve):
            def after(st, b):
                go = Steps(f"{st}_mom", b * 4)
                if due(b):
                    dve.wait_ge(*reached(f"{st}_x", b, dve))
                for i in range(PER):
                    src = x[:, b * PER + i, :] if isinstance(b, int) else x[:, bass.ds(b * PER + i, 1), :].rearrange("p a d -> p (a d)")
                    dve.bn_stats(bn6[:, i, :], src).then_inc(go.sem, go.step())
                dve.wait_ge(go.sem, plain(dve, go.n))
                for i in range(PER):
                    dve.bn_aggr(fresh[:, i, :], bn6[:, i, :]).then_inc(go.sem, go.step())
                dve.wait_ge(go.sem, plain(dve, go.n))
                dve.tensor_copy(moments[:, batch(b), :], fresh[:]).then_inc(sem(f"{st}_x"), 1)

            def moe_vector(st):
                def tokens(b, p):
                    dve.wait_ge(*reached(f"{st}_zthi", b + 1))
                    dve.tensor_tensor(zt_lo[:, p, :], ps[:, 4, 0:SEQ], as32(zt_hi[:, p, :]), ALU.subtract)\
                        .then_inc(sem(f"{st}_ztlo"), 1)

                def max_n(b, p):
                    if due((b - 1) * 4):
                        dve.wait_ge(*reached(f"{st}_shifted", (b - 1) * 4))
                    for i in range(PER):
                        dve.wait_ge(*reached(f"{st}_copied", b * 2 + (i + 1)))
                        dve.tensor_reduce(negmax_n[:, p, i:i + 1], logits[:, p, i, :], AX_X, ALU.max, negate=True)\
                            .then_inc(sem(f"{st}_maxn"), 1)

                def max_s(b, p, ks):
                    for k in ks:
                        dve.wait_ge(*reached(f"{st}_columns", b * 4 + (k + 1)))
                        dve.tensor_reduce(negmax_s[:, p, 2 * k:2 * k + 2], ps[:, k, :].rearrange("p (t n) -> p t n", t=2),
                                          AX_X, ALU.max, negate=True).then_inc(sem(f"{st}_maxs"), 1)

                def subtract(b, p):
                    dve.wait_ge(*reached(f"{st}_spread", b + 1))
                    for i in range(PER):
                        dve.tensor_tensor(logits[:, p, i, :], logits[:, p, i, :],
                                          ps[:, 4:6, :].rearrange("p h n -> p (h n)"), ALU.add).then_inc(sem(f"{st}_sub"), 1)

                def slots_out(b, j, p):
                    dve.wait_ge(*reached(f"{st}_slots", b + 1))
                    store_slots(dve.tensor_copy, j, p, 1).then_inc(sem(f"{st}_slots_b"), 1)

                tokens(0, 0)
                max_n(0, 0)
                max_s(0, 0, range(4))
                tokens(1, 1)

                def step(b, j, p, ahead=True, last=False):
                    if not last:
                        max_s(b + 1, 1 - p, (0, 1))
                    subtract(b, p)
                    if not last:
                        max_s(b + 1, 1 - p, (2, 3))
                        max_n(b + 1, 1 - p)
                    slots_out(b, j, p)
                    if ahead:
                        tokens(b + 2, p)

                step(0, 0, 0)
                looped(dve, step, 1, BATCHES - 3)
                step(BATCHES - 3, 2, 1)
                step(BATCHES - 2, 3, 0, False)
                step(BATCHES - 1, 3, 1, False, True)

                def mix(e, p):
                    for f in range(2):
                        dve.wait_ge(*reached(f"{st}_gelu", e * 2 + (f + 1)))
                        dve.wait_ge(*reached(f"{st}_up", e * 2 + (f + 1)))
                        if due(e - 1):
                            dve.wait_ge(*reached(f"{st}_down", e - 1))
                        bias = bgu[:, 1, e, f:f + 1] if isinstance(e, int) else bgu[:, 1, bass.ds(e, 1), f]
                        dve.scalar_tensor_tensor(hmid[:, p, f, :], ps[:, 2 + f, :], bias, gate[:, f, :], ALU.add, ALU.mult)\
                            .then_inc(sem(f"{st}_h"), 1)

                def outputs(e, t, p):
                    dve.wait_ge(*reached(f"{st}_down", e + 1))
                    for half in range(2):
                        rows = slice(half * 64, half * 64 + 64)
                        block_t = expert_io[rows, t, :] if isinstance(t, int) else expert_io[rows, bass.ds(t, 1), :].rearrange("p a n -> p (a n)")
                        dst = block_t.rearrange("p (j q o) -> p q j o", q=2, o=OW)[:, half ^ p, :, 0:D]
                        bias = bd_bc[rows, e:e + 1, :] if isinstance(e, int) else bd_bc[rows, bass.ds(e, 1), :]
                        dve.tensor_tensor(dst, ps[rows, 4 + p, :].rearrange("p (j o) -> p j o", o=D),
                                          bias.broadcast_to([64, BATCHES // 2, D]), ALU.add).then_inc(sem(f"{st}_eo"), 1)

                dve.wait_ge(sem("dve_two"), 1)

                def sum_columns(t):
                    block_t = expert_io[:, t, :] if isinstance(t, int) else expert_io[:, bass.ds(t, 1), :].rearrange("p a n -> p (a n)")
                    dve.tensor_copy(block_t.rearrange("p (b o) -> p b o", o=OW)[:, :, D:OW], two[:].rearrange("p (b o) -> p b o", o=2)).then_inc(sem(f"{st}_sums"), 1)

                mix(0, 0)
                with dve.Fori(0, ST - 1) as t:
                    mix(t * 2 + 1, 1)
                    outputs(t * 2, t, 0)
                    mix(t * 2 + 2, 0)
                    outputs(t * 2 + 1, t, 1)
                    sum_columns(t)
                mix(EXPERTS - 1, 1)
                outputs(EXPERTS - 2, ST - 1, 0)
                outputs(EXPERTS - 1, ST - 1, 1)
                sum_columns(ST - 1)

                def stage(b, j, p):
                    if due((b - 1) * 2):
                        dve.wait_ge(*reached(f"{st}_combined", (b - 1) * 2))
                    src = comb[:, b, ST // 2:ST, :] if isinstance(b, int) else comb[:, bass.ds(b, 1), ST // 2:ST, :].rearrange("p a t n -> p (a t) n")
                    dve.tensor_copy(logits[:, p, 1, :].rearrange("p (t n) -> p t n", t=ST // 2), src).then_inc(sem(f"{st}_staged_b"), 1)

                def residual(b, j, p):
                    go = Steps(f"{st}_steps", b * 4)
                    for i in range(PER):
                        dve.wait_ge(*reached(f"{st}_combined", b * 2 + (i + 1)))
                        dve.reciprocal(zcol[:, p, i:i + 1], ps[:, 2 * p + i, D:D + 1]).then_inc(go.sem, go.step())
                    dve.wait_ge(go.sem, go.n)
                    for i in range(PER):
                        tile = b * PER + i
                        xt = x[:, tile, :] if isinstance(b, int) else x[:, bass.ds(tile, 1), :].rearrange("p a d -> p (a d)")
                        dve.scalar_tensor_tensor(xt, ps[:, 2 * p + i, 0:D], zcol[:, p, i:i + 1], xt, ALU.mult, ALU.add).then_inc(go.sem, go.step())
                    dve.wait_ge(go.sem, plain(dve, go.n))
                    after(st, b)

                stage(0, 0, 0)
                def finish(b, j, p):
                    if not (isinstance(b, int) and b == BATCHES - 1):
                        stage(b + 1, None, 1 - p)
                    residual(b, j, p)
                all_batches(dve, finish)

            def linear_attention_vector(st):
                def minima(b, p):
                    dve.wait_ge(*reached(f"{st}_qkp", b + 1))
                    dve.tensor_scalar(la_min[:, p, :], ps[:, 4 * p, :], 0.0, None, ALU.min).then_inc(sem(f"{st}_min"), 1)

                def features(b, p):
                    dve.wait_ge(*reached(f"{st}_exp", b + 1))
                    dve.scalar_tensor_tensor(la_qk[:, p, :], ps[:, 4 * p, :], 0.0, la_min[:, p, :], ALU.max, ALU.add)\
                        .then_inc(sem(f"{st}_qk"), 1)

                def sums(b, p):
                    B = 4 * p
                    dve.wait_ge(*reached(f"{st}_kvp", b + 1))
                    dve.tensor_tensor(la_kv[:, p, 0, :], ps[:, B + 1, SEQ:SEQ + D], headmask[:], ALU.mult).then_inc(sem(f"{st}_kv"), 1)
                    dve.tensor_scalar(la_kv[:, p, 1, :], headmask[:], ps[:, B + 1, SEQ + D:SEQ + D + 1], None, ALU.mult)\
                        .then_inc(sem(f"{st}_kv"), 1)

                def divide(b, p):
                    go = Steps(f"{st}_steps", b * 3)
                    den = la_o[:, p, 1, :]
                    dve.wait_ge(*reached(f"{st}_op", b + 1))
                    dve.tensor_scalar(den, ps[:, 4 * p + 3, SEQ:2 * SEQ], ATT_EPS, None, ALU.add).then_inc(go.sem, go.step())
                    dve.wait_ge(go.sem, go.n)
                    dve.reciprocal(den, den).then_inc(go.sem, go.step())
                    dve.wait_ge(go.sem, go.n)
                    dve.tensor_tensor(la_o[:, p, 0, :], ps[:, 4 * p + 3, 0:SEQ], den, ALU.mult).then_inc(go.sem, go.step())

                def residual(b, p):
                    go = Steps(f"{st}_added", b * 2)
                    dve.wait_ge(*reached(f"{st}_yp", b + 1))
                    tmp = la_o[:, p, 1, :].rearrange("p (i d) -> p i d", i=PER)
                    dve.tensor_tensor(tmp, ps[:, 4 * p + 2, SEQ:2 * SEQ].rearrange("p (i d) -> p i d", i=PER),
                                      bproj_bc[:].unsqueeze(1).broadcast_to([P, PER, D]), ALU.add).then_inc(go.sem, go.step())
                    dve.wait_ge(go.sem, go.n)
                    xb = x[:, batch(b), :]
                    dve.tensor_tensor(xb, xb, tmp, ALU.add).then_inc(go.sem, go.step())
                    dve.wait_ge(go.sem, plain(dve, go.n))
                    after(st, b)

                def step(b, j, p):
                    more = not (isinstance(b, int) and b == BATCHES - 1)
                    sums(b, p)
                    if more:
                        minima(b + 1, 1 - p)
                    if due(b):
                        residual(b - 1, 1 - p)
                    if more:
                        features(b + 1, 1 - p)
                    divide(b, p)

                dve.memset(la_v[:, :, :, D:D + 1], 1.0).then_inc(sem(f"{st}_vones"), 1)
                minima(0, 0)
                features(0, 0)
                all_batches(dve, step)
                residual(BATCHES - 1, 1)

            def ffn_vector(st):
                def tokens(c, q):
                    dve.wait_ge(*reached(f"{st}_zthi", c + 1))
                    dve.tensor_tensor(fz_lo[:, q, :], ps[:, 6 + q, :], as32(fz_hi[:, q, :]), ALU.subtract).then_inc(sem(f"{st}_ztlo"), 1)

                def low(hi, lo, o):
                    dve.tensor_tensor(lo[:, o, :], whole[:, o, :], as32(hi[:, o, :]), ALU.subtract).then_inc(sem(f"{st}_lo"), 1)

                def mixes(c, q, os):
                    for o in os:
                        n = c * HK + o
                        dve.wait_ge(*reached(f"{st}_p2", n + 1))
                        dve.wait_ge(*reached(f"{st}_silu", n + 1))
                        done = (c // 2 * 6 + q) * HK + o + 1 - HK
                        if done > 0:
                            dve.wait_ge(*reached(f"{st}_lo", done))
                        dve.scalar_tensor_tensor(whole[:, o, :], ps[:, 2 * (o % 2) + 1, :], ffn_s[:, 1, o:o + 1], silu_out[:, o % 2, :],
                                                 ALU.mult, ALU.mult).then_inc(sem(f"{st}_mixed"), 1)
                        if n % (2 * HK) >= 1:
                            low_mixed(n - 1)

                def low_mixed(n):
                    dve.wait_ge(*reached(f"{st}_mixhi", n + 1))
                    low(even_hi[:, n // HK % 2], even_lo[:, n // HK % 2], n % HK)

                def splits(j, layer, q):
                    hi, lo = ((odd_hi, odd_lo), (even_hi, even_lo))[layer - 1]
                    for o in range(HK):
                        n = (j * 4 + (layer - 1) * 2 + q) * HK + o
                        dve.wait_ge(*reached(f"{st}_gelu", n + 1))
                        dve.tensor_copy(hi[:, q, o, :], whole[:, o, :]).then_inc(sem(f"{st}_gelhi"), 1)
                        dve.wait_ge(*reached(f"{st}_gelhi", n + 1))
                        low(hi[:, q], lo[:, q], o)

                def residual(c, q):
                    dve.wait_ge(*reached(f"{st}_yp", c + 1))
                    xc = x[:, 4 * c:4 * c + 4, :]
                    dve.tensor_tensor(xc, xc, ps[:, 6 + q, :].rearrange("p (t d) -> p t d", d=D), ALU.add)\
                        .then_inc(sem(f"{st}_added"), 1)

                def norms(c):
                    dve.wait_ge(*reached(f"{st}_added", c + 1))
                    for b in (2 * c, 2 * c + 1):
                        after(st, b)

                if st == ffns[0]:
                    for n, part in enumerate((slice(0, W12), slice(W12, H1))):
                        dve.wait_ge(sem("first_w_hi"), n + 1)
                        dve.tensor_tensor(ffw_lo[:, part], ffw[:, part], as32(ffw_hi[:, part]), ALU.subtract).then_inc(sem("first_w_lo"), 1)
                for j in range(CHUNKS // 2 + 1):
                    c = 2 * j
                    if c < CHUNKS:
                        tokens(c, 0)
                        mixes(c, 0, (0, 1))
                        tokens(c + 1, 1)
                        mixes(c, 0, (2, 3))
                    if j > 0:
                        residual(c - 2, 0)
                        residual(c - 1, 1)
                    if c < CHUNKS:
                        mixes(c + 1, 1, range(HK))
                        low_mixed((c + 2) * HK - 1)
                        splits(j, 1, 0)
                    if j > 0:
                        norms(c - 2)
                        norms(c - 1)
                    if c < CHUNKS:
                        splits(j, 1, 1)
                        splits(j, 2, 0)
                        splits(j, 2, 1)

            def favor_vector(st):
                def maxima(b, p):
                    cc = fa_c[:, p]
                    go = Steps(f"{st}_maxs", b * 5)
                    for n, a in enumerate((2, 3, 0, 1)):
                        dve.wait_ge(*reached(f"{st}_xw", b * 4 + (n + 1)))
                        dve.tensor_reduce(cc[:, 0, a * HEADS:a * HEADS + HEADS], ps[:, 4 + a, :].rearrange("p (h m) -> p h m", m=FEAT),
                                          AX_X, ALU.max).then_inc(go.sem, go.step())

                def shifts(b, p):
                    cc = fa_c[:, p]
                    go = Steps(f"{st}_maxs", b * 5 + 4)
                    dve.wait_ge(go.sem, go.n)
                    dve.wait_ge(*reached(f"{st}_norms", b + 1))
                    dve.tensor_tensor(cc[:, 1, :], ps[:, 3, NORMS:NORMS + 4 * HEADS], cc[:, 0, :], ALU.add).then_inc(go.sem, go.step())

                def subtract(b, p, n):
                    dve.wait_ge(*reached(f"{st}_maxs", b * 5 + 5))
                    for a in (2 - 2 * n, 3 - 2 * n):
                        dve.tensor_tensor(fa_phi[:, p, a, :].rearrange("p (h m) -> p h m", m=FEAT),
                                          ps[:, 4 + a, :].rearrange("p (h m) -> p h m", m=FEAT),
                                          fa_c[:, p, 1, a * HEADS:a * HEADS + HEADS].unsqueeze(2).broadcast_to([P, HEADS, FEAT]),
                                          ALU.subtract).then_inc(sem(f"{st}_sub"), 1)

                def guards(b, p):
                    for n in range(2):
                        dve.wait_ge(*reached(f"{st}_exp", b * 2 + (n + 1)))
                        phi = fa_phi[:, p, 2 - 2 * n:4 - 2 * n].rearrange("p a f -> p (a f)")
                        dve.tensor_scalar(phi, phi, ATT_EPS, None, ALU.add).then_inc(sem(f"{st}_phi"), 1)

                def sums(b, p):
                    dve.wait_ge(*reached(f"{st}_kvp", b + 1))
                    dve.tensor_tensor(fa_kv[:, p], ps[:, 3, SEQ:SEQ + FG * VA].rearrange("p (g v) -> p g v", g=FG),
                                      featmask[:].unsqueeze(1).broadcast_to([P, FG, VA]), ALU.mult).then_inc(sem(f"{st}_kv"), 1)

                def divide(b, p):
                    go = Steps(f"{st}_steps", b * 3)
                    dve.wait_ge(*reached(f"{st}_np", b + 1))
                    num = ps[:, 2, :].rearrange("p (i r) -> p i r", i=PER)[:, :, 0:FG * VA].rearrange("p i (g v) -> p i g v", g=FG)
                    den = fa_den[:, p, :].rearrange("p (i g h) -> p i g h", i=PER, g=FG)
                    dve.tensor_scalar(den, num[:, :, :, VA - 4:VA], ATT_EPS * FEAT, None, ALU.add).then_inc(go.sem, go.step())
                    dve.wait_ge(go.sem, go.n)
                    dve.reciprocal(fa_den[:, p, :], fa_den[:, p, :]).then_inc(go.sem, go.step())
                    dve.wait_ge(go.sem, go.n)
                    for i in range(PER):
                        last = dve.tensor_tensor(fa_o[:, p, i, :].rearrange("p (g h d) -> p g h d", g=FG, h=4),
                                                 num[:, i, :, 0:VA - 4].rearrange("p g (h d) -> p g h d", h=4),
                                                 den[:, i].unsqueeze(3).broadcast_to([P, FG, 4, HD]), ALU.mult)
                    last.then_inc(sem(f"{st}_o"), 1)

                def residual(b, p):
                    dve.wait_ge(*reached(f"{st}_yp", b + 1))
                    dve.tensor_tensor(fa_y[:, p], ps[:, 1, 0:SEQ].rearrange("p (i d) -> p i d", i=PER),
                                      bo_bc[:].unsqueeze(1).broadcast_to([P, PER, D]), ALU.add).then_inc(sem(f"{st}_yout"), 1)
                    dve.wait_ge(*reached(f"{st}_yout", b + 1))
                    xb = x[:, batch(b), :]
                    go = Steps(f"{st}_steps", b * 3 + 2)
                    dve.tensor_tensor(xb, xb, fa_y[:, p], ALU.add).then_inc(go.sem, go.step())
                    dve.wait_ge(go.sem, plain(dve, go.n))
                    after(st, b)

                def step(b, j, p):
                    more = not (isinstance(b, int) and b == BATCHES - 1)
                    guards(b, p)
                    if more:
                        maxima(b + 1, 1 - p)
                    sums(b, p)
                    if more:
                        shifts(b + 1, 1 - p)
                        subtract(b + 1, 1 - p, 0)
                    divide(b, p)
                    if more:
                        subtract(b + 1, 1 - p, 1)
                    residual(b, p)

                dve.memset(fa_vaug[:, :, :, :, VA - 4:VA], 1.0).then_inc(sem(f"{st}_vones"), 1)
                maxima(0, 0)
                shifts(0, 0)
                subtract(0, 0, 0)
                subtract(0, 0, 1)
                all_batches(dve, step)

            dve.memset(two[:], 2.0).then_inc(sem("dve_two"), 1)
            dve.wait_ge(sem("ld_const"), 16)
            dve.tensor_copy(ident_r[:], ident[:]).then_inc(sem("dve_const"), 1)
            dve.wait_ge(sem("dve_const"), 1)
            for b in range(BATCHES):
                if b % 4 == 0:
                    dve.wait_ge(sem(f"ld_x{b // 4}"), 16)
                after("init", b)
            if "m0" in stages:
                dve.wait_ge(sem("ld_se"), 32)
                go = Steps("se_steps")
                for k in range(2):
                    dve.tensor_tensor(cols[:, 3 + k:4 + k], cols[:, k:k + 1], cols[:, 2:3], ALU.mult).then_inc(go.sem, go.step())
                for t in range(ST):
                    dve.bn_stats(se_stat[:, t, 0:6], logits[:, 1, 0, t * D:t * D + D]).then_inc(go.sem, go.step())
                dve.wait_ge(go.sem, go.n)
                for t in range(ST):
                    dve.bn_aggr(se_stat[:, t, 6:8], se_stat[:, t, 0:6]).then_inc(sem("se_moments"), 1)
                flat = logits[:, 0, 0, :]
                for k in range(2):
                    dve.wait_ge(sem("se_turned"), 4 * k + 4)
                    dve.tensor_scalar(flat[:, k * 512:k * 512 + 512], ps[:, k, :], cols[:, 3:4], cols[:, 4:5], ALU.mult, ALU.add).then_inc(go.sem, go.step())
                dve.wait_ge(go.sem, go.n)
                pairs = flat.rearrange("p (t h s) -> p t h s", t=ST, h=2)
                go2 = Steps("se_ready")
                dve.tensor_copy(se_hi[:, 0, :], flat).then_inc(go2.sem, go2.step())
                swapped = [t[:, 1, :].rearrange("p (t h s) -> p t h s", t=ST, h=2) for t in (se_hi, se_lo)]
                for h in range(2):
                    dve.tensor_copy(swapped[0][:, :, 1 - h, :], pairs[:, :, h, :]).then_inc(go2.sem, go2.step())
                dve.wait_ge(go2.sem, go2.n)
                dve.tensor_tensor(se_lo[:, 0, :], flat, as32(se_hi[:, 0, :]), ALU.subtract).then_inc(go2.sem, go2.step())
                for h in range(2):
                    dve.tensor_tensor(swapped[1][:, :, 1 - h, :], pairs[:, :, h, :],
                                              as32(swapped[0][:, :, 1 - h, :]), ALU.subtract).then_inc(go2.sem, go2.step())
                dve.memset(junk[:, 0, 0:1], 0.0).then_inc(sem("se_ready"), 1)
                go2.n += 1
                dve.wait_ge(go2.sem, go2.n)
            for st in stages:
                if before[st] != "init":
                    dve.wait_ge(sem(f"{before[st]}_x"), BATCHES)
                if before[st] == "init":
                    dve.wait_ge(sem("ld_w"), 16 * 12)
                if st == "f0":
                    dve.tensor_scalar(w3_s[:, 1:2], w3_s[:, 0:1], 0.5, None, ALU.mult).then_inc(sem("w3_half"), 1)
                {"m": moe_vector, "l": linear_attention_vector, "f": ffn_vector}[st[0]](st) if st != "fa" else favor_vector(st)


def arrange(a):
    f = np.float32
    t = lambda m: np.ascontiguousarray(np.transpose(m))
    rows = lambda m, k: np.ascontiguousarray(m.reshape(k, P, -1).transpose(1, 0, 2).reshape(P, -1))
    got = {
        "x": np.ascontiguousarray(a["L0_attn_x"].reshape(BATCHES * SEQ, D)),
        "ident": np.eye(P, dtype=f),
        "slot_embeds": np.ascontiguousarray(a["L0_ffn_slot_embeds"].reshape(NSLOT, D)),
        "cols": np.ascontiguousarray(np.stack([a["L0_ffn_slot_g"], a["L0_ffn_slot_b"], np.broadcast_to(a["L0_ffn_scale"], (D,))], 1)),
        "affine": np.stack([a["L0_ffn_norm_g"], a["L0_ffn_norm_b"]]),
        "bgu": np.ascontiguousarray(np.stack([a["L0_ffn_bg"], a["L0_ffn_bu"]]).reshape(2, EXPERTS, 2, P).transpose(3, 0, 1, 2).reshape(P, -1)),
        "bd": np.ascontiguousarray(a["L0_ffn_bd"]),
        "wqkv": t(a["L0_attn_Wqkv"]),
        "wproj": t(a["L0_attn_Wproj"]),
        "headmask": np.kron(np.eye(HEADS, dtype=f), np.ones((HD, HD), f)),
        "bproj": np.ascontiguousarray(a["L0_attn_bproj"]),
        "bo": np.ascontiguousarray(a["L1_attn_bo"]),
        "fw": np.concatenate([t(a[f"L1_attn_W{k}"]) for k in "qkvo"], 1),
        "ffn_s": np.concatenate([a[f"L1_ffn_{k}_s"].reshape(HK, P).T for k in ("w1", "w2", "h1", "h2")], 1),
        "w3_s": np.ascontiguousarray(a["L1_ffn_w3_s"].reshape(D, 1)),
        "wx": np.concatenate([a["L0_ffn_Wg"], a["L0_ffn_Wu"],
                              a["L0_ffn_Wd"].reshape(EXPERTS, 2, P, D).transpose(0, 2, 1, 3).reshape(EXPERTS, P, 2 * D)], 2),
        "ffw": np.concatenate([t(a["L1_ffn_w1_w"]), t(a["L1_ffn_w2_w"]), rows(t(a["L1_ffn_h1_w"]), HK),
                               rows(t(a["L1_ffn_h2_w"]), HK), rows(t(a["L1_ffn_w3_w"]), HK)], 1),
    }
    bd = np.zeros((HEADS, HD, HEADS, FEAT), f)
    for h in range(HEADS):
        bd[h, :, h, :] = a["L1_attn_proj"][h].T
    got["proj_bd"] = bd.reshape(P, HF)
    mask = np.zeros((P, VA), f)
    for h in range(4):
        mask[h * FEAT:h * FEAT + FEAT, h * HD:h * HD + HD] = 1.0
        mask[h * FEAT:h * FEAT + FEAT, 4 * HD + h] = 1.0
    got["featmask"] = mask
    return {k: np.ascontiguousarray(v) for k, v in got.items()}


def kernel(**inputs):
    import concourse.bacc as bacc
    from concourse.bass_utils import run_bass_kernel_spmd

    nc = bacc.Bacc("TRN2", target_bir_lowering=False, num_devices=1)
    arrays = {f"in_{k}": v for k, v in arrange({k: np.asarray(v) for k, v in inputs.items()}).items()}
    ins = {k[3:]: nc.dram_tensor(k, v.shape, F32, kind="ExternalInput").ap() for k, v in arrays.items()}
    out = nc.dram_tensor("out_0", (BATCHES * SEQ, D), F32, kind="ExternalOutput").ap()
    build(nc, ins, out)
    r = run_bass_kernel_spmd(nc, [arrays], core_ids=[0])
    return r.results[0]["out_0"].reshape(BATCHES, SEQ, D)
```

```python
from contextlib import ExitStack

import concourse.bass as bass
import concourse.mybir as mybir
import numpy as np

ALU = mybir.AluOpType
ACT = mybir.ActivationFunctionType
F32 = mybir.dt.float32
F32R = mybir.dt.float32r
AX_X = mybir.AxisListType.X

P = 128
BATCHES, SEQ, D = 8, 256, 128
TILES = BATCHES * SEQ // P
PER = SEQ // P
EXPERTS, SLOTS, FE = 16, 64, 256
NSLOT = EXPERTS * SLOTS
ST = NSLOT // P
OW = D + 2
HEADS, HD = 16, 8
FEAT = 32
HF = HEADS * FEAT
FG = HF // P
VA = P // FEAT * HD + P // FEAT
NORMS = SEQ + FG * VA
HID = 512
HK = HID // P
CHUNK = 512
CHUNKS = BATCHES * SEQ // CHUNK
LN_EPS = 1e-5
ATT_EPS = 1e-6
QK_SCALE = HD ** -0.5


LN_STEPS = {"m": 11, "a": 4}
MOE_TOTALS = dict(
    pool=BATCHES * LN_STEPS["m"], turned=BATCHES, kept=BATCHES, zthi=BATCHES, ztlo=BATCHES, rows=BATCHES * PER,
    copied=BATCHES * PER, maxn=BATCHES * PER, columns=BATCHES * 4, maxs=BATCHES * 4,
    zs=BATCHES * 4, lnz=BATCHES, shift=BATCHES * 3, spread=BATCHES, sub=BATCHES * PER,
    disp=BATCHES * PER, shifted=BATCHES * 4, comb=BATCHES * 4, slots=BATCHES, slots_a=BATCHES, slots_b=BATCHES,
    wgu0=EXPERTS // 2 * 16, wgu1=EXPERTS // 2 * 16, wd0=EXPERTS // 2 * 16, wd1=EXPERTS // 2 * 16, gate=EXPERTS * 2, up=EXPERTS * 2, gelu=EXPERTS * 2, h=EXPERTS * 2,
    whi=EXPERTS, wlo=EXPERTS, eshi=EXPERTS, eslo=EXPERTS,
    down=EXPERTS, eo=EXPERTS * 2, sums=ST, staged_a=BATCHES, staged_b=BATCHES, combined=BATCHES * PER,
    steps=BATCHES * 4, mom=BATCHES * 4)
FFN_TOTALS = dict(
    pool=BATCHES * LN_STEPS["a"], turned=BATCHES, zthi=CHUNKS, ztlo=CHUNKS, p1=CHUNKS * HK, p2=CHUNKS * HK,
    silu=CHUNKS * HK, mixed=CHUNKS * HK, mixhi=CHUNKS * HK, prod=2 * CHUNKS * HK, gelu=2 * CHUNKS * HK,
    gelhi=2 * CHUNKS * HK, lo=3 * CHUNKS * HK, p3=CHUNKS, yt=CHUNKS, yp=CHUNKS, added=CHUNKS, mom=BATCHES * 4)
TOTALS = {"m0": MOE_TOTALS, "m1": MOE_TOTALS, "f0": FFN_TOTALS, "f1": FFN_TOTALS}


def as32(ap):
    return ap.bitcast(F32)


def build(nc, ins, out, stages=("m0", "la", "m1", "f0", "fa", "f1")):
    ffns = [st for st in stages if st in ("f0", "f1")]
    before = dict(zip(stages, ("init",) + tuple(stages[:-1])))
    with ExitStack() as ctx:
        def sb(name, shape, dtype=F32, scope=ctx):
            return scope.enter_context(nc.sbuf_tensor(name, shape, dtype))

        sems = {}

        def sem(name):
            stage, _, what = name.partition("_")
            if stage in TOTALS and what != "x":
                name = f"{stage[0]}_{what}"
            if name not in sems:
                sems[name] = ctx.enter_context(nc.semaphore(name))
            return sems[name]

        def earlier(name):
            stage, _, what = name.partition("_")
            second = stage in ("m1", "f1") and stage[0] + "0" in stages and what != "x"
            return TOTALS[stage][what] if second else 0

        def plain(eng, value):
            if isinstance(value, int):
                return value
            count = eng.to_reg(value)
            eng.wait_ge(sem("pool_const" if eng is nc.gpsimd else "dve_const"), 1)
            return count

        def reached(name, value, eng=None):
            value = value + earlier(name)
            return sem(name), value if eng is None else plain(eng, value)

        def due(value):
            return not isinstance(value, int) or value > 0

        class Steps:
            def __init__(self, name, base=0):
                self.sem, self.n = sem(name), base + earlier(name)

            def step(self):
                self.n = self.n + 1
                return 1

        x = sb("x", [P, TILES, D])
        moments = sb("moments", [P, TILES, 2])
        ident = sb("ident", [P, P])
        ident_r = sb("ident_r", [P, P], F32R)
        half_power = sb("half_power", [P, 16])
        eps2 = sb("eps2", [P, PER])
        two = sb("two", [P, 2 * BATCHES])
        fresh = sb("fresh", [P, PER, 2])
        bn6 = sb("bn6", [P, 4, 6])
        rstd = sb("rstd", [P, 2, 8])
        z_in = sb("z_in", [P, 2, PER, D])
        bproj_bc = sb("bproj_bc", [P, D])
        bo_bc = sb("bo_bc", [P, D])
        headmask = sb("headmask", [P, D])
        featmask = sb("featmask", [P, VA])
        wqkv = sb("wqkv", [P, 3 * D])
        wproj = sb("wproj", [P, D])
        fw = sb("fw", [P, 4, D])
        proj_bd = sb("proj_bd", [P, HF])
        ffn_s = sb("ffn_s", [P, 4, HK])
        w3_s = sb("w3_s", [P, 2])

        moe = ExitStack()
        se_hi = sb("se_hi", [P, 2, NSLOT], F32R, moe)
        se_lo = sb("se_lo", [P, 2, NSLOT], F32R, moe)
        first_phase = ExitStack()
        zt_hi = sb("zt_hi", [P, 2, SEQ], F32R, first_phase)
        zt_lo = sb("zt_lo", [P, 2, SEQ], F32R, first_phase)
        junk = sb("junk", [P, 4, SEQ], F32, first_phase)
        first_phase.close()
        es_hi = sb("es_hi", [P, 2, CHUNK], F32R, moe)
        es_lo = sb("es_lo", [P, 2, CHUNK], F32R, moe)
        moe2 = ExitStack()
        expert_io = sb("expert_io", [P, ST + 1, BATCHES * OW], F32, moe2)
        bd_bc = sb("bd_bc", [P, EXPERTS, D], F32, moe2)
        wx = sb("wx", [P, 2, 3 * FE], F32, moe2)
        bgu = sb("bgu", [P, 2, EXPERTS, 2], F32, moe2)
        logits = sb("logits", [P, 2, PER, NSLOT], F32, moe2)
        wx_hi = sb("wx_hi", [P, 2, 2 * FE], F32R, moe2)
        wx_lo = sb("wx_lo", [P, 2, 2 * FE], F32R, moe2)
        negmax_n = sb("negmax_n", [P, 2, PER], F32R, moe2)
        negmax_s = sb("negmax_s", [P, 2, ST], F32, moe2)
        zsum_s = sb("zsum_s", [P, 2, ST], F32, moe2)
        lnz_s = sb("lnz_s", [P, 2, ST], F32, moe2)
        shift_s = sb("shift_s", [P, 2, ST], F32, moe2)
        shift_hi = sb("shift_hi", [P, 2, ST], F32R, moe2)
        shift_lo = sb("shift_lo", [P, 2, ST], F32R, moe2)
        z_slots = sb("z_slots", [P, 2, PER, D], F32, moe2)
        gate = sb("gate", [P, 2, CHUNK], F32, moe2)
        hmid = sb("hmid", [P, 2, 2, CHUNK], F32, moe2)
        affine = sb("affine", [P, 2, D], F32, moe2)
        cols = sb("cols", [P, 6], F32, moe2)
        zcol = sb("zcol", [P, 2, PER], F32, moe2)
        se_stat = sb("se_stat", [P, ST, 8], F32, moe2)
        se_r = sb("se_r", [P, 2, ST], F32, moe2)
        moe3 = ExitStack()
        comb = sb("comb", [P, BATCHES, ST, SEQ], F32, moe3)
        moe3.close()
        la = ExitStack()
        la_zt = sb("la_zt", [P, 2, SEQ], F32, la)
        la_min = sb("la_min", [P, 2, 2 * SEQ], F32, la)
        la_qk = sb("la_qk", [P, 2, 2 * SEQ], F32, la)
        la_v = sb("la_v", [P, 2, PER, D + 1], F32, la)
        la_kv = sb("la_kv", [P, 2, 2, D], F32, la)
        la_o = sb("la_o", [P, 2, 2, SEQ], F32, la)
        la.close()
        moe2.close()
        moe.close()

        l1 = ExitStack()
        ffw = sb("ffw", [P, 2 * HID + 2 * HK * HID + HK * D], F32, l1)
        pad = sb("pad", [P, 4 * NSLOT + 8 * SEQ - ffw.shape[1]], F32, l1)
        ffw_hi = sb("ffw_hi", ffw.shape, F32R, l1)
        ffw_lo = sb("ffw_lo", ffw.shape, F32R, l1)
        low_sum = sb("low_sum", [P, 2], F32, l1)
        split_w = sb("split_w", [1, 1], mybir.dt.int32, l1)
        W12 = 2 * HID
        H1 = W12 + HK * HID
        H2 = H1 + HK * HID
        ffn = ExitStack()
        fz_hi = sb("fz_hi", [P, 2, CHUNK], F32R, ffn)
        fz_lo = sb("fz_lo", [P, 2, CHUNK], F32R, ffn)
        even_hi = sb("even_hi", [P, 2, HK, CHUNK], F32R, ffn)
        even_lo = sb("even_lo", [P, 2, HK, CHUNK], F32R, ffn)
        odd_hi = sb("odd_hi", [P, 2, HK, CHUNK], F32R, ffn)
        odd_lo = sb("odd_lo", [P, 2, HK, CHUNK], F32R, ffn)
        whole = sb("whole", [P, HK, CHUNK], F32, ffn)
        silu_out = sb("silu_out", [P, 2, CHUNK], F32, ffn)
        y_t = sb("y_t", [P, 2, CHUNK], F32, ffn)
        ffn.close()
        fa = ExitStack()
        fa_zt = sb("fa_zt", [P, 2, SEQ], F32, fa)
        fa_qkt = sb("fa_qkt", [P, 2, 2, SEQ], F32, fa)
        fa_sq = sb("fa_sq", [P, 2, 2 * SEQ], F32, fa)
        fa_c = sb("fa_c", [P, 2, 2, 4 * HEADS], F32, fa)
        fa_phi = sb("fa_phi", [P, 2, 4, HF], F32, fa)
        fa_phit = sb("fa_phit", [P, 2, PER, FG, P], F32, fa)
        fa_vaug = sb("fa_vaug", [P, 2, PER, FG, VA], F32, fa)
        fa_kv = sb("fa_kv", [P, 2, FG, VA], F32, fa)
        fa_den = sb("fa_den", [P, 2, PER * HEADS], F32, fa)
        fa_o = sb("fa_o", [P, 2, PER, D], F32, fa)
        fa_ot = sb("fa_ot", [P, 2, SEQ], F32, fa)
        fa_y = sb("fa_y", [P, 2, PER, D], F32, fa)
        fa.close()
        l1.close()

        ps = ctx.enter_context(nc.psum_tensor("ps", [P, 8, 512], F32))
        block = ctx.enter_context(nc.Block())

        def batch(b):
            return bass.ds(b * PER, PER) if not isinstance(b, int) else slice(b * PER, b * PER + PER)

        def looped(eng, step, first, last):
            pairs = (last - first) // 2
            with eng.Fori(0, pairs) as it:
                step(it * 2 + first, it + (first // 2), 1)
                step(it * 2 + (first + 1), it + (first + 1) // 2, 0)

        def all_batches(eng, step):
            step(0, 0, 0)
            looped(eng, step, 1, BATCHES - 1)
            step(BATCHES - 1, (BATCHES - 1) // 2, 1)

        def store_slots(copy, j, p, k):
            for h in range(2):
                col = (h ^ p) * 512 + h * SLOTS
                dst = expert_io[:, 1 + 4 * k:5 + 4 * k, :]
                dst = dst[:, :, j * P + col:j * P + col + SLOTS] if isinstance(j, int) else dst[:, :, bass.ds(j * P + col, SLOTS)]
                last = copy(dst, ps[:, 6 + k, :].rearrange("p (t h s) -> p t h s", t=4, h=2)[:, :, h, :])
            return last


        @block.sync
        def _(sp):
            sp.dma_start(ident[:], ins["ident"]).then_inc(sem("ld_const"), 16)
            sp.dma_start(affine[:], ins["affine"].partition_broadcast(P)).then_inc(sem("ld_affine"), 16)
            for h in range(2):
                sp.dma_start(x[:, h * 8:h * 8 + 8, :],
                             ins["x"].rearrange("(t p) d -> p t d", p=P)[:, h * 8:h * 8 + 8, :]).then_inc(sem(f"ld_x{h}"), 16)
            sp.dma_start(logits[:, 1, 0, :].rearrange("p (t d) -> p t d", t=ST),
                         ins["slot_embeds"].rearrange("(t p) d -> p t d", p=P)).then_inc(sem("ld_se"), 16)
            sp.dma_start(cols[:, 0:3], ins["cols"]).then_inc(sem("ld_se"), 16)
            sp.dma_start(bgu[:].rearrange("p a b c -> p (a b c)"), ins["bgu"]).then_inc(sem("ld_w"), 16)
            sp.dma_start(bd_bc[:], ins["bd"].partition_broadcast(P)).then_inc(sem("ld_w"), 16)
            for dst, name in ((wqkv, "wqkv"), (wproj, "wproj"), (headmask, "headmask"), (featmask, "featmask"),
                              (proj_bd, "proj_bd"), (w3_s[:, 0:1], "w3_s")):
                sp.dma_start(dst[:] if dst is not w3_s else dst, ins[name]).then_inc(sem("ld_w"), 16)
            sp.dma_start(bproj_bc[:], ins["bproj"].partition_broadcast(P)).then_inc(sem("ld_w"), 16)
            sp.dma_start(bo_bc[:], ins["bo"].partition_broadcast(P)).then_inc(sem("ld_w"), 16)
            sp.dma_start(fw[:].rearrange("p a d -> p (a d)"), ins["fw"]).then_inc(sem("ld_w"), 16)
            sp.dma_start(ffn_s[:].rearrange("p a k -> p (a k)"), ins["ffn_s"]).then_inc(sem("ld_w"), 16)

            for st in stages:
                if st[0] == "m":
                    if st == "m1":
                        sp.wait_ge(*reached("m0_down", EXPERTS))
                    for p in range(2):
                        sp.dma_start(wx[:, p, 0:2 * FE], ins["wx"][p, :, 0:2 * FE]).then_inc(sem(f"{st}_wgu{p}"), 16)
                        sp.dma_start(wx[:, p, 2 * FE:], ins["wx"][p, :, 2 * FE:]).then_inc(sem(f"{st}_wd{p}"), 16)
                    sp.wait_ge(*reached(f"{st}_wlo", 1))
                    sp.dma_start(wx[:, 0, 0:2 * FE], ins["wx"][2, :, 0:2 * FE]).then_inc(sem(f"{st}_wgu0"), 16)
                    with sp.Fori(0, EXPERTS // 2 - 2) as t:
                        for p in range(2):
                            sp.wait_ge(*reached(f"{st}_wlo", t * 2 + (p + 2)))
                            sp.dma_start(wx[:, 1 - p, 0:2 * FE], ins["wx"][t * 2 + (p + 3), :, 0:2 * FE]).then_inc(sem(f"{st}_wgu{1 - p}"), 16)
                            sp.wait_ge(*reached(f"{st}_down", t * 2 + (p + 1)))
                            sp.dma_start(wx[:, p, 2 * FE:], ins["wx"][t * 2 + (p + 2), :, 2 * FE:]).then_inc(sem(f"{st}_wd{p}"), 16)
                    sp.wait_ge(*reached(f"{st}_wlo", EXPERTS - 2))
                    sp.dma_start(wx[:, 1, 0:2 * FE], ins["wx"][EXPERTS - 1, :, 0:2 * FE]).then_inc(sem(f"{st}_wgu1"), 16)
                    for p in range(2):
                        sp.wait_ge(*reached(f"{st}_down", EXPERTS - 3 + p))
                        sp.dma_start(wx[:, p, 2 * FE:], ins["wx"][EXPERTS - 2 + p, :, 2 * FE:]).then_inc(sem(f"{st}_wd{p}"), 16)
                if st == "f0":
                    if "m1" in stages:
                        sp.wait_ge(*reached("m1_down", EXPERTS))
                    sp.dma_start(ffw[:], ins["ffw"]).then_inc(sem("ld_ffw"), 16)
            last = stages[-1]
            view = out.rearrange("(t p) d -> p t d", p=P)
            for c in range(CHUNKS):
                sp.wait_ge(sem(f"{last}_x"), 2 * c + 2)
                sp.dma_start(view[:, 4 * c:4 * c + 4, :], x[:, 4 * c:4 * c + 4, :]).then_inc(sem("stored"), 16)
            sp.wait_ge(sem("stored"), 16 * CHUNKS)

        @block.gpsimd
        def _(pool):
            pool.memset(half_power[:], -0.5).then_inc(sem("pool_const"), 1)
            pool.memset(eps2[:], LN_EPS).then_inc(sem("pool_const"), 1)
            pool.wait_ge(sem("pool_const"), 2)

            def slot_scale():
                pool.wait_ge(sem("se_moments"), ST)
                go = Steps("se_scale")
                pool.tensor_scalar(se_r[:, 0, :], se_stat[:, :, 7], LN_EPS, None, ALU.add).then_inc(go.sem, go.step())
                pool.wait_ge(go.sem, go.n)
                pool.tensor_tensor(se_r[:, 1, :], se_r[:, 0, :], half_power[:, 0:ST], ALU.pow).then_inc(go.sem, go.step())

            def norm(st, b, p):
                moe_ln = st[0] == "m"
                key = "m" if moe_ln else "a"
                pool.wait_ge(*reached(f"{before[st]}_x", b + 1, pool))
                go = Steps(f"{st}_pool", b * LN_STEPS[key])
                var = moments[:, batch(b), 1]
                r = rstd[:, p, :]
                pool.tensor_tensor(r[:, 0:2], var, eps2[:], ALU.add).then_inc(go.sem, go.step())
                pool.wait_ge(go.sem, plain(pool, go.n))
                pool.tensor_tensor(r[:, 2:4], r[:, 0:2], half_power[:, 0:2], ALU.pow).then_inc(go.sem, go.step())
                pool.wait_ge(go.sem, plain(pool, go.n))
                scale = r[:, 2:4]
                if moe_ln:
                    pool.tensor_tensor(r[:, 4:6], scale, scale, ALU.mult).then_inc(go.sem, go.step())
                    pool.wait_ge(go.sem, plain(pool, go.n))
                    pool.tensor_tensor(r[:, 0:2], r[:, 4:6], var, ALU.mult).then_inc(go.sem, go.step())
                    pool.wait_ge(go.sem, plain(pool, go.n))
                    pool.tensor_scalar(r[:, 4:6], r[:, 0:2], LN_EPS, None, ALU.add).then_inc(go.sem, go.step())
                    pool.wait_ge(go.sem, plain(pool, go.n))
                    pool.tensor_tensor(r[:, 0:2], r[:, 4:6], half_power[:, 0:2], ALU.pow).then_inc(go.sem, go.step())
                    pool.wait_ge(go.sem, plain(pool, go.n))
                    pool.tensor_tensor(r[:, 6:8], r[:, 0:2], scale, ALU.mult).then_inc(go.sem, go.step())
                    pool.wait_ge(go.sem, plain(pool, go.n))
                    scale = r[:, 6:8]
                if due(b - 1):
                    pool.wait_ge(*reached(f"{st}_turned", b - 1, pool))
                if isinstance(b, int) and b == 0 and before[st] != "init":
                    pool.wait_ge(*reached(f"{before[st]}_turned", BATCHES, pool))
                pool.tensor_tensor(z_in[:, p], x[:, batch(b), :],
                                          moments[:, batch(b), 0:1].broadcast_to([P, PER, D]), ALU.subtract).then_inc(go.sem, go.step())
                pool.wait_ge(go.sem, plain(pool, go.n))
                pool.tensor_tensor(z_in[:, p], z_in[:, p], scale.unsqueeze(2).broadcast_to([P, PER, D]), ALU.mult).then_inc(go.sem, go.step())
                if moe_ln:
                    pool.wait_ge(go.sem, plain(pool, go.n))
                    pool.tensor_tensor(z_in[:, p], z_in[:, p],
                                              affine[:, 0:1, :].broadcast_to([P, PER, D]), ALU.mult).then_inc(go.sem, go.step())
                    pool.wait_ge(go.sem, plain(pool, go.n))
                    pool.tensor_tensor(z_in[:, p], z_in[:, p],
                                              affine[:, 1:2, :].broadcast_to([P, PER, D]), ALU.add).then_inc(go.sem, go.step())

            def moe_pool(st):
                def keep(b, p):
                    if due(b - 1):
                        pool.wait_ge(*reached(f"{st}_slots", b - 1, pool))
                    pool.wait_ge(*reached(f"{st}_pool", b * LN_STEPS["m"] + LN_STEPS["m"], pool))
                    pool.tensor_copy(z_slots[:, p], z_in[:, p]).then_inc(sem(f"{st}_kept"), 1)

                def slot_shifts(b, p):
                    if due(b - 1):
                        pool.wait_ge(*reached(f"{st}_spread", b - 1, pool))
                    pool.wait_ge(*reached(f"{st}_lnz", b + 1, pool))
                    go = Steps(f"{st}_shift", b * 3)
                    pool.tensor_tensor(shift_s[:, p], negmax_s[:, p, :], lnz_s[:, p, :], ALU.subtract).then_inc(go.sem, go.step())
                    pool.wait_ge(go.sem, plain(pool, go.n))
                    pool.tensor_copy(shift_hi[:, p], shift_s[:, p]).then_inc(go.sem, go.step())
                    pool.wait_ge(go.sem, plain(pool, go.n))
                    pool.tensor_tensor(shift_lo[:, p], shift_s[:, p], as32(shift_hi[:, p]), ALU.subtract).then_inc(go.sem, go.step())

                norm(st, 0, 0)
                if st == "m0":
                    slot_scale()
                keep(0, 0)
                norm(st, 1, 1)
                keep(1, 1)
                slot_shifts(0, 0)

                def step(b, j, p, ahead=True):
                    if ahead:
                        norm(st, b + 2, p)
                    if ahead or isinstance(b, int) and b < BATCHES - 1:
                        slot_shifts(b + 1, 1 - p)
                    if ahead:
                        keep(b + 2, p)

                step(0, 0, 0)
                looped(pool, step, 1, BATCHES - 3)
                step(BATCHES - 3, 2, 1)
                step(BATCHES - 2, 3, 0, False)

                def low_weights(e, p):
                    pool.wait_ge(*reached(f"{st}_whi", e + 1, pool))
                    pool.tensor_tensor(wx_lo[:, p, :], wx[:, p, 0:2 * FE], as32(wx_hi[:, p, :]), ALU.subtract).then_inc(sem(f"{st}_wlo"), 1)

                def low_slots(e, t, p):
                    src = expert_io[:, t + 1, p * CHUNK:p * CHUNK + CHUNK] if isinstance(t, int) else \
                        expert_io[:, bass.ds(t + 1, 1), p * CHUNK:p * CHUNK + CHUNK].rearrange("p a n -> p (a n)")
                    pool.wait_ge(*reached(f"{st}_eshi", e + 1, pool))
                    pool.tensor_tensor(es_lo[:, p, :], src, as32(es_hi[:, p, :]), ALU.subtract).then_inc(sem(f"{st}_eslo"), 1)

                low_weights(0, 0)
                low_weights(1, 1)
                low_slots(0, 0, 0)
                low_slots(1, 0, 1)
                with pool.Fori(1, ST) as t:
                    for p in range(2):
                        low_weights(t * 2 + p, p)
                        low_slots(t * 2 + p, t, p)

            for st in stages:
                if st[0] == "m":
                    pool.wait_ge(sem("ld_affine"), 16)
                    moe_pool(st)
                elif st in ("f0", "f1"):
                    for b in range(BATCHES):
                        if b == 4 and st == ffns[0]:
                            if before[st] != "init":
                                pool.wait_ge(sem(f"{before[st]}_x"), BATCHES)
                            pool.wait_ge(sem("ld_ffw"), 16)
                            for n, part in enumerate((slice(H1, H2), slice(H2, ffw.shape[1]))):
                                pool.tensor_scalar(ffw_hi[:, part], ffw[:, part], 1.0, None, ALU.mult).then_inc(sem("deep_w"), 1)
                                pool.wait_ge(sem("deep_w"), 2 * n + 1)
                                pool.tensor_tensor(ffw_lo[:, part], ffw[:, part], as32(ffw_hi[:, part]), ALU.subtract).then_inc(sem("deep_w"), 1)
                        norm(st, b, b % 2)
                else:
                    all_batches(pool, lambda b, j, p: norm(st, b, p))

        @block.tensor
        def _(pe):
            def turn(dst, src):
                return pe.transpose(dst, src, ident[:])

            def three(dst, a_hi, a_lo, b_hi, b_lo, start, stop):
                pe.matmul(dst, a_hi, b_lo, start=start, stop=False, skip_group_check=True)
                pe.matmul(dst, a_lo, b_hi, start=False, stop=False, skip_group_check=True)
                return pe.matmul(dst, a_hi, b_hi, start=False, stop=stop, skip_group_check=True)

            def turn_batch(st, b, p, bank, at=0):
                k = LN_STEPS["m" if st[0] == "m" else "a"]
                pe.wait_ge(*reached(f"{st}_pool", b * k + k))
                for i in range(PER):
                    mm = turn(ps[:, bank, at + i * P:at + i * P + P], z_in[:, p, i, :])
                mm.then_inc(sem(f"{st}_turned"), 1)

            def moe_tensor(st):
                def tokens(b, p):
                    if due(b * 2):
                        pe.wait_ge(*reached(f"{st}_copied", b * 2))
                    turn_batch(st, b, p, 4)

                def rows(b, p, i):
                    pe.wait_ge(*reached(f"{st}_zthi", b + 1))
                    pe.wait_ge(*reached(f"{st}_ztlo", b + 1))
                    if i == 0 and due(b - 1):
                        pe.wait_ge(*reached(f"{st}_slots_a", b - 1))
                        pe.wait_ge(*reached(f"{st}_slots_b", b - 1))
                    elif i == 1 and due(b * 2):
                        pe.wait_ge(*reached(f"{st}_sub", b * 2))
                    for h in range(2):
                        cut = slice(h * 512, h * 512 + 512)
                        mm = three(ps[:, (6, 4)[i] + h, :], zt_hi[:, p, i * P:i * P + P], zt_lo[:, p, i * P:i * P + P],
                                   se_hi[:, p, cut], se_lo[:, p, cut], True, True)
                    mm.then_inc(sem(f"{st}_rows"), 1)

                def columns(b, p, ks):
                    for k in ks:
                        if due((b - 1) * 4 + (k + 1)):
                            pe.wait_ge(*reached(f"{st}_comb", (b - 1) * 4 + (k + 1)))
                        for h in range(2):
                            t = 2 * k + h
                            cut = slice(t * P, t * P + P)
                            mm = three(ps[:, k, h * SEQ:h * SEQ + SEQ], se_hi[:, p, cut], se_lo[:, p, cut],
                                       zt_hi[:, p, :], zt_lo[:, p, :], h == 0, False)
                        mm.then_inc(sem(f"{st}_columns"), 1)

                def spread(b, p):
                    pe.wait_ge(*reached(f"{st}_shift", b * 3 + 3))
                    pe.wait_ge(*reached(f"{st}_ztlo", min(b + 2, BATCHES) if isinstance(b, int) else b + 2))
                    for t in range(ST):
                        dst = ps[:, 4 + t // 4, t % 4 * P:t % 4 * P + P]
                        pe.matmul(dst, shift_lo[:, p, t:t + 1].broadcast_to([P, P]), ident_r[:], start=True, stop=False)
                        mm = pe.matmul(dst, shift_hi[:, p, t:t + 1].broadcast_to([P, P]), ident_r[:], start=False, stop=True)
                    mm.then_inc(sem(f"{st}_spread"), 1)

                def shift(b, p):
                    pe.wait_ge(*reached(f"{st}_maxn", b * 2 + 2))
                    for k in range(4):
                        pe.wait_ge(*reached(f"{st}_zs", b * 4 + (k + 1)))
                        for i in range(PER):
                            mm = pe.matmul(ps[:, k, :].rearrange("p (h i n) -> p i h n", h=2, i=PER)[:, i],
                                           negmax_n[:, p, i:i + 1].broadcast_to([P, P]),
                                           ident_r[:].unsqueeze(1).broadcast_to([P, 2, P]),
                                           start=False, stop=i == PER - 1, skip_group_check=True)
                        mm.then_inc(sem(f"{st}_shifted"), 1)

                def slots(b, p):
                    if not (isinstance(b, int) and b == BATCHES - 1):
                        pe.wait_ge(*reached(f"{st}_copied", b * 2 + 3))
                    pe.wait_ge(*reached(f"{st}_disp", b * 2 + 2))
                    pe.wait_ge(*reached(f"{st}_kept", b + 1))
                    for h in range(2):
                        for i in range(PER):
                            mm = pe.matmul(ps[:, 6 + h, :], z_slots[:, p, i, :], logits[:, p, i, h * 512:h * 512 + 512],
                                           start=i == 0, stop=i == PER - 1)
                    mm.then_inc(sem(f"{st}_slots"), 1)

                tokens(0, 0)
                if st == "m0":
                    for t in range(ST):
                        pe.wait_ge(sem("se_norm"), t + 1)
                        turn(ps[:, t // 4, t % 4 * P:t % 4 * P + P], logits[:, 1, 0, t * D:t * D + D]).then_inc(sem("se_turned"), 1)
                    pe.wait_ge(sem("se_ready"), 2)
                    pe.wait_ge(sem("dve_const"), 1)
                rows(0, 0, 0)
                columns(0, 0, range(4))
                rows(0, 0, 1)
                tokens(1, 1)
                shift(0, 0)
                spread(0, 0)
                if st == "m0":
                    pe.wait_ge(sem("se_ready"), 6)

                def step(b, j, p, ahead=True, last=False):
                    if not last:
                        rows(b + 1, 1 - p, 0)
                        columns(b + 1, 1 - p, range(4))
                        rows(b + 1, 1 - p, 1)
                    slots(b, p)
                    if ahead:
                        tokens(b + 2, p)
                    if not last:
                        shift(b + 1, 1 - p)
                        spread(b + 1, 1 - p)

                step(0, 0, 0)
                looped(pe, step, 1, BATCHES - 3)
                step(BATCHES - 3, 2, 1)
                step(BATCHES - 2, 3, 0, False)
                step(BATCHES - 1, 3, 1, False, True)

                def up(e, t, p):
                    pe.wait_ge(*reached(f"{st}_wlo", e + 1))
                    pe.wait_ge(*reached(f"{st}_eslo", e + 1))
                    for which in range(2):
                        for f in range(2):
                            if due((e - 1) * 2 + (f + 1)):
                                pe.wait_ge(*reached(f"{st}_gelu" if which == 0 else f"{st}_h", (e - 1) * 2 + (f + 1)))
                            w = slice(which * FE + f * P, which * FE + f * P + P)
                            three(ps[:, 2 * which + f, :], wx_hi[:, p, w], wx_lo[:, p, w], es_hi[:, p, :], es_lo[:, p, :], True, True)\
                                .then_inc(sem(f"{st}_gate" if which == 0 else f"{st}_up"), 1)

                def down(e, t, p):
                    pe.wait_ge(*reached(f"{st}_wd{p}", (t + 1) * 16))
                    pe.wait_ge(*reached(f"{st}_h", e * 2 + 2))
                    if due((e - 1) * 2):
                        pe.wait_ge(*reached(f"{st}_eo", (e - 1) * 2))
                    for jj in range(BATCHES // 2):
                        for f in range(2):
                            mm = pe.matmul(ps[:, 4 + p, jj * P:jj * P + P], hmid[:, p, f, jj * P:jj * P + P],
                                           wx[:, p, 2 * FE + f * D:2 * FE + f * D + D], start=f == 0, stop=f == 1)
                    mm.then_inc(sem(f"{st}_down"), 1)

                pe.wait_ge(*reached(f"{st}_comb", BATCHES * 4))
                pe.wait_ge(*reached(f"{st}_slots_a", BATCHES))
                pe.wait_ge(*reached(f"{st}_slots_b", BATCHES))
                def pair(t):
                    up(t * 2 + 1, t, 1)
                    down(t * 2, t, 0)
                    up(t * 2 + 2, t + 1, 0)
                    down(t * 2 + 1, t, 1)

                up(0, 0, 0)
                pair(0)
                with pe.Fori(1, ST - 1) as t:
                    pair(t)
                up(EXPERTS - 1, ST - 1, 1)
                down(EXPERTS - 2, ST - 1, 0)
                down(EXPERTS - 1, ST - 1, 1)

                def combine(b, j, p):
                    pe.wait_ge(*reached(f"{st}_staged_a", b + 1))
                    pe.wait_ge(*reached(f"{st}_staged_b", b + 1))
                    if due(b - 1):
                        pe.wait_ge(*reached(f"{st}_x", b - 1))
                    for i in range(PER):
                        for t in range(ST):
                            w = logits[:, p].rearrange("p i (t n) -> p (i t) n", t=ST // PER)
                            mm = pe.matmul(ps[:, 2 * p + i, 0:OW - 1], w[:, t, i * P:i * P + P],
                                           expert_io[:, t, b * OW:b * OW + OW - 1] if isinstance(b, int) else
                                           expert_io[:, t, bass.ds(b * OW, OW - 1)],
                                           start=t == 0, stop=t == ST - 1)
                        mm.then_inc(sem(f"{st}_combined"), 1)

                pe.wait_ge(*reached(f"{st}_eo", EXPERTS * 2))
                pe.wait_ge(*reached(f"{st}_sums", ST))
                pe.wait_ge(*reached(f"{st}_gelu", EXPERTS * 2))
                all_batches(pe, combine)

            def linear_attention_tensor(st):
                def tokens(b, p):
                    turn_batch(st, b, p, 4 * p + 2)

                def first(b, p):
                    B = 4 * p
                    pe.wait_ge(*reached(f"{st}_zt", b + 1))
                    if due(b - 1):
                        pe.wait_ge(*reached(f"{st}_qk", b - 1))
                    pe.matmul(ps[:, B, 0:SEQ], wqkv[:, 0:D], la_zt[:, p, :], start=True, stop=True)
                    for i in range(PER):
                        mm = pe.matmul(ps[:, B, SEQ + i * P:SEQ + i * P + P], la_zt[:, p, i * P:i * P + P], wqkv[:, D:2 * D],
                                       start=True, stop=True)
                    mm.then_inc(sem(f"{st}_qkp"), 1)
                    if due(b - 1):
                        pe.wait_ge(*reached(f"{st}_kv", b * 2 - 2))
                    for i in range(PER):
                        mm = pe.matmul(ps[:, B + 1, i * P:i * P + P], la_zt[:, p, i * P:i * P + P], wqkv[:, 2 * D:3 * D],
                                       start=True, stop=True)
                    mm.then_inc(sem(f"{st}_vp"), 1)

                def sums(b, p):
                    B = 4 * p
                    pe.wait_ge(*reached(f"{st}_v", b + 1))
                    pe.wait_ge(*reached(f"{st}_qk", b + 1))
                    for i in range(PER):
                        mm = pe.matmul(ps[:, B + 1, SEQ:SEQ + D + 1], la_qk[:, p, SEQ + i * P:SEQ + i * P + P],
                                       la_v[:, p, i, :], start=i == 0, stop=i == PER - 1)
                    mm.then_inc(sem(f"{st}_kvp"), 1)

                def outputs(b, p):
                    pe.wait_ge(*reached(f"{st}_kv", b * 2 + 2))
                    if due(b * 3 - 3):
                        pe.wait_ge(*reached(f"{st}_steps", b * 3 - 3))
                    for k in range(2):
                        mm = pe.matmul(ps[:, 4 * p + 3, k * SEQ:k * SEQ + SEQ], la_kv[:, p, k, :], la_qk[:, p, 0:SEQ],
                                       start=True, stop=True)
                    mm.then_inc(sem(f"{st}_op"), 1)

                def project(b, p):
                    pe.wait_ge(*reached(f"{st}_steps", b * 3 + 3))
                    for i in range(PER):
                        mm = pe.matmul(ps[:, 4 * p + 2, SEQ + i * P:SEQ + i * P + P], la_o[:, p, 0, i * P:i * P + P], wproj[:],
                                       start=True, stop=True)
                    mm.then_inc(sem(f"{st}_yp"), 1)

                def step(b, j, p):
                    more = not (isinstance(b, int) and b == BATCHES - 1)
                    if more:
                        tokens(b + 1, 1 - p)
                    sums(b, p)
                    if more:
                        first(b + 1, 1 - p)
                    if due(b):
                        project(b - 1, 1 - p)
                    outputs(b, p)

                tokens(0, 0)
                first(0, 0)
                all_batches(pe, step)
                project(BATCHES - 1, 1)

            def ffn_tensor(st):
                def tokens(c, q):
                    if due(c - 1):
                        pe.wait_ge(*reached(f"{st}_gelu", c // 2 * 4 * HK - HK))
                    turn_batch(st, 2 * c, 0, 6 + q)
                    turn_batch(st, 2 * c + 1, 1, 6 + q, SEQ)

                def gated(c, q, os):
                    pe.wait_ge(*reached(f"{st}_ztlo", c + 1))
                    if c < 2:
                        pe.wait_ge(sem("first_w_lo"), 1)
                    for o in os:
                        r = o % 2
                        for which in range(2):
                            n = c * HK + o
                            if q == 0 and o < 2 and c > 0:
                                pe.wait_ge(*reached(f"{st}_gelu", c * 2 * HK))
                            elif n >= 2:
                                pe.wait_ge(*reached(f"{st}_silu" if which == 0 else f"{st}_mixed", n - 1))
                            w = slice(which * HID + o * P, which * HID + o * P + P)
                            three(ps[:, 2 * r + which, :], ffw_hi[:, w], ffw_lo[:, w], fz_hi[:, q, :], fz_lo[:, q, :], True, True)\
                                .then_inc(sem(f"{st}_p1" if which == 0 else f"{st}_p2"), 1)

                def deep(dst, w0, width, o, hi, lo, whole_w):
                    for k in range(HK):
                        w = slice(w0 + k * width + o * P, w0 + k * width + o * P + P)
                        if whole_w:
                            pe.matmul(dst, ffw_hi[:, w], lo[:, k, :], start=k == 0, stop=False)
                            mm = pe.matmul(dst, ffw_hi[:, w], hi[:, k, :], start=False, stop=k == HK - 1)
                        else:
                            mm = three(dst, ffw_hi[:, w], ffw_lo[:, w], hi[:, k, :], lo[:, k, :], k == 0, k == HK - 1)
                    return mm

                def either_way(products):
                    with pe.If(low_parts != 0):
                        products(False)
                    with pe.If(low_parts == 0):
                        products(True)

                def hidden(j, layer, q, whole_w):
                    pe.wait_ge(*reached(f"{st}_lo", ((j * 3 + layer - 1) * 2 + q) * HK + HK))
                    hi, lo = ((even_hi, even_lo), (odd_hi, odd_lo))[layer - 1]
                    for o in range(HK):
                        if layer == 1 and q == 0 and j > 0:
                            pe.wait_ge(*reached(f"{st}_yt", 2 * j))
                            pe.wait_ge(*reached(f"{st}_added", 2 * j))
                        elif layer == 1 and q == 0:
                            pe.wait_ge(*reached(f"{st}_ztlo", 2))
                        elif layer == 1:
                            pe.wait_ge(*reached(f"{st}_mixed", (j * 2 + 2) * HK))
                        else:
                            pe.wait_ge(*reached(f"{st}_gelu", (j * 4 + q) * HK + o + 1))
                        deep(ps[:, (4, 0)[q] + o, :], (W12, H1)[layer - 1], HID, o, hi[:, q], lo[:, q], whole_w).then_inc(sem(f"{st}_prod"), 1)

                def last_product(c, q, whole_w):
                    pe.wait_ge(*reached(f"{st}_lo", ((c // 2 * 3 + 2) * 2 + q) * HK + HK))
                    deep(ps[:, 4 + q, :], H2, D, 0, even_hi[:, q], even_lo[:, q], whole_w).then_inc(sem(f"{st}_p3"), 1)

                def turn_back(c, q):
                    pe.wait_ge(*reached(f"{st}_yt", c + 1))
                    if c < CHUNKS - 2:
                        pe.wait_ge(*reached(f"{st}_ztlo", c + 3))
                    for i in range(CHUNK // P):
                        mm = turn(ps[:, 6 + q, i * P:i * P + P], y_t[:, q, i * P:i * P + P])
                    mm.then_inc(sem(f"{st}_yp"), 1)

                def last_pair(c, whole_w):
                    last_product(c, 0, whole_w)
                    last_product(c + 1, 1, whole_w)

                def hidden_pair(j, layer, whole_w):
                    hidden(j, layer, 0, whole_w)
                    hidden(j, layer, 1, whole_w)

                first = st == ffns[0]
                if not first:
                    low_parts = pe.value_load(split_w[:], min_val=0, max_val=1)
                for j in range(CHUNKS // 2 + 1):
                    c = 2 * j
                    if c < CHUNKS:
                        tokens(c, 0)
                    if j > 0:
                        either_way(lambda whole_w: last_pair(c - 2, whole_w))
                    if c < CHUNKS:
                        gated(c, 0, (0, 1))
                        tokens(c + 1, 1)
                        gated(c, 0, (2, 3))
                    if j > 0:
                        turn_back(c - 2, 0)
                        turn_back(c - 1, 1)
                    if c < CHUNKS:
                        gated(c + 1, 1, range(HK))
                        if j == 0 and first:
                            pe.wait_ge(sem("first_w_lo"), 2)
                            hidden_pair(0, 1, False)
                            pe.wait_ge(sem("low_sum"), 1)
                            pe.wait_ge(*reached(f"{st}_gelu", HK + 1))
                            turn(ps[0:1, 0, 0:P], low_sum[:, 0:1]).then_inc(sem("low_turned"), 1)
                            pe.wait_ge(sem("deep_w"), 4)
                            hidden(0, 2, 0, False)
                            pe.wait_ge(sem("low_known"), 1)
                            low_parts = pe.value_load(split_w[:], min_val=0, max_val=1)
                            either_way(lambda whole_w: hidden(0, 2, 1, whole_w))
                        else:
                            either_way(lambda whole_w: hidden_pair(j, 1, whole_w))
                            either_way(lambda whole_w: hidden_pair(j, 2, whole_w))

            def favor_tensor(st):
                def tokens(b, p):
                    turn_batch(st, b, p, 1)

                def queries(b, p):
                    pe.wait_ge(*reached(f"{st}_zt", b + 1))
                    for k in range(2):
                        mm = pe.matmul(ps[:, 1, k * SEQ:k * SEQ + SEQ], fw[:, k, :], fa_zt[:, p, :], start=True, stop=True)
                    mm.then_inc(sem(f"{st}_qktp"), 1)

                def values(b, p):
                    for i in range(PER):
                        mm = pe.matmul(ps[:, 3, i * P:i * P + P], fa_zt[:, p, i * P:i * P + P], fw[:, 2, :], start=True, stop=True)
                    mm.then_inc(sem(f"{st}_vp"), 1)

                def products(b, p):
                    pe.wait_ge(*reached(f"{st}_qkt", b + 1))
                    for n, a in enumerate((2, 3, 0, 1)):
                        if due((b - 1) * 4 + n + 1):
                            pe.wait_ge(*reached(f"{st}_sub", (b - 1) * 4 + (n + 1)))
                        pe.matmul(ps[:, 4 + a, :], fa_qkt[:, p, a // 2, a % 2 * P:a % 2 * P + P], proj_bd[:], start=True, stop=True)\
                            .then_inc(sem(f"{st}_xw"), 1)
                    pe.wait_ge(*reached(f"{st}_sq", b + 1))
                    pe.wait_ge(*reached(f"{st}_v", b + 1))
                    if due(b * 5):
                        pe.wait_ge(*reached(f"{st}_maxs", b * 5))
                    for a in range(4):
                        mm = pe.matmul(ps[:, 3, NORMS + a * HEADS:NORMS + a * HEADS + HEADS], fa_sq[:, p, a * P:a * P + P],
                                       headmask[:].rearrange("p (h d) -> p h d", d=HD)[:, :, 0], start=True, stop=True)
                    mm.then_inc(sem(f"{st}_norms"), 1)

                def sums(b, p):
                    pe.wait_ge(*reached(f"{st}_phi", b * 2 + 1))
                    for g in range(FG):
                        for i in range(PER):
                            mm = pe.matmul(ps[:, 3, SEQ + g * VA:SEQ + g * VA + VA], fa_phi[:, p, 2 + i, g * P:g * P + P],
                                           fa_vaug[:, p, i, g, :], start=i == 0, stop=i == PER - 1)
                    mm.then_inc(sem(f"{st}_kvp"), 1)
                    pe.wait_ge(*reached(f"{st}_phi", b * 2 + 2))
                    if due(b):
                        pe.wait_ge(*reached(f"{st}_yout", b))
                    for i in range(PER):
                        for g in range(FG):
                            mm = turn(ps[:, i, g * P:g * P + P], fa_phi[:, p, i, g * P:g * P + P])
                        mm.then_inc(sem(f"{st}_phitp"), 1)
                    pe.wait_ge(*reached(f"{st}_kv", b + 1))
                    for i in range(PER):
                        pe.wait_ge(*reached(f"{st}_phit", b * 2 + (i + 1)))
                        for g in range(FG):
                            mm = pe.matmul(ps[:, 2, i * SEQ + g * VA:i * SEQ + g * VA + VA], fa_phit[:, p, i, g, :], fa_kv[:, p, g, :],
                                           start=True, stop=True)
                    mm.then_inc(sem(f"{st}_np"), 1)

                def outputs(b, p):
                    pe.wait_ge(*reached(f"{st}_o", b + 1))
                    for i in range(PER):
                        mm = turn(ps[:, 0, i * P:i * P + P], fa_o[:, p, i, :])
                    mm.then_inc(sem(f"{st}_otp"), 1)

                def project(b, p):
                    pe.wait_ge(*reached(f"{st}_ot", b + 1))
                    for i in range(PER):
                        mm = pe.matmul(ps[:, 0, SEQ + i * P:SEQ + i * P + P], fa_ot[:, p, i * P:i * P + P], fw[:, 3, :], start=True, stop=True)
                    mm.then_inc(sem(f"{st}_yp"), 1)

                def step(b, j, p, ahead=True, last=False):
                    if not last:
                        products(b + 1, 1 - p)
                    sums(b, p)
                    if ahead:
                        tokens(b + 2, p)
                        queries(b + 2, p)
                    outputs(b, p)
                    if ahead:
                        values(b + 2, p)
                    project(b, p)

                tokens(0, 0)
                queries(0, 0)
                values(0, 0)
                products(0, 0)
                tokens(1, 1)
                queries(1, 1)
                values(1, 1)
                step(0, 0, 0)
                looped(pe, step, 1, BATCHES - 3)
                step(BATCHES - 3, 2, 1)
                step(BATCHES - 2, 3, 0, False)
                step(BATCHES - 1, 3, 1, False, True)

            pe.wait_ge(sem("ld_const"), 16)
            for st in stages:
                if before[st] != "init":
                    pe.wait_ge(sem(f"{before[st]}_x"), BATCHES)
                if st == "la" or before[st] == "init" and st != "m0":
                    pe.wait_ge(sem("ld_w"), 16 * 12)
                {"m": moe_tensor, "l": linear_attention_tensor, "f": ffn_tensor}[st[0]](st) if st != "fa" else favor_tensor(st)

        @block.scalar
        def _(act):
            def moe_scalar(st):
                def tokens(b, p):
                    act.wait_ge(*reached(f"{st}_turned", b + 1))
                    act.copy(zt_hi[:, p, :], ps[:, 4, 0:SEQ]).then_inc(sem(f"{st}_zthi"), 1)

                def copies(b, p, i):
                    if i == 0 and due(b - 1):
                        act.wait_ge(*reached(f"{st}_slots", b - 1))
                    act.wait_ge(*reached(f"{st}_rows", b * 2 + (i + 1)))
                    act.copy(logits[:, p, i, :], ps[:, 6 - 2 * i:8 - 2 * i, :].rearrange("p h n -> p (h n)"))\
                        .then_inc(sem(f"{st}_copied"), 1)

                def sums(b, p, ks):
                    for k in ks:
                        act.wait_ge(*reached(f"{st}_maxs", b * 4 + (k + 1)))
                        if due(b * 4 + (k - 1)):
                            act.wait_ge(*reached(f"{st}_zs", b * 4 + (k - 1)))
                        for h in range(2):
                            t = 2 * k + h
                            last = act.activation(junk[:, 2 * (k % 2) + h, :], ps[:, k, h * SEQ:h * SEQ + SEQ], ACT.Exp,
                                                  bias=negmax_s[:, p, t:t + 1], accum_out=zsum_s[:, p, t:t + 1])
                        last.then_inc(sem(f"{st}_zs"), 1)

                def logs(b, p):
                    act.wait_ge(*reached(f"{st}_zs", b * 4 + 4))
                    act.activation(lnz_s[:, p, :], zsum_s[:, p, :], ACT.Ln).then_inc(sem(f"{st}_lnz"), 1)

                def dispatch(b, p):
                    for i in range(PER):
                        act.wait_ge(*reached(f"{st}_sub", b * 2 + (i + 1)))
                        act.activation(logits[:, p, i, :], logits[:, p, i, :], ACT.Exp).then_inc(sem(f"{st}_disp"), 1)

                def weights(b, p):
                    for k in range(4):
                        act.wait_ge(*reached(f"{st}_shifted", b * 4 + (k + 1)))
                        dst = comb[:, b, 2 * k:2 * k + 2, :] if isinstance(b, int) else comb[:, bass.ds(b, 1), 2 * k:2 * k + 2, :].rearrange("p a t n -> p (a t) n")
                        act.activation(dst, ps[:, k, :].rearrange("p (t n) -> p t n", t=2), ACT.Exp).then_inc(sem(f"{st}_comb"), 1)

                def slots_out(b, j, p):
                    act.wait_ge(*reached(f"{st}_slots", b + 1))
                    store_slots(act.copy, j, p, 0).then_inc(sem(f"{st}_slots_a"), 1)

                def weights_of(e, t, p):
                    act.wait_ge(*reached(f"{st}_wgu{p}", (t + 1) * 16))
                    if due(e * 2 - 2):
                        act.wait_ge(*reached(f"{st}_up", e * 2 - 2))
                    act.copy(wx_hi[:, p, :], wx[:, p, 0:2 * FE]).then_inc(sem(f"{st}_whi"), 1)

                def slots_of(e, t, p):
                    src = expert_io[:, t + 1, p * CHUNK:p * CHUNK + CHUNK] if isinstance(t, int) else \
                        expert_io[:, bass.ds(t + 1, 1), p * CHUNK:p * CHUNK + CHUNK].rearrange("p a n -> p (a n)")
                    act.copy(es_hi[:, p, :], src).then_inc(sem(f"{st}_eshi"), 1)

                act.preload_act_table_set("natural_log_exp_and_others")
                tokens(0, 0)
                if st == "m0":
                    act.wait_ge(sem("se_ready"), 6)
                copies(0, 0, 0)
                sums(0, 0, (0, 1))
                copies(0, 0, 1)
                sums(0, 0, (2, 3))
                logs(0, 0)
                tokens(1, 1)
                weights(0, 0)

                def step(b, j, p, ahead=True, last=False):
                    if not last:
                        copies(b + 1, 1 - p, 0)
                    dispatch(b, p)
                    if last:
                        act.preload_act_table(ACT.Gelu)
                    if not last:
                        sums(b + 1, 1 - p, (0, 1))
                        copies(b + 1, 1 - p, 1)
                        sums(b + 1, 1 - p, (2, 3))
                        logs(b + 1, 1 - p)
                    if ahead:
                        tokens(b + 2, p)
                    slots_out(b, j, p)
                    if not last:
                        weights(b + 1, 1 - p)

                step(0, 0, 0)
                looped(act, step, 1, BATCHES - 3)
                step(BATCHES - 3, 2, 1)
                step(BATCHES - 2, 3, 0, False)
                weights_of(0, 0, 0)
                weights_of(1, 0, 1)
                step(BATCHES - 1, 3, 1, False, True)

                def gelus(e, p):
                    for f in range(2):
                        act.wait_ge(*reached(f"{st}_gate", e * 2 + (f + 1)))
                        if due((e - 1) * 2 + (f + 1)):
                            act.wait_ge(*reached(f"{st}_h", (e - 1) * 2 + (f + 1)))
                        bias = bgu[:, 0, e, f:f + 1] if isinstance(e, int) else bgu[:, 0, bass.ds(e, 1), f]
                        act.activation(gate[:, f, :], ps[:, f, :], ACT.Gelu, bias=bias).then_inc(sem(f"{st}_gelu"), 1)

                def expert(e, t, p, ahead=True):
                    gelus(e, p)
                    if ahead:
                        weights_of(e + 2, t + 1, p)
                        slots_of(e + 2, t + 1, p)

                act.wait_ge(sem("ld_w"), 16 * 12)
                act.wait_ge(*reached(f"{st}_slots_b", BATCHES))
                act.wait_ge(*reached(f"{st}_slots_a", BATCHES))
                slots_of(0, 0, 0)
                slots_of(1, 0, 1)
                expert(0, 0, 0)
                expert(1, 0, 1)
                with act.Fori(1, ST - 1) as t:
                    expert(t * 2, t, 0)
                    expert(t * 2 + 1, t, 1)
                expert(EXPERTS - 2, ST - 1, 0, False)
                expert(EXPERTS - 1, ST - 1, 1, False)

                def stage(b, j, p):
                    if due((b - 1) * 2):
                        act.wait_ge(*reached(f"{st}_combined", (b - 1) * 2))
                    src = comb[:, b, 0:ST // 2, :] if isinstance(b, int) else comb[:, bass.ds(b, 1), 0:ST // 2, :].rearrange("p a t n -> p (a t) n")
                    act.copy(logits[:, p, 0, :].rearrange("p (t n) -> p t n", t=ST // 2), src).then_inc(sem(f"{st}_staged_a"), 1)

                all_batches(act, stage)

            def linear_attention_scalar(st):
                def first(b, p):
                    B = 4 * p
                    act.wait_ge(*reached(f"{st}_turned", b + 1))
                    act.copy(la_zt[:, p, :], ps[:, B + 2, 0:SEQ]).then_inc(sem(f"{st}_zt"), 1)
                    act.wait_ge(*reached(f"{st}_vp", b + 1))
                    act.copy(la_v[:, p, :, 0:D], ps[:, B + 1, 0:SEQ].rearrange("p (i d) -> p i d", i=PER)).then_inc(sem(f"{st}_v"), 1)
                    act.wait_ge(*reached(f"{st}_min", b + 1))
                    act.activation(la_min[:, p, :], la_min[:, p, :], ACT.Exp).then_inc(sem(f"{st}_exp"), 1)
                act.wait_ge(*reached(f"{st}_vones", 1))
                all_batches(act, lambda b, j, p: first(b, p))

            def ffn_scalar(st):
                def tokens(c, q):
                    act.wait_ge(*reached(f"{st}_turned", 2 * c + 2))
                    act.copy(fz_hi[:, q, :], ps[:, 6 + q, :]).then_inc(sem(f"{st}_zthi"), 1)

                def silus(c, q, os):
                    for o in os:
                        n = c * HK + o
                        act.wait_ge(*reached(f"{st}_p1", n + 1))
                        if n >= 2:
                            act.wait_ge(*reached(f"{st}_mixed", n - 1))
                        act.activation(silu_out[:, o % 2, :], ps[:, 2 * (o % 2), :], ACT.Silu, scale=ffn_s[:, 0, o:o + 1])\
                            .then_inc(sem(f"{st}_silu"), 1)
                        if n % (2 * HK) >= 1:
                            high(n - 1)
                def high(n):
                    c, o = n // HK, n % HK
                    act.wait_ge(*reached(f"{st}_mixed", n + 1))
                    act.copy(even_hi[:, c % 2, o, :], whole[:, o, :]).then_inc(sem(f"{st}_mixhi"), 1)

                def gelus(j, layer, q):
                    for o in range(HK):
                        n = (j * 4 + (layer - 1) * 2 + q) * HK + o
                        act.wait_ge(*reached(f"{st}_prod", n + 1))
                        act.wait_ge(*reached(f"{st}_lo", ((j * 3 + layer) * 2 + q - 1) * HK + o + 1))
                        act.activation(whole[:, o, :], ps[:, (4, 0)[q] + o, :], ACT.Gelu, scale=ffn_s[:, 1 + layer, o:o + 1])\
                            .then_inc(sem(f"{st}_gelu"), 1)

                def scaled(c, q):
                    act.wait_ge(*reached(f"{st}_p3", c + 1))
                    if c >= 2:
                        act.wait_ge(*reached(f"{st}_yp", c - 1))
                    act.mul(y_t[:, q, :], ps[:, 4 + q, :], w3_s[:, 1:2]).then_inc(sem(f"{st}_yt"), 1)

                if st == ffns[0]:
                    act.wait_ge(sem("ld_ffw"), 16)
                    for part in (slice(0, W12), slice(W12, H1)):
                        act.copy(ffw_hi[:, part], ffw[:, part]).then_inc(sem("first_w_hi"), 1)
                for j in range(CHUNKS // 2 + 1):
                    c = 2 * j
                    if c < CHUNKS:
                        tokens(c, 0)
                    if j > 0:
                        scaled(c - 2, 0)
                        scaled(c - 1, 1)
                    if c < CHUNKS:
                        silus(c, 0, (0, 1))
                        tokens(c + 1, 1)
                        silus(c, 0, (2, 3))
                        silus(c + 1, 1, range(HK))
                        high((c + 2) * HK - 1)
                        gelus(j, 1, 0)
                        if j == 0 and st == ffns[0]:
                            act.wait_ge(sem("deep_w"), 4)
                            act.wait_ge(sem("first_w_lo"), 2)
                            act.activation(ffw[:, W12:], as32(ffw_lo[:, W12:]), ACT.Abs, accum_out=low_sum[:, 0:1]).then_inc(sem("low_sum"), 1)
                        gelus(j, 1, 1)
                        gelus(j, 2, 0)
                        gelus(j, 2, 1)

            def favor_scalar(st):
                def tokens(b, p):
                    act.wait_ge(*reached(f"{st}_turned", b + 1))
                    act.copy(fa_zt[:, p, :], ps[:, 1, 0:SEQ]).then_inc(sem(f"{st}_zt"), 1)
                    act.wait_ge(*reached(f"{st}_qktp", b + 1))
                    act.mul(fa_qkt[:, p].rearrange("p k n -> p (k n)"), ps[:, 1, :], QK_SCALE).then_inc(sem(f"{st}_qkt"), 1)

                def values(b, p):
                    act.activation(fa_sq[:, p, :], ps[:, 1, :], ACT.Square, scale=QK_SCALE * 0.5 ** 0.5).then_inc(sem(f"{st}_sq"), 1)
                    act.wait_ge(*reached(f"{st}_vp", b + 1))
                    act.copy(fa_vaug[:, p, :, :, 0:VA - 4], ps[:, 3, 0:SEQ].rearrange("p (i g d) -> p i g d", i=PER, g=FG))\
                        .then_inc(sem(f"{st}_v"), 1)

                def exponentials(b, p, n):
                    act.wait_ge(*reached(f"{st}_sub", b * 4 + (2 * n + 2)))
                    phi = fa_phi[:, p, 2 - 2 * n:4 - 2 * n].rearrange("p a f -> p (a f)")
                    act.activation(phi, phi, ACT.Exp).then_inc(sem(f"{st}_exp"), 1)

                def turned(b, p):
                    for i in range(PER):
                        act.wait_ge(*reached(f"{st}_phitp", b * 2 + (i + 1)))
                        act.copy(fa_phit[:, p, i].rearrange("p g n -> p (g n)"), ps[:, i, :]).then_inc(sem(f"{st}_phit"), 1)

                def outputs(b, p):
                    act.wait_ge(*reached(f"{st}_otp", b + 1))
                    act.copy(fa_ot[:, p, :], ps[:, 0, 0:SEQ]).then_inc(sem(f"{st}_ot"), 1)

                def step(b, j, p, ahead=True, last=False):
                    turned(b, p)
                    if not last:
                        exponentials(b + 1, 1 - p, 0)
                    if ahead:
                        tokens(b + 2, p)
                    outputs(b, p)
                    if ahead:
                        values(b + 2, p)
                    if not last:
                        exponentials(b + 1, 1 - p, 1)

                act.wait_ge(*reached(f"{st}_vones", 1))
                tokens(0, 0)
                values(0, 0)
                exponentials(0, 0, 0)
                exponentials(0, 0, 1)
                tokens(1, 1)
                values(1, 1)
                step(0, 0, 0)
                looped(act, step, 1, BATCHES - 3)
                step(BATCHES - 3, 2, 1)
                step(BATCHES - 2, 3, 0, False)
                step(BATCHES - 1, 3, 1, False, True)

            for st in stages:
                if before[st] != "init":
                    act.wait_ge(sem(f"{before[st]}_x"), BATCHES)
                if before[st] == "init" and st != "m0":
                    act.wait_ge(sem("ld_w"), 16 * 12)
                {"m": moe_scalar, "l": linear_attention_scalar, "f": ffn_scalar}[st[0]](st) if st != "fa" else favor_scalar(st)

        @block.vector
        def _(dve):
            def after(st, b):
                go = Steps(f"{st}_mom", b * 4)
                if due(b):
                    dve.wait_ge(*reached(f"{st}_x", b, dve))
                for i in range(PER):
                    src = x[:, b * PER + i, :] if isinstance(b, int) else x[:, bass.ds(b * PER + i, 1), :].rearrange("p a d -> p (a d)")
                    dve.bn_stats(bn6[:, i, :], src).then_inc(go.sem, go.step())
                dve.wait_ge(go.sem, plain(dve, go.n))
                for i in range(PER):
                    dve.bn_aggr(fresh[:, i, :], bn6[:, i, :]).then_inc(go.sem, go.step())
                dve.wait_ge(go.sem, plain(dve, go.n))
                dve.tensor_copy(moments[:, batch(b), :], fresh[:]).then_inc(sem(f"{st}_x"), 1)

            def moments_of(bs):
                for b in bs:
                    if b % 4 == 0:
                        dve.wait_ge(sem(f"ld_x{b // 4}"), 16)
                    after("init", b)

            def moe_vector(st):
                def tokens(b, p):
                    dve.wait_ge(*reached(f"{st}_zthi", b + 1))
                    dve.tensor_tensor(zt_lo[:, p, :], ps[:, 4, 0:SEQ], as32(zt_hi[:, p, :]), ALU.subtract)\
                        .then_inc(sem(f"{st}_ztlo"), 1)

                def max_n(b, p, i):
                    if i == 0 and due(b * 4 - 4):
                        dve.wait_ge(*reached(f"{st}_shifted", b * 4 - 4))
                    dve.wait_ge(*reached(f"{st}_copied", b * 2 + (i + 1)))
                    dve.tensor_reduce(negmax_n[:, p, i:i + 1], logits[:, p, i, :], AX_X, ALU.max, negate=True)\
                        .then_inc(sem(f"{st}_maxn"), 1)

                def max_s(b, p, ks):
                    for k in ks:
                        dve.wait_ge(*reached(f"{st}_columns", b * 4 + (k + 1)))
                        dve.tensor_reduce(negmax_s[:, p, 2 * k:2 * k + 2], ps[:, k, :].rearrange("p (t n) -> p t n", t=2),
                                          AX_X, ALU.max, negate=True).then_inc(sem(f"{st}_maxs"), 1)

                def subtract(b, p):
                    dve.wait_ge(*reached(f"{st}_spread", b + 1))
                    for i in range(PER):
                        dve.tensor_tensor(logits[:, p, i, :], logits[:, p, i, :],
                                          ps[:, 4:6, :].rearrange("p h n -> p (h n)"), ALU.add).then_inc(sem(f"{st}_sub"), 1)

                def slots_out(b, j, p):
                    dve.wait_ge(*reached(f"{st}_slots", b + 1))
                    store_slots(dve.tensor_copy, j, p, 1).then_inc(sem(f"{st}_slots_b"), 1)

                def swapped_slots():
                    pairs = logits[:, 0, 0, :].rearrange("p (t h s) -> p t h s", t=ST, h=2)
                    swapped = [t[:, 1, :].rearrange("p (t h s) -> p t h s", t=ST, h=2) for t in (se_hi, se_lo)]
                    for h in range(2):
                        dve.tensor_copy(swapped[0][:, :, 1 - h, :], pairs[:, :, h, :]).then_inc(sem("se_ready"), 1)
                    dve.wait_ge(sem("se_ready"), 4)
                    for h in range(2):
                        dve.tensor_tensor(swapped[1][:, :, 1 - h, :], pairs[:, :, h, :],
                                          as32(swapped[0][:, :, 1 - h, :]), ALU.subtract).then_inc(sem("se_ready"), 1)
                    dve.wait_ge(sem("se_ready"), 6)

                tokens(0, 0)
                if st == "m0":
                    swapped_slots()
                max_n(0, 0, 0)
                max_s(0, 0, range(4))
                max_n(0, 0, 1)
                tokens(1, 1)
                if st == "m0":
                    moments_of((4, 5, 6, 7))

                def step(b, j, p, ahead=True, last=False):
                    subtract(b, p)
                    if not last:
                        max_n(b + 1, 1 - p, 0)
                        max_s(b + 1, 1 - p, range(4))
                        max_n(b + 1, 1 - p, 1)
                    slots_out(b, j, p)
                    if ahead:
                        tokens(b + 2, p)

                step(0, 0, 0)
                looped(dve, step, 1, BATCHES - 3)
                step(BATCHES - 3, 2, 1)
                step(BATCHES - 2, 3, 0, False)
                step(BATCHES - 1, 3, 1, False, True)

                def mix(e, p):
                    for f in range(2):
                        dve.wait_ge(*reached(f"{st}_gelu", e * 2 + (f + 1)))
                        dve.wait_ge(*reached(f"{st}_up", e * 2 + (f + 1)))
                        if due(e - 1):
                            dve.wait_ge(*reached(f"{st}_down", e - 1))
                        bias = bgu[:, 1, e, f:f + 1] if isinstance(e, int) else bgu[:, 1, bass.ds(e, 1), f]
                        dve.scalar_tensor_tensor(hmid[:, p, f, :], ps[:, 2 + f, :], bias, gate[:, f, :], ALU.add, ALU.mult)\
                            .then_inc(sem(f"{st}_h"), 1)

                def outputs(e, t, p):
                    dve.wait_ge(*reached(f"{st}_down", e + 1))
                    for half in range(2):
                        rows = slice(half * 64, half * 64 + 64)
                        block_t = expert_io[rows, t, :] if isinstance(t, int) else expert_io[rows, bass.ds(t, 1), :].rearrange("p a n -> p (a n)")
                        dst = block_t.rearrange("p (j q o) -> p q j o", q=2, o=OW)[:, half ^ p, :, 0:D]
                        bias = bd_bc[rows, e:e + 1, :] if isinstance(e, int) else bd_bc[rows, bass.ds(e, 1), :]
                        dve.tensor_tensor(dst, ps[rows, 4 + p, :].rearrange("p (j o) -> p j o", o=D),
                                          bias.broadcast_to([64, BATCHES // 2, D]), ALU.add).then_inc(sem(f"{st}_eo"), 1)

                dve.wait_ge(sem("dve_two"), 1)

                def sum_columns(t):
                    block_t = expert_io[:, t, :] if isinstance(t, int) else expert_io[:, bass.ds(t, 1), :].rearrange("p a n -> p (a n)")
                    dve.tensor_copy(block_t.rearrange("p (b o) -> p b o", o=OW)[:, :, D:OW], two[:].rearrange("p (b o) -> p b o", o=2)).then_inc(sem(f"{st}_sums"), 1)

                dve.wait_ge(sem("ld_w"), 16 * 12)
                mix(0, 0)
                with dve.Fori(0, ST - 1) as t:
                    mix(t * 2 + 1, 1)
                    outputs(t * 2, t, 0)
                    mix(t * 2 + 2, 0)
                    outputs(t * 2 + 1, t, 1)
                    sum_columns(t)
                mix(EXPERTS - 1, 1)
                outputs(EXPERTS - 2, ST - 1, 0)
                outputs(EXPERTS - 1, ST - 1, 1)
                sum_columns(ST - 1)

                def stage(b, j, p):
                    if due((b - 1) * 2):
                        dve.wait_ge(*reached(f"{st}_combined", (b - 1) * 2))
                    src = comb[:, b, ST // 2:ST, :] if isinstance(b, int) else comb[:, bass.ds(b, 1), ST // 2:ST, :].rearrange("p a t n -> p (a t) n")
                    dve.tensor_copy(logits[:, p, 1, :].rearrange("p (t n) -> p t n", t=ST // 2), src).then_inc(sem(f"{st}_staged_b"), 1)

                def residual(b, j, p):
                    go = Steps(f"{st}_steps", b * 4)
                    for i in range(PER):
                        dve.wait_ge(*reached(f"{st}_combined", b * 2 + (i + 1)))
                        dve.reciprocal(zcol[:, p, i:i + 1], ps[:, 2 * p + i, D:D + 1]).then_inc(go.sem, go.step())
                    dve.wait_ge(go.sem, go.n)
                    for i in range(PER):
                        tile = b * PER + i
                        xt = x[:, tile, :] if isinstance(b, int) else x[:, bass.ds(tile, 1), :].rearrange("p a d -> p (a d)")
                        dve.scalar_tensor_tensor(xt, ps[:, 2 * p + i, 0:D], zcol[:, p, i:i + 1], xt, ALU.mult, ALU.add).then_inc(go.sem, go.step())
                    dve.wait_ge(go.sem, plain(dve, go.n))
                    after(st, b)

                stage(0, 0, 0)
                def finish(b, j, p):
                    if not (isinstance(b, int) and b == BATCHES - 1):
                        stage(b + 1, None, 1 - p)
                    residual(b, j, p)
                all_batches(dve, finish)

            def linear_attention_vector(st):
                def minima(b, p):
                    dve.wait_ge(*reached(f"{st}_qkp", b + 1))
                    dve.tensor_scalar(la_min[:, p, :], ps[:, 4 * p, :], 0.0, None, ALU.min).then_inc(sem(f"{st}_min"), 1)

                def features(b, p):
                    dve.wait_ge(*reached(f"{st}_exp", b + 1))
                    dve.scalar_tensor_tensor(la_qk[:, p, :], ps[:, 4 * p, :], 0.0, la_min[:, p, :], ALU.max, ALU.add)\
                        .then_inc(sem(f"{st}_qk"), 1)

                def sums(b, p):
                    B = 4 * p
                    dve.wait_ge(*reached(f"{st}_kvp", b + 1))
                    dve.tensor_tensor(la_kv[:, p, 0, :], ps[:, B + 1, SEQ:SEQ + D], headmask[:], ALU.mult).then_inc(sem(f"{st}_kv"), 1)
                    dve.tensor_scalar(la_kv[:, p, 1, :], headmask[:], ps[:, B + 1, SEQ + D:SEQ + D + 1], None, ALU.mult)\
                        .then_inc(sem(f"{st}_kv"), 1)

                def divide(b, p):
                    go = Steps(f"{st}_steps", b * 3)
                    den = la_o[:, p, 1, :]
                    dve.wait_ge(*reached(f"{st}_op", b + 1))
                    dve.tensor_scalar(den, ps[:, 4 * p + 3, SEQ:2 * SEQ], ATT_EPS, None, ALU.add).then_inc(go.sem, go.step())
                    dve.wait_ge(go.sem, go.n)
                    dve.reciprocal(den, den).then_inc(go.sem, go.step())
                    dve.wait_ge(go.sem, go.n)
                    dve.tensor_tensor(la_o[:, p, 0, :], ps[:, 4 * p + 3, 0:SEQ], den, ALU.mult).then_inc(go.sem, go.step())

                def residual(b, p):
                    go = Steps(f"{st}_added", b * 2)
                    dve.wait_ge(*reached(f"{st}_yp", b + 1))
                    tmp = la_o[:, p, 1, :].rearrange("p (i d) -> p i d", i=PER)
                    dve.tensor_tensor(tmp, ps[:, 4 * p + 2, SEQ:2 * SEQ].rearrange("p (i d) -> p i d", i=PER),
                                      bproj_bc[:].unsqueeze(1).broadcast_to([P, PER, D]), ALU.add).then_inc(go.sem, go.step())
                    dve.wait_ge(go.sem, go.n)
                    xb = x[:, batch(b), :]
                    dve.tensor_tensor(xb, xb, tmp, ALU.add).then_inc(go.sem, go.step())
                    dve.wait_ge(go.sem, plain(dve, go.n))
                    after(st, b)

                def step(b, j, p):
                    more = not (isinstance(b, int) and b == BATCHES - 1)
                    sums(b, p)
                    if more:
                        minima(b + 1, 1 - p)
                    if due(b):
                        residual(b - 1, 1 - p)
                    if more:
                        features(b + 1, 1 - p)
                    divide(b, p)

                dve.memset(la_v[:, :, :, D:D + 1], 1.0).then_inc(sem(f"{st}_vones"), 1)
                minima(0, 0)
                features(0, 0)
                all_batches(dve, step)
                residual(BATCHES - 1, 1)

            def ffn_vector(st):
                def tokens(c, q):
                    dve.wait_ge(*reached(f"{st}_zthi", c + 1))
                    dve.tensor_tensor(fz_lo[:, q, :], ps[:, 6 + q, :], as32(fz_hi[:, q, :]), ALU.subtract).then_inc(sem(f"{st}_ztlo"), 1)

                def low(hi, lo, o):
                    dve.tensor_tensor(lo[:, o, :], whole[:, o, :], as32(hi[:, o, :]), ALU.subtract).then_inc(sem(f"{st}_lo"), 1)

                def mixes(c, q, os):
                    for o in os:
                        n = c * HK + o
                        dve.wait_ge(*reached(f"{st}_p2", n + 1))
                        dve.wait_ge(*reached(f"{st}_silu", n + 1))
                        done = (c // 2 * 6 + q) * HK + o + 1 - HK
                        if done > 0:
                            dve.wait_ge(*reached(f"{st}_lo", done))
                        dve.scalar_tensor_tensor(whole[:, o, :], ps[:, 2 * (o % 2) + 1, :], ffn_s[:, 1, o:o + 1], silu_out[:, o % 2, :],
                                                 ALU.mult, ALU.mult).then_inc(sem(f"{st}_mixed"), 1)
                        if n % (2 * HK) >= 1:
                            low_mixed(n - 1)

                def low_mixed(n):
                    dve.wait_ge(*reached(f"{st}_mixhi", n + 1))
                    low(even_hi[:, n // HK % 2], even_lo[:, n // HK % 2], n % HK)

                def splits(j, layer, q):
                    hi, lo = ((odd_hi, odd_lo), (even_hi, even_lo))[layer - 1]
                    for o in range(HK):
                        n = (j * 4 + (layer - 1) * 2 + q) * HK + o
                        dve.wait_ge(*reached(f"{st}_gelu", n + 1))
                        dve.tensor_copy(hi[:, q, o, :], whole[:, o, :]).then_inc(sem(f"{st}_gelhi"), 1)
                        dve.wait_ge(*reached(f"{st}_gelhi", n + 1))
                        low(hi[:, q], lo[:, q], o)

                def residual(c, q):
                    dve.wait_ge(*reached(f"{st}_yp", c + 1))
                    xc = x[:, 4 * c:4 * c + 4, :]
                    dve.tensor_tensor(xc, xc, ps[:, 6 + q, :].rearrange("p (t d) -> p t d", d=D), ALU.add)\
                        .then_inc(sem(f"{st}_added"), 1)

                def norms(c):
                    dve.wait_ge(*reached(f"{st}_added", c + 1))
                    for b in (2 * c, 2 * c + 1):
                        after(st, b)

                if st == ffns[0]:
                    for n, part in enumerate((slice(0, W12), slice(W12, H1))):
                        dve.wait_ge(sem("first_w_hi"), n + 1)
                        dve.tensor_tensor(ffw_lo[:, part], ffw[:, part], as32(ffw_hi[:, part]), ALU.subtract).then_inc(sem("first_w_lo"), 1)
                for j in range(CHUNKS // 2 + 1):
                    c = 2 * j
                    if c < CHUNKS:
                        tokens(c, 0)
                        mixes(c, 0, (0, 1))
                        tokens(c + 1, 1)
                        mixes(c, 0, (2, 3))
                    if j > 0:
                        residual(c - 2, 0)
                        residual(c - 1, 1)
                    if c < CHUNKS:
                        mixes(c + 1, 1, range(HK))
                        low_mixed((c + 2) * HK - 1)
                        splits(j, 1, 0)
                    if j > 0:
                        norms(c - 2)
                        norms(c - 1)
                    if c < CHUNKS:
                        splits(j, 1, 1)
                        if j == 0 and st == ffns[0]:
                            dve.wait_ge(sem("low_turned"), 1)
                            dve.tensor_reduce(low_sum[0:1, 1:2], ps[0:1, 0, 0:P], AX_X, ALU.max).then_inc(sem("low_sum"), 1)
                            dve.wait_ge(sem("low_sum"), 2)
                            dve.tensor_scalar(split_w[:], low_sum[0:1, 1:2], 0.0, None, ALU.not_equal).then_inc(sem("low_known"), 1)
                        splits(j, 2, 0)
                        splits(j, 2, 1)

            def favor_vector(st):
                def maxima(b, p):
                    cc = fa_c[:, p]
                    go = Steps(f"{st}_maxs", b * 5)
                    for n, a in enumerate((2, 3, 0, 1)):
                        dve.wait_ge(*reached(f"{st}_xw", b * 4 + (n + 1)))
                        dve.tensor_reduce(cc[:, 0, a * HEADS:a * HEADS + HEADS], ps[:, 4 + a, :].rearrange("p (h m) -> p h m", m=FEAT),
                                          AX_X, ALU.max).then_inc(go.sem, go.step())

                def shifts(b, p):
                    cc = fa_c[:, p]
                    go = Steps(f"{st}_maxs", b * 5 + 4)
                    dve.wait_ge(go.sem, go.n)
                    dve.wait_ge(*reached(f"{st}_norms", b + 1))
                    dve.tensor_tensor(cc[:, 1, :], ps[:, 3, NORMS:NORMS + 4 * HEADS], cc[:, 0, :], ALU.add).then_inc(go.sem, go.step())

                def subtract(b, p, n):
                    dve.wait_ge(*reached(f"{st}_maxs", b * 5 + 5))
                    for a in (2 - 2 * n, 3 - 2 * n):
                        dve.tensor_tensor(fa_phi[:, p, a, :].rearrange("p (h m) -> p h m", m=FEAT),
                                          ps[:, 4 + a, :].rearrange("p (h m) -> p h m", m=FEAT),
                                          fa_c[:, p, 1, a * HEADS:a * HEADS + HEADS].unsqueeze(2).broadcast_to([P, HEADS, FEAT]),
                                          ALU.subtract).then_inc(sem(f"{st}_sub"), 1)

                def guards(b, p):
                    for n in range(2):
                        dve.wait_ge(*reached(f"{st}_exp", b * 2 + (n + 1)))
                        phi = fa_phi[:, p, 2 - 2 * n:4 - 2 * n].rearrange("p a f -> p (a f)")
                        dve.tensor_scalar(phi, phi, ATT_EPS, None, ALU.add).then_inc(sem(f"{st}_phi"), 1)

                def sums(b, p):
                    dve.wait_ge(*reached(f"{st}_kvp", b + 1))
                    dve.tensor_tensor(fa_kv[:, p], ps[:, 3, SEQ:SEQ + FG * VA].rearrange("p (g v) -> p g v", g=FG),
                                      featmask[:].unsqueeze(1).broadcast_to([P, FG, VA]), ALU.mult).then_inc(sem(f"{st}_kv"), 1)

                def divide(b, p):
                    go = Steps(f"{st}_steps", b * 3)
                    dve.wait_ge(*reached(f"{st}_np", b + 1))
                    num = ps[:, 2, :].rearrange("p (i r) -> p i r", i=PER)[:, :, 0:FG * VA].rearrange("p i (g v) -> p i g v", g=FG)
                    den = fa_den[:, p, :].rearrange("p (i g h) -> p i g h", i=PER, g=FG)
                    dve.tensor_scalar(den, num[:, :, :, VA - 4:VA], ATT_EPS * FEAT, None, ALU.add).then_inc(go.sem, go.step())
                    dve.wait_ge(go.sem, go.n)
                    dve.reciprocal(fa_den[:, p, :], fa_den[:, p, :]).then_inc(go.sem, go.step())
                    dve.wait_ge(go.sem, go.n)
                    for i in range(PER):
                        last = dve.tensor_tensor(fa_o[:, p, i, :].rearrange("p (g h d) -> p g h d", g=FG, h=4),
                                                 num[:, i, :, 0:VA - 4].rearrange("p g (h d) -> p g h d", h=4),
                                                 den[:, i].unsqueeze(3).broadcast_to([P, FG, 4, HD]), ALU.mult)
                    last.then_inc(sem(f"{st}_o"), 1)

                def residual(b, p):
                    dve.wait_ge(*reached(f"{st}_yp", b + 1))
                    dve.tensor_tensor(fa_y[:, p], ps[:, 0, SEQ:2 * SEQ].rearrange("p (i d) -> p i d", i=PER),
                                      bo_bc[:].unsqueeze(1).broadcast_to([P, PER, D]), ALU.add).then_inc(sem(f"{st}_yout"), 1)
                    dve.wait_ge(*reached(f"{st}_yout", b + 1))
                    xb = x[:, batch(b), :]
                    go = Steps(f"{st}_steps", b * 3 + 2)
                    dve.tensor_tensor(xb, xb, fa_y[:, p], ALU.add).then_inc(go.sem, go.step())
                    dve.wait_ge(go.sem, plain(dve, go.n))
                    after(st, b)

                def step(b, j, p):
                    more = not (isinstance(b, int) and b == BATCHES - 1)
                    guards(b, p)
                    if more:
                        maxima(b + 1, 1 - p)
                    sums(b, p)
                    if more:
                        shifts(b + 1, 1 - p)
                        subtract(b + 1, 1 - p, 0)
                    divide(b, p)
                    if more:
                        subtract(b + 1, 1 - p, 1)
                    residual(b, p)

                dve.memset(fa_vaug[:, :, :, :, VA - 4:VA], 1.0).then_inc(sem(f"{st}_vones"), 1)
                maxima(0, 0)
                shifts(0, 0)
                subtract(0, 0, 0)
                subtract(0, 0, 1)
                all_batches(dve, step)

            dve.memset(two[:], 2.0).then_inc(sem("dve_two"), 1)
            dve.wait_ge(sem("ld_const"), 16)
            dve.tensor_copy(ident_r[:], ident[:]).then_inc(sem("dve_const"), 1)
            dve.wait_ge(sem("dve_const"), 1)
            moments_of((0, 1))
            if "m0" in stages:
                dve.wait_ge(sem("ld_se"), 32)
                go = Steps("se_steps")
                for k in range(2):
                    dve.tensor_tensor(cols[:, 3 + k:4 + k], cols[:, k:k + 1], cols[:, 2:3], ALU.mult).then_inc(go.sem, go.step())
                for t in range(ST):
                    dve.bn_stats(se_stat[:, t, 0:6], logits[:, 1, 0, t * D:t * D + D]).then_inc(go.sem, go.step())
                dve.wait_ge(go.sem, go.n)
                for t in range(ST):
                    dve.bn_aggr(se_stat[:, t, 6:8], se_stat[:, t, 0:6]).then_inc(sem("se_moments"), 1)
            moments_of((2, 3))
            if "m0" in stages:
                dve.wait_ge(sem("se_scale"), 2)
                dve.wait_ge(sem("se_moments"), ST)
                for t in range(ST):
                    row = logits[:, 1, 0, t * D:t * D + D]
                    dve.tensor_scalar(row, row, se_stat[:, t, 6:7], se_r[:, 1, t:t + 1], ALU.subtract, ALU.mult).then_inc(sem("se_norm"), 1)
                flat = logits[:, 0, 0, :]
                for k in range(2):
                    dve.wait_ge(sem("se_turned"), 4 * k + 4)
                    dve.tensor_scalar(flat[:, k * 512:k * 512 + 512], ps[:, k, :], cols[:, 3:4], cols[:, 4:5], ALU.mult, ALU.add).then_inc(go.sem, go.step())
                dve.wait_ge(go.sem, go.n)
                dve.tensor_copy(se_hi[:, 0, :], flat).then_inc(sem("se_ready"), 1)
                dve.wait_ge(sem("se_ready"), 1)
                dve.tensor_tensor(se_lo[:, 0, :], flat, as32(se_hi[:, 0, :]), ALU.subtract).then_inc(sem("se_ready"), 1)
            if stages[0] != "m0":
                moments_of((4, 5, 6, 7))
            for st in stages:
                if before[st] != "init":
                    dve.wait_ge(sem(f"{before[st]}_x"), BATCHES)
                if before[st] == "init" and st != "m0":
                    dve.wait_ge(sem("ld_w"), 16 * 12)
                if st == "f0":
                    dve.tensor_scalar(w3_s[:, 1:2], w3_s[:, 0:1], 0.5, None, ALU.mult).then_inc(sem("w3_half"), 1)
                {"m": moe_vector, "l": linear_attention_vector, "f": ffn_vector}[st[0]](st) if st != "fa" else favor_vector(st)


def arrange(a):
    f = np.float32
    t = lambda m: np.ascontiguousarray(np.transpose(m))
    rows = lambda m, k: np.ascontiguousarray(m.reshape(k, P, -1).transpose(1, 0, 2).reshape(P, -1))
    got = {
        "x": np.ascontiguousarray(a["L0_attn_x"].reshape(BATCHES * SEQ, D)),
        "ident": np.eye(P, dtype=f),
        "slot_embeds": np.ascontiguousarray(a["L0_ffn_slot_embeds"].reshape(NSLOT, D)),
        "cols": np.ascontiguousarray(np.stack([a["L0_ffn_slot_g"], a["L0_ffn_slot_b"], np.broadcast_to(a["L0_ffn_scale"], (D,))], 1)),
        "affine": np.stack([a["L0_ffn_norm_g"], a["L0_ffn_norm_b"]]),
        "bgu": np.ascontiguousarray(np.stack([a["L0_ffn_bg"], a["L0_ffn_bu"]]).reshape(2, EXPERTS, 2, P).transpose(3, 0, 1, 2).reshape(P, -1)),
        "bd": np.ascontiguousarray(a["L0_ffn_bd"]),
        "wqkv": t(a["L0_attn_Wqkv"]),
        "wproj": t(a["L0_attn_Wproj"]),
        "headmask": np.kron(np.eye(HEADS, dtype=f), np.ones((HD, HD), f)),
        "bproj": np.ascontiguousarray(a["L0_attn_bproj"]),
        "bo": np.ascontiguousarray(a["L1_attn_bo"]),
        "fw": np.concatenate([t(a[f"L1_attn_W{k}"]) for k in "qkvo"], 1),
        "ffn_s": np.concatenate([a[f"L1_ffn_{k}_s"].reshape(HK, P).T for k in ("w1", "w2", "h1", "h2")], 1),
        "w3_s": np.ascontiguousarray(a["L1_ffn_w3_s"].reshape(D, 1)),
        "wx": np.concatenate([a["L0_ffn_Wg"], a["L0_ffn_Wu"],
                              a["L0_ffn_Wd"].reshape(EXPERTS, 2, P, D).transpose(0, 2, 1, 3).reshape(EXPERTS, P, 2 * D)], 2),
        "ffw": np.concatenate([t(a["L1_ffn_w1_w"]), t(a["L1_ffn_w2_w"]), rows(t(a["L1_ffn_h1_w"]), HK),
                               rows(t(a["L1_ffn_h2_w"]), HK), rows(t(a["L1_ffn_w3_w"]), HK)], 1),
    }
    bd = np.zeros((HEADS, HD, HEADS, FEAT), f)
    for h in range(HEADS):
        bd[h, :, h, :] = a["L1_attn_proj"][h].T
    got["proj_bd"] = bd.reshape(P, HF)
    mask = np.zeros((P, VA), f)
    for h in range(4):
        mask[h * FEAT:h * FEAT + FEAT, h * HD:h * HD + HD] = 1.0
        mask[h * FEAT:h * FEAT + FEAT, 4 * HD + h] = 1.0
    got["featmask"] = mask
    return {k: np.ascontiguousarray(v) for k, v in got.items()}


def kernel(**inputs):
    import concourse.bacc as bacc
    from concourse.bass_utils import run_bass_kernel_spmd

    nc = bacc.Bacc("TRN2", target_bir_lowering=False, num_devices=1)
    arrays = {f"in_{k}": v for k, v in arrange({k: np.asarray(v) for k, v in inputs.items()}).items()}
    ins = {k[3:]: nc.dram_tensor(k, v.shape, F32, kind="ExternalInput").ap() for k, v in arrays.items()}
    out = nc.dram_tensor("out_0", (BATCHES * SEQ, D), F32, kind="ExternalOutput").ap()
    build(nc, ins, out)
    r = run_bass_kernel_spmd(nc, [arrays], core_ids=[0])
    return r.results[0]["out_0"].reshape(BATCHES, SEQ, D)
```
